# Optimizing a Trainium2 kernel written in Bass

```python
import numpy as np
import jax
import jax.numpy as jnp

def _softmax(x, axis=-1):
    return jax.nn.softmax(x, axis=axis)

def _gelu(x):
    return jax.nn.gelu(x, approximate=True)

def _silu(x):
    return jax.nn.silu(x)

def _sigmoid(x):
    return jax.nn.sigmoid(x)

def _layernorm(x, axis=-1, eps=1e-05):
    m = jnp.mean(x, axis=axis, keepdims=True)
    v = jnp.var(x, axis=axis, keepdims=True)
    return (x - m) / jnp.sqrt(v + eps)

def _scatter_add(tgt, idx, src, axis=0):
    return tgt.at[idx].add(src)

def _segment_sum(src, seg, n):
    return jax.ops.segment_sum(src, seg, n)
kernel_name = 'mk_sandwich_d2_jaxref_r8_966fe1'

def setup_inputs(seed: int=0):
    np.random.seed(seed)
    _w = jnp.asarray

    def _L0_attn_setup():
        import jax, jax.numpy as jnp
        import numpy as np
        H = 512
        D_IN = 1024
        N = 16
        K = 4
        R = 32
        EPS = 1e-06

        def rms_forward(x, eps=EPS):
            xf = x.astype(jnp.float32)
            var = jnp.mean(xf * xf, axis=-1, keepdims=True)
            return (xf * jax.lax.rsqrt(var + eps)).astype(x.dtype)
        key = jax.random.key(seed)
        ks = jax.random.split(key, 10)
        s = 0.02
        hidden_states = jax.random.normal(ks[0], (2, 128, H), dtype=jnp.float32)
        W_in = jax.random.normal(ks[1], (2 * D_IN, H), dtype=jnp.float32) * s
        conv_w = jax.random.normal(ks[2], (D_IN, K), dtype=jnp.float32) * 0.2
        conv_b = jax.random.normal(ks[3], (D_IN,), dtype=jnp.float32) * 0.02
        W_x = jax.random.normal(ks[4], (R + 2 * N, D_IN), dtype=jnp.float32) * s
        W_dt = jax.random.normal(ks[5], (D_IN, R), dtype=jnp.float32) * s
        b_dt = jax.random.normal(ks[6], (D_IN,), dtype=jnp.float32) * 0.02
        A_log = jnp.log(jnp.broadcast_to(jnp.arange(1, N + 1, dtype=jnp.float32)[None, :], (D_IN, N)))
        D = jnp.ones((D_IN,), dtype=jnp.float32)
        W_out = jax.random.normal(ks[7], (H, D_IN), dtype=jnp.float32) * s
        return {'hidden_states': hidden_states, 'W_in': W_in, 'conv_w': conv_w, 'conv_b': conv_b, 'W_x': W_x, 'W_dt': W_dt, 'b_dt': b_dt, 'A_log': A_log, 'D': D, 'W_out': W_out}
    _L0_attn_in = _L0_attn_setup()

    def _L0_ffn_setup():
        import jax, jax.numpy as jnp
        import numpy as np
        HIDDEN = 512
        INTER = 1376
        GROUPSIZE = 128
        PACK = 8

        def dequant_gptq(qweight, scales, zeros, groupsize):
            K = qweight.shape[0] * PACK
            N = qweight.shape[1]
            k = jnp.arange(K)
            q = qweight[k // PACK, :] >> (k % PACK * 4)[:, None] & 15
            n = jnp.arange(N)
            z = zeros[:, n // PACK] >> (n % PACK * 4)[None, :] & 15
            s = scales.astype(jnp.float32)
            zp = (z.astype(jnp.float32) + 1.0) * s
            g = k // groupsize
            return q.astype(jnp.float32) * s[g] - zp[g]
        key = jax.random.key(seed)
        ks = jax.random.split(key, 11)
        imax = 2147483647
        G_h = HIDDEN // GROUPSIZE
        G_i = (INTER + GROUPSIZE - 1) // GROUPSIZE
        x = (jax.random.normal(ks[0], (2, 256, HIDDEN), dtype=jnp.float32) * 0.5).astype(jnp.float16)
        return {'x': x, 'gate_qweight': jax.random.randint(ks[1], (HIDDEN // PACK, INTER), 0, imax, dtype=jnp.int32), 'gate_scales': (jax.random.uniform(ks[2], (G_h, INTER), dtype=jnp.float32) * 0.01 + 0.001).astype(jnp.float16), 'gate_zeros': jax.random.randint(ks[3], (G_h, INTER // PACK), 0, imax, dtype=jnp.int32), 'up_qweight': jax.random.randint(ks[4], (HIDDEN // PACK, INTER), 0, imax, dtype=jnp.int32), 'up_scales': (jax.random.uniform(ks[5], (G_h, INTER), dtype=jnp.float32) * 0.01 + 0.001).astype(jnp.float16), 'up_zeros': jax.random.randint(ks[6], (G_h, INTER // PACK), 0, imax, dtype=jnp.int32), 'down_qweight': jax.random.randint(ks[7], (INTER // PACK, HIDDEN), 0, imax, dtype=jnp.int32), 'down_scales': (jax.random.uniform(ks[8], (G_i, HIDDEN), dtype=jnp.float32) * 0.01 + 0.001).astype(jnp.float16), 'down_zeros': jax.random.randint(ks[9], (G_i, HIDDEN // PACK), 0, imax, dtype=jnp.int32)}
    _L0_ffn_in = _L0_ffn_setup()

    def _L1_attn_setup():
        import jax, jax.numpy as jnp
        import numpy as np
        EMB_DIM = 512
        N_HEADS = 32
        QKV_DIM = EMB_DIM // N_HEADS
        B, S = (4, 512)
        key = jax.random.key(seed)
        ks = jax.random.split(key, 7)
        std = 1.0 / np.sqrt(EMB_DIM)
        x = jax.random.normal(ks[0], (B, S, EMB_DIM), dtype=jnp.float32)
        Wq = jax.random.normal(ks[1], (EMB_DIM, QKV_DIM, N_HEADS), dtype=jnp.float32) * std
        bq = jnp.zeros((QKV_DIM, N_HEADS), dtype=jnp.float32)
        Wk = jax.random.normal(ks[2], (EMB_DIM, QKV_DIM, 1), dtype=jnp.float32) * std
        bk = jnp.zeros((QKV_DIM, 1), dtype=jnp.float32)
        Wv = jax.random.normal(ks[3], (EMB_DIM, QKV_DIM, 1), dtype=jnp.float32) * std
        bv = jnp.zeros((QKV_DIM, 1), dtype=jnp.float32)
        return {'x': x, 'Wq': Wq, 'bq': bq, 'Wk': Wk, 'bk': bk, 'Wv': Wv, 'bv': bv}
    _L1_attn_in = _L1_attn_setup()

    def _L1_ffn_setup():
        import jax, jax.numpy as jnp
        import numpy as np
        HID, INT, LAT, NE, K = (512, 1024, 256, 8, 2)
        LN_EPS = 1e-05

        def _layernorm(x, gamma, beta):
            mu = jnp.mean(x, axis=-1, keepdims=True)
            var = jnp.var(x, axis=-1, keepdims=True)
            return (x - mu) * jax.lax.rsqrt(var + LN_EPS) * gamma + beta
        key = jax.random.key(seed)
        ks = jax.random.split(key, 8)
        s = lambda d: 1.0 / np.sqrt(d)
        return {'hidden_states': jax.random.normal(ks[0], (4, 256, HID), jnp.float32), 'gate_w': jax.random.normal(ks[1], (HID, NE), jnp.float32) * s(HID), 'up_w': jax.random.normal(ks[2], (HID, INT), jnp.float32) * s(HID), 'down_w': jax.random.normal(ks[3], (INT, HID), jnp.float32) * s(INT), 'fc1_w': jax.random.normal(ks[4], (HID, LAT), jnp.float32) * s(HID), 'fc2_w': jax.random.normal(ks[5], (LAT, HID), jnp.float32) * s(LAT), 'expert_w': jax.random.normal(ks[6], (LAT, LAT), jnp.float32), 'ln_gamma': jnp.ones((HID,), jnp.float32), 'ln_beta': jnp.zeros((HID,), jnp.float32)}
    _L1_ffn_in = _L1_ffn_setup()
    _d = {'L0_attn_hidden_states': _L0_attn_in['hidden_states'], 'L0_attn_W_in': _L0_attn_in['W_in'], 'L0_attn_conv_w': _L0_attn_in['conv_w'], 'L0_attn_conv_b': _L0_attn_in['conv_b'], 'L0_attn_W_x': _L0_attn_in['W_x'], 'L0_attn_W_dt': _L0_attn_in['W_dt'], 'L0_attn_b_dt': _L0_attn_in['b_dt'], 'L0_attn_A_log': _L0_attn_in['A_log'], 'L0_attn_D': _L0_attn_in['D'], 'L0_attn_W_out': _L0_attn_in['W_out'], 'L0_ffn_gate_qweight': _L0_ffn_in['gate_qweight'], 'L0_ffn_gate_scales': _L0_ffn_in['gate_scales'], 'L0_ffn_gate_zeros': _L0_ffn_in['gate_zeros'], 'L0_ffn_up_qweight': _L0_ffn_in['up_qweight'], 'L0_ffn_up_scales': _L0_ffn_in['up_scales'], 'L0_ffn_up_zeros': _L0_ffn_in['up_zeros'], 'L0_ffn_down_qweight': _L0_ffn_in['down_qweight'], 'L0_ffn_down_scales': _L0_ffn_in['down_scales'], 'L0_ffn_down_zeros': _L0_ffn_in['down_zeros'], 'L1_attn_Wq': _L1_attn_in['Wq'], 'L1_attn_bq': _L1_attn_in['bq'], 'L1_attn_Wk': _L1_attn_in['Wk'], 'L1_attn_bk': _L1_attn_in['bk'], 'L1_attn_Wv': _L1_attn_in['Wv'], 'L1_attn_bv': _L1_attn_in['bv'], 'L1_ffn_gate_w': _L1_ffn_in['gate_w'], 'L1_ffn_up_w': _L1_ffn_in['up_w'], 'L1_ffn_down_w': _L1_ffn_in['down_w'], 'L1_ffn_fc1_w': _L1_ffn_in['fc1_w'], 'L1_ffn_fc2_w': _L1_ffn_in['fc2_w'], 'L1_ffn_expert_w': _L1_ffn_in['expert_w'], 'L1_ffn_ln_gamma': _L1_ffn_in['ln_gamma'], 'L1_ffn_ln_beta': _L1_ffn_in['ln_beta']}
    _x0 = _d['L0_attn_hidden_states']
    _d['L0_attn_hidden_states'] = jax.random.normal(jax.random.fold_in(jax.random.key(seed), 1), (2, 512, 512), dtype=_x0.dtype)
    del _x0
    return _d

def reference(L0_attn_hidden_states, L0_attn_W_in, L0_attn_conv_w, L0_attn_conv_b, L0_attn_W_x, L0_attn_W_dt, L0_attn_b_dt, L0_attn_A_log, L0_attn_D, L0_attn_W_out, L0_ffn_gate_qweight, L0_ffn_gate_scales, L0_ffn_gate_zeros, L0_ffn_up_qweight, L0_ffn_up_scales, L0_ffn_up_zeros, L0_ffn_down_qweight, L0_ffn_down_scales, L0_ffn_down_zeros, L1_attn_Wq, L1_attn_bq, L1_attn_Wk, L1_attn_bk, L1_attn_Wv, L1_attn_bv, L1_ffn_gate_w, L1_ffn_up_w, L1_ffn_down_w, L1_ffn_fc1_w, L1_ffn_fc2_w, L1_ffn_expert_w, L1_ffn_ln_gamma, L1_ffn_ln_beta):

    def _L0_attn_ref(hidden_states, W_in, conv_w, conv_b, W_x, W_dt, b_dt, A_log, D, W_out):
        import jax, jax.numpy as jnp
        import numpy as np
        H = 512
        D_IN = 1024
        N = 16
        K = 4
        R = 32
        EPS = 1e-06

        def rms_forward(x, eps=EPS):
            xf = x.astype(jnp.float32)
            var = jnp.mean(xf * xf, axis=-1, keepdims=True)
            return (xf * jax.lax.rsqrt(var + eps)).astype(x.dtype)
        b, L, _ = hidden_states.shape
        proj = hidden_states @ W_in.T
        x, gate = (proj[..., :D_IN], proj[..., D_IN:])
        xpad = jnp.pad(x, ((0, 0), (K - 1, 0), (0, 0)))
        xc = conv_b
        for j in range(K):
            xc = xc + conv_w[:, j] * xpad[:, j:j + L, :]
        x = jax.nn.silu(xc)
        ssm = x @ W_x.T
        ts, Bm, Cm = (ssm[..., :R], ssm[..., R:R + N], ssm[..., R + N:])
        ts = rms_forward(ts)
        Bm = rms_forward(Bm)
        Cm = rms_forward(Cm)
        dt = jax.nn.softplus(ts @ W_dt.T + b_dt)
        A = -jnp.exp(A_log.astype(jnp.float32))

        def step(state, inp):
            dt_t, B_t, C_t, u_t = inp
            dA = jnp.exp(dt_t[..., None] * A)
            state = state * dA + (dt_t * u_t)[..., None] * B_t[:, None, :]
            y = jnp.einsum('bdn,bn->bd', state, C_t)
            return (state, y)
        init = jnp.zeros((b, D_IN, N), dtype=jnp.float32)
        xs = (dt.transpose(1, 0, 2), Bm.transpose(1, 0, 2), Cm.transpose(1, 0, 2), x.transpose(1, 0, 2))
        _, ys = jax.lax.scan(step, init, xs)
        y = ys.transpose(1, 0, 2) + x * D
        y = y * jax.nn.silu(gate)
        return y @ W_out.T

    def _L0_ffn_ref(x, gate_qweight, gate_scales, gate_zeros, up_qweight, up_scales, up_zeros, down_qweight, down_scales, down_zeros):
        import jax, jax.numpy as jnp
        import numpy as np
        HIDDEN = 512
        INTER = 1376
        GROUPSIZE = 128
        PACK = 8

        def dequant_gptq(qweight, scales, zeros, groupsize):
            K = qweight.shape[0] * PACK
            N = qweight.shape[1]
            k = jnp.arange(K)
            q = qweight[k // PACK, :] >> (k % PACK * 4)[:, None] & 15
            n = jnp.arange(N)
            z = zeros[:, n // PACK] >> (n % PACK * 4)[None, :] & 15
            s = scales.astype(jnp.float32)
            zp = (z.astype(jnp.float32) + 1.0) * s
            g = k // groupsize
            return q.astype(jnp.float32) * s[g] - zp[g]
        B, S, H = x.shape
        x2 = x.reshape(-1, H).astype(jnp.float32)
        Wg = dequant_gptq(gate_qweight, gate_scales, gate_zeros, GROUPSIZE)
        Wu = dequant_gptq(up_qweight, up_scales, up_zeros, GROUPSIZE)
        Wd = dequant_gptq(down_qweight, down_scales, down_zeros, GROUPSIZE)
        gate = x2 @ Wg
        up = x2 @ Wu
        inter = gate * jax.nn.sigmoid(gate) * up
        out = (inter @ Wd).astype(jnp.float16)
        return out.reshape(B, S, H)

    def _L1_attn_ref(x, Wq, bq, Wk, bk, Wv, bv):
        import jax, jax.numpy as jnp
        import numpy as np
        EMB_DIM = 512
        N_HEADS = 32
        QKV_DIM = EMB_DIM // N_HEADS
        B, S = (4, 512)
        q = jnp.einsum('bsD,Ddh->bsdh', x, Wq) + bq
        k = (jnp.einsum('bsD,Ddh->bsdh', x, Wk) + bk)[..., 0]
        v = (jnp.einsum('bsD,Ddh->bsdh', x, Wv) + bv)[..., 0]
        qkv_dim = q.shape[-2]
        n_heads = q.shape[-1]
        scale = 1.0 / jnp.sqrt(jnp.asarray(qkv_dim, dtype=q.dtype))
        scores = jnp.einsum('bsdh,bse->bsde', q, k) * scale
        p = jax.nn.softmax(scores, axis=-1)
        o = jnp.einsum('bsde,bse->bsd', p, v)
        out = jnp.broadcast_to(o[..., None], o.shape + (n_heads,))
        return out.reshape(x.shape[:-1] + (qkv_dim * n_heads,))

    def _L1_ffn_ref(hidden_states, gate_w, up_w, down_w, fc1_w, fc2_w, expert_w, ln_gamma, ln_beta):
        import jax, jax.numpy as jnp
        import numpy as np
        HID, INT, LAT, NE, K = (512, 1024, 256, 8, 2)
        LN_EPS = 1e-05

        def _layernorm(x, gamma, beta):
            mu = jnp.mean(x, axis=-1, keepdims=True)
            var = jnp.var(x, axis=-1, keepdims=True)
            return (x - mu) * jax.lax.rsqrt(var + LN_EPS) * gamma + beta
        logits = jnp.einsum('bsh,he->bse', hidden_states, gate_w)
        routing_weights, selected_experts = jax.lax.top_k(logits, K)
        h = jax.nn.relu(jnp.einsum('bsh,hi->bsi', hidden_states, up_w)) ** 2
        shared_out = jnp.einsum('bsi,ih->bsh', h, down_w)
        x_latent = jnp.einsum('bsh,hl->bsl', hidden_states, fc1_w)
        expert_out = jnp.einsum('bsl,lm->bsm', x_latent, expert_w)
        moe_out = expert_out * jnp.sum(routing_weights, axis=-1, keepdims=True)
        routed_out = jnp.einsum('bsl,lh->bsh', moe_out, fc2_w)
        return _layernorm(shared_out + routed_out, ln_gamma, ln_beta)
    x = L0_attn_hidden_states
    x = x + _layernorm(_L0_attn_ref(_layernorm(x, axis=-1), L0_attn_W_in, L0_attn_conv_w, L0_attn_conv_b, L0_attn_W_x, L0_attn_W_dt, L0_attn_b_dt, L0_attn_A_log, L0_attn_D, L0_attn_W_out), axis=-1)
    x = x + _layernorm(_L0_ffn_ref(_layernorm(x, axis=-1), L0_ffn_gate_qweight, L0_ffn_gate_scales, L0_ffn_gate_zeros, L0_ffn_up_qweight, L0_ffn_up_scales, L0_ffn_up_zeros, L0_ffn_down_qweight, L0_ffn_down_scales, L0_ffn_down_zeros), axis=-1)
    x = x + _layernorm(_L1_attn_ref(_layernorm(x, axis=-1), L1_attn_Wq, L1_attn_bq, L1_attn_Wk, L1_attn_bk, L1_attn_Wv, L1_attn_bv), axis=-1)
    x = x + _layernorm(_L1_ffn_ref(_layernorm(x, axis=-1), L1_ffn_gate_w, L1_ffn_up_w, L1_ffn_down_w, L1_ffn_fc1_w, L1_ffn_fc2_w, L1_ffn_expert_w, L1_ffn_ln_gamma, L1_ffn_ln_beta), axis=-1)
    return x

_drawn_inputs = setup_inputs


def setup_inputs(seed=0):
    import zlib

    import numpy as np

    out = dict(_drawn_inputs(seed))
    spreads = {'L0_attn_D': (1.0, 0.2),
     'L1_attn_bq': (0.0, 0.1),
     'L1_attn_bk': (0.0, 0.1),
     'L1_attn_bv': (0.0, 0.1),
     'L1_ffn_ln_gamma': (1.0, 0.2),
     'L1_ffn_ln_beta': (0.0, 0.1)}
    factors = {}
    for name, (base, spread) in spreads.items():
        noise = np.random.default_rng([zlib.crc32(name.encode()), seed]).standard_normal(out[name].shape)
        drawn = base * np.exp(spread * noise) if base else spread * noise
        out[name] = jnp.asarray(drawn.astype(out[name].dtype))
    for name, factor in factors.items():
        out[name] = (out[name] * factor).astype(out[name].dtype)
    return out
```

```python
import numpy as np

import concourse.bass as bass
from concourse import mybir
from contextlib import ExitStack

F32 = mybir.dt.float32
F16 = mybir.dt.float16
I32 = mybir.dt.int32
ALU = mybir.AluOpType
ACT = mybir.ActivationFunctionType
AX = mybir.AxisListType

P = 128
NB = 2
L = 512
NT = L // P
H = 512
KH = H // P
DIN = 1024
DC = DIN // P
NS = 16
R = 32
KCONV = 4
INTER = 1376
IC = -(-INTER // P)
IPAD = IC * P
DH = 16
NH = 32
QKV = 3 * DH
MI = 1024 // P
LAT = 256 // P
NE = 8
PAIRS = NS // 2
SLOTS = 3
EPS = 1e-5
EPS16 = float(np.float16(1e-5))
EPS_RMS = 1e-6


def pe_order():
    items = []
    for b in range(NB):
        items += [("tr", "ssm", b, t) for t in range(NT)]
        items += [("x", b, c) for c in range(DC)]
        items += [("gate", b, c) for c in range(3)]
        items += [("ms", b)]
        items += [("gate", b, c) for c in range(3, DC)]
        items += [("dt", b, c) for c in range(DC)]
        items += [("out", b, t) for t in range(NT)]
    for b in range(NB):
        items += [("tr", "ffn", b, t) for t in range(NT)]
        for i in range(IC):
            items += [("g", b, i), ("u", b, i)]
    for b in range(NB):
        items += [("tr", "att", b, t) for t in range(NT)]
        items += [("qkv", b)]
    for b in range(NB):
        items += [("tr", "moe", b, t) for t in range(NT)]
        items += [("logits", b)]
        items += [("fc1", b, m) for m in range(LAT)]
        items += [("exp", b, m) for m in range(LAT)]
        items += [("up", b, i) for i in range(MI)]
        items += [("routed", b, t) for t in range(NT)]
    return {item: n for n, item in enumerate(items)}


def ln_order():
    groups = []
    for b in range(NB):
        groups += [("ssm", b)] + [("out", b, t) for t in range(NT)]
    for b in range(NB):
        groups += [("ffn", b), ("ffn16", b)]
    groups += [("att", b) for b in range(NB)]
    groups += [("atto", b) for b in range(NB)]
    for b in range(NB):
        groups += [("moe", b)]
        for t in range(NT):
            groups += [("moei", b, t), ("moeo", b, t)]
    return {g: n for n, g in enumerate(groups)}


def build(nc, x_in, ident_in, meanmat_in, shift_in, shifts_in, w_in, conv_in, par_in, alog_in, wx_in, wdt_in,
          wout_in, qgu_in, qd_in, sgu_in, zgu_in, sd_in, zd_in, wq_in, wkv_in, bq_in, bkv_in, gate_in, up_in,
          down_in, fc1_in, fc2_in, exp_in, gamma_in, beta_in, out):
    WORK = pe_order()
    LN = ln_order()
    NG = len(LN)
    bc_dram = nc.dram_tensor("bc_scratch", [NB, 2 * NS, L], F32).ap()
    zgu_dram = nc.dram_tensor("zgu_scratch", [2 * KH, IPAD], F32).ap()
    zd_dram = nc.dram_tensor("zd_scratch", [IC, H], F32).ap()

    with ExitStack() as ctx:
        def sb(name, shape, dt=F32):
            return ctx.enter_context(nc.sbuf_tensor(name, shape, dt))

        def sem(name):
            return ctx.enter_context(nc.semaphore(name))

        x = sb("x", [P, NB * NT, H])
        ident = sb("ident", [P, P])
        meanmat = sb("meanmat", [64, 64])
        shift = sb("shift", [P, 1], I32)
        epst = sb("epst", [P, 2])
        NGT = 4
        bst = sb("bst", [P, NT, 6])
        mv = sb("mv", [P, NG, NGT, 2])
        std = sb("std", [P, NG, NGT])
        rstd = sb("rstd", [P, NG, NGT])
        r_win = sb("r_win", [P, 8192])
        r_bc = sb("r_bc", [P, 16384])
        r_u = sb("r_u", [P, 8192])
        r_g = sb("r_g", [P, 4096])
        r_t = sb("r_t", [P, 4096])
        r_w = sb("r_w", [P, 4096])
        r_s = sb("r_s", [P, 2 * 512 + 256])
        r_c = sb("r_c", [P, 1792])
        psum = ctx.enter_context(nc.psum_tensor("psum", [P, 8, L], F32))

        def view(t, a, shape, dt=None):
            n = int(np.prod(shape))
            v = t[:, a:a + n]
            if dt is not None:
                v = v.bitcast(dt)
            if len(shape) == 1:
                return v
            names = "abcde"[:len(shape)]
            return v.rearrange(f"p ({' '.join(names)}) -> p {' '.join(names)}",
                               **{k: s for k, s in zip(names, shape)})

        w_in_sb = view(r_win, 0, [KH, 2 * DIN])
        bc = view(r_bc, 0, [2 * NS, L])
        u = view(r_u, 0, [DC, L])
        dtv = view(r_u, 4096, [DC, L])
        g = view(r_g, 0, [DC, L])
        sp = view(r_t, 0, [DC, L])
        dbu = view(r_t, 0, [2, 2, L])
        hc = view(r_t, 2048, [2, 2, L])
        xT = view(r_w, 0, [KH, L])
        xn = view(r_w, 2048, [2, H])
        cacc = view(r_w, 3072, [2, L])
        wout = view(r_w, 0, [DC, H])
        du = view(r_s, 0, [2, L])
        wx = view(r_c, 0, [DC, 64])
        wdt = view(r_c, 512, [DIN])
        par = view(r_c, 1536, [3, DC])
        convw = view(r_c, 1560, [DC, KCONV])
        aneg = view(r_c, 1600, [DC, NS])
        ssm = view(r_t, 0, [L])
        sq = view(r_t, 512, [L])
        rr = view(r_t, 1024, [L])
        ssmn = view(r_s, 0, [L])
        wgu = view(r_bc, 0, [IC, 2 * KH, P])
        wd = view(r_u, 0, [IC, H])
        STG = 1024 + 512 + 1024 + 512 + 256 + 512
        q_gu = [view(r_win, s * STG, [2 * KH, P], I32) for s in range(2)]
        s_gu = [view(r_win, s * STG + 1024, [512], F16) for s in range(2)]
        z_gu = [view(r_win, s * STG + 1536, [2 * KH, P]) for s in range(2)]
        q_d = [view(r_win, s * STG + 2560, [H], I32) for s in range(2)]
        s_d = [view(r_win, s * STG + 3072, [256], F16) for s in range(2)]
        z_d = [view(r_win, s * STG + 3328, [H]) for s in range(2)]
        xTc = view(r_g, 0, [KH, L])
        xnc = view(r_g, 2048, [2, H])
        inter = view(r_g, 3072, [2, L])
        sg = view(r_w, 0, [2, L])
        y16 = view(r_w, 1024, [NT * H // 2], F16).rearrange("p (t n) -> p t n", t=NT)
        d16 = view(r_w, 2048, [H // 2], F16)
        n16 = view(r_w, 2304, [H // 2], F16)
        m16 = view(r_w, 2560, [NB * NT], F16).rearrange("p (b t k) -> p b t k", b=NB, t=NT)
        ve16 = view(r_w, 2600, [NB * NT], F16).rearrange("p (b t k) -> p b t k", b=NB, t=NT)
        wqraw = view(r_t, 0, [KH, DH, NH])
        bqraw = view(r_t, 2048, [DH, NH])
        wqkv = view(r_s, 0, [KH, QKV])
        bqkv = view(r_s, 256, [QKV])
        sc = view(r_win, 0, [NT, DH, DH])
        pr = view(r_win, 1024, [NT, DH, DH])
        qkv = view(r_win, 2048, [NT, QKV])
        smax = view(r_win, 2304, [NT, DH])
        den = view(r_win, 2432, [NT, DH])
        num = view(r_win, 2560, [NT, DH])
        on = view(r_win, 2688, [NT, DH])
        wup = view(r_bc, 11264, [KH, 1024])
        wfc1 = view(r_bc, 15360, [KH, 256])
        wdn = view(r_win, 3072, [MI, H])
        wexp = view(r_u, 5632, [LAT, 256])
        wfc2 = view(r_u, 6144, [LAT, H])
        wgate = view(r_u, 7168, [KH, NE])
        h1 = view(r_t, 0, [2, L])
        h2 = view(r_t, 1024, [2, L])
        lat = view(r_t, 2048, [LAT, L])
        eo = view(r_t, 3072, [LAT, L])
        rt = view(r_w, 0, [2, H])
        ym = view(r_w, 1024, [2, H])
        top8 = view(r_w, 2048, [NB, NT, 8])
        rw = view(r_w, 2176, [NB, NT])
        gam = view(r_s, 320, [H])
        bet = view(r_u, 7200, [H])
        tmp = view(r_w, 3584, [H])
        otmp = view(r_s, 0, [2, H])
        zr = view(r_u, 4096, [512], I32)
        zi = view(r_u, 4608, [IPAD], I32)
        zs = view(r_u, 6144, [IPAD // 2], F16)
        zo = view(r_bc, 0, [IPAD])
        zdr = view(r_bc, 2048, [64], I32)
        zdi = view(r_bc, 2560, [H], I32)
        zds = view(r_bc, 3072, [H // 2], F16)
        zdo = view(r_bc, 3584, [H])
        shifts = view(r_bc, 4096, [8], I32)

        ld_x = [sem(f"ld_x{b}") for b in range(NB)]
        ld_const = sem("ld_const")
        ld_z = sem("ld_z")
        ld_win = [sem(f"ld_win{k}") for k in range(KH)]
        ld_ssmw = sem("ld_ssmw")
        ld_wout = [sem(f"ld_wout{b}") for b in range(NB)]
        ld_bc = [[sem(f"ld_bc{b}_{n}") for n in range(4)] for b in range(NB)]
        ld_stage = [sem(f"ld_stage{s}") for s in range(2)]
        ld_att = sem("ld_att")
        ld_moe = sem("ld_moe")
        ld_moe2 = sem("ld_moe2")
        bc_stored = sem("bc_stored")
        z_stored = sem("z_stored")
        x_stored = sem("x_stored")
        z_done = sem("z_done")
        a_ready = sem("a_ready")
        work_ready = sem("work_ready")
        taken = [sem(f"taken{j}") for j in range(4)]
        ssm_ready = sem("ssm_ready")
        stats_ready = sem("stats_ready")
        std_ready = sem("std_ready")
        xn_ready = sem("xn_ready")
        conv_ready = sem("conv_ready")
        u_ready = sem("u_ready")
        sq_ready = sem("sq_ready")
        ms_ready = sem("ms_ready")
        rms_ready = sem("rms_ready")
        ssmn_ready = sem("ssmn_ready")
        sp_ready = sem("sp_ready")
        dt_ready = sem("dt_ready")
        eps_ready = sem("eps_ready")
        exp_done = sem("exp_done")
        bmul_done = sem("bmul_done")
        scan_done = sem("scan_done")
        cmul_done = sem("cmul_done")
        ysum_done = sem("ysum_done")
        y_taken = sem("y_taken")
        yg_done = sem("yg_done")
        q_done = sem("q_done")
        w_done = sem("w_done")
        acc_ready = sem("acc_ready")
        y16_done = sem("y16_done")
        wq_done = sem("wq_done")
        s_ready = sem("s_ready")
        p_ready = sem("p_ready")
        rw_ready = sem("rw_ready")
        h1_done = sem("h1_done")
        h2_done = sem("h2_done")
        ym_done = sem("ym_done")
        x_done = sem("x_done")
        down_used = sem("down_used")
        dve_chain = sem("dve_chain")
        pool_chain = sem("pool_chain")
        act_chain = sem("act_chain")

        block = ctx.enter_context(nc.Block())

        def bank(item):
            return psum[:, 4 + WORK[item] % 4, :]

        def taken_sem(item):
            return taken[WORK[item] % 4]

        def wait_work(eng, item):
            eng.wait_ge(work_ready, WORK[item] + 1)

        def wait_taken(eng, item):
            eng.wait_ge(taken_sem(item), WORK[item] // 4 + 1)

        NPAIR = DC * PAIRS
        XN = {}
        for item in WORK:
            if item[0] == "tr":
                XN[item[1:]] = len(XN)

        @block.sync
        def _(sp_):
            def load(dst, src, s):
                sp_.dma_start(dst, src).then_inc(s, 16)

            load(x[:, 0:NT, :], x_in[0:L, :].rearrange("(t p) n -> p t n", p=P), ld_x[0])
            load(ident[:], ident_in, ld_const)
            load(meanmat[:], meanmat_in, ld_const)
            load(shift[:], shift_in, ld_const)
            load(convw, conv_in.rearrange("p (c k) -> p c k", c=DC), ld_const)
            load(par, par_in.rearrange("p (c k) -> p c k", c=3), ld_const)
            load(aneg, alog_in.rearrange("p (c k) -> p c k", c=DC), ld_const)
            for k in range(KH):
                load(w_in_sb[:, k, :], w_in[k * P:(k + 1) * P, :], ld_win[k])
            load(wx, wx_in.rearrange("p (c k) -> p c k", c=DC), ld_ssmw)
            load(wdt[0:R, :], wdt_in, ld_ssmw)
            load(x[:, NT:2 * NT, :], x_in[L:2 * L, :].rearrange("(t p) n -> p t n", p=P), ld_x[1])
            load(zr[0:8, 0:176], zgu_in, ld_z)
            load(zs[0:8, :], sgu_in, ld_z)
            load(zdr[0:IC, :], zd_in, ld_z)
            load(zds[0:IC, :], sd_in, ld_z)
            load(shifts, shifts_in, ld_z)
            sp_.wait_ge(z_done, 2)
            sp_.dma_start(zgu_dram, zo[0:8, :]).then_inc(z_stored, 16)
            sp_.dma_start(zd_dram, zdo[0:IC, :]).then_inc(z_stored, 16)
            sp_.wait_ge(z_stored, 32)
            for b in range(NB):
                sp_.wait_ge(ssmn_ready, b + 1)
                sp_.dma_start(bc_dram[b], ssmn[R:R + 2 * NS, :]).then_inc(bc_stored, 16)
                sp_.wait_ge(bc_stored, 16 * (b + 1))
                if b:
                    sp_.wait_ge(cmul_done, NPAIR * b)
                for n in range(4):
                    for h in range(2):
                        a = h * NS + n * 4
                        load(bc[:, a:a + 4, :], bc_dram[b:b + 1, a:a + 4, :].broadcast_to([P, 4, L]), ld_bc[b][n])
                wait_taken(sp_, ("gate", b, DC - 1))
                sp_.wait_ge(u_ready, DC * (b + 1))
                load(wout, wout_in.rearrange("p (c k) -> p c k", c=DC), ld_wout[b])

            wait_taken(sp_, ("gate", NB - 1, DC - 1))
            for i in range(IC):
                s = i % 2
                if i >= 2:
                    sp_.wait_ge(w_done, 2 * (i - 1))
                cols = slice(i * P, (i + 1) * P)
                load(q_gu[s].rearrange("p a b -> p (a b)"),
                     qgu_in[i].rearrange("r n -> r () n").broadcast_to([16, 8, 2 * KH * P]), ld_stage[s])
                load(q_d[s], qd_in[i].rearrange("r n -> r () n").broadcast_to([16, 8, H]), ld_stage[s])
                load(s_gu[s].rearrange("p (a b) -> p a b", a=2 * KH),
                     sgu_in[:, cols].rearrange("(o g) n -> o g n", o=1).broadcast_to([P, 2 * KH, P]), ld_stage[s])
                load(z_gu[s], zgu_dram[:, cols].rearrange("(o g) n -> o g n", o=1).broadcast_to([P, 2 * KH, P]),
                     ld_stage[s])
                load(s_d[s], sd_in[i:i + 1, :].broadcast_to([P, H]), ld_stage[s])
                load(z_d[s], zd_dram[i:i + 1, :].broadcast_to([P, H]), ld_stage[s])
                if i == 0:
                    sp_.wait_ge(yg_done, NB * DC)
                    load(wqraw.rearrange("p a b c -> p (a b c)"), wq_in, ld_att)
                    load(bqraw.rearrange("p b c -> p (b c)"), bq_in.broadcast_to([P, DH * NH]), ld_att)
                    wait_taken(sp_, ("out", NB - 1, NT - 1))
                    load(wqkv[:, :, DH:QKV], wkv_in.rearrange("p (c k) -> p c k", c=KH), ld_att)
                    load(bqkv[:, DH:QKV], bkv_in.broadcast_to([P, 2 * DH]), ld_att)
                    load(wup, up_in.rearrange("(k p) n -> p k n", p=P), ld_moe)
                    load(wfc1, fc1_in.rearrange("(k p) n -> p k n", p=P), ld_moe)
                    load(wexp, exp_in.rearrange("(k p) n -> p k n", p=P), ld_moe)
                    load(wfc2, fc2_in.rearrange("(k p) n -> p k n", p=P), ld_moe)
                    load(wgate, gate_in.rearrange("p (c k) -> p c k", c=KH), ld_moe)
            load_gb_after = 2 * IC
            sp_.wait_ge(w_done, load_gb_after)
            load(wdn, down_in.rearrange("(k p) n -> p k n", p=P), ld_moe2)
            load(gam, gamma_in.broadcast_to([P, H]), ld_moe2)
            load(bet, beta_in.broadcast_to([P, H]), ld_moe2)
            for n in range(NB * NT):
                sp_.wait_ge(x_done, n + 1)
                sp_.dma_start(out[n * P:(n + 1) * P, :], x[:, n, :]).then_inc(x_stored, 16)
            sp_.wait_ge(x_stored, 16 * NB * NT)

        @block.tensor
        def _(pe):
            def start(item):
                if WORK[item] >= 4:
                    pe.wait_ge(taken_sem(item), WORK[item] // 4)

            def turn(layer, b, t, src):
                item = ("tr", layer, b, t)
                start(item)
                pe.wait_ge(xn_ready, XN[item[1:]] + 1)
                n = XN[item[1:]] % 2
                for k in range(KH):
                    last = pe.transpose(bank(item)[:, k * P:(k + 1) * P], src[:, n, k * P:(k + 1) * P], ident[:])
                last.then_inc(work_ready, 1)

            def product(item, parts, rows=P, cols=slice(0, L)):
                for n, (lhsT, rhs) in enumerate(parts):
                    last = pe.matmul(bank(item)[0:rows, cols], lhsT, rhs, start=(n == 0), stop=(n == len(parts) - 1))
                return last

            pe.wait_ge(ld_const, 16 * 6)
            for b in range(NB):
                for t in range(NT):
                    turn("ssm", b, t, xn)
                for t in range(NT):
                    wait_taken(pe, ("tr", "ssm", b, t))

                def ssm_part(c):
                    pe.wait_ge(u_ready, b * DC + c + 1)
                    last = pe.matmul(psum[0:64, 3, :], wx[:, c, :], u[:, c, :], start=(c == 0), stop=(c == DC - 1))
                    if c == DC - 1:
                        last.then_inc(ssm_ready, 1)

                for c in range(DC):
                    item = ("x", b, c)
                    start(item)
                    if b == 0 and c == 0:
                        for k in range(KH):
                            pe.wait_ge(ld_win[k], 16)
                    product(item, [(w_in_sb[:, k, c * P:(c + 1) * P], xT[:, k, :]) for k in range(KH)])\
                        .then_inc(work_ready, 1)
                    if b == 0 and c == 2:
                        pe.wait_ge(ld_ssmw, 32)
                    if c >= 2:
                        ssm_part(c - 2)
                for c in range(DC):
                    item = ("gate", b, c)
                    start(item)
                    product(item, [(w_in_sb[:, k, DIN + c * P:DIN + (c + 1) * P], xT[:, k, :]) for k in range(KH)])\
                        .then_inc(work_ready, 1)
                    if c < 2:
                        ssm_part(DC - 2 + c)
                    if c == 2:
                        start(("ms", b))
                        pe.wait_ge(sq_ready, b + 1)
                        pe.matmul(bank(("ms", b))[0:64, :], meanmat[:], sq[0:64, :], start=True, stop=True)\
                            .then_inc(work_ready, 1)
                pe.wait_ge(ssmn_ready, b + 1)
                for c in range(DC):
                    item = ("dt", b, c)
                    start(item)
                    pe.matmul(bank(item), wdt[0:R, c * P:(c + 1) * P], ssmn[0:R, :], start=True, stop=True)\
                        .then_inc(work_ready, 1)
                for i in range(NPAIR):
                    c, p = divmod(i, PAIRS)
                    if p == 0 and b * DC + c >= 2:
                        pe.wait_ge(y_taken, b * DC + c - 1)
                    pe.wait_ge(cmul_done, b * NPAIR + i + 1)
                    for j in range(2):
                        last = pe.matmul(psum[:, 6 + c % 2, :], ident[:], hc[:, i % 2, j, :],
                                         start=(p == 0 and j == 0), stop=(p == PAIRS - 1 and j == 1))
                    last.then_inc(ysum_done, 1)
                pe.wait_ge(ld_wout[b], 16)
                pe.wait_ge(yg_done, DC * (b + 1))
                for t in range(NT):
                    item = ("out", b, t)
                    start(item)
                    product(item, [(g[:, c, t * P:(t + 1) * P], wout[:, c, :]) for c in range(DC)])\
                        .then_inc(work_ready, 1)

            for b in range(NB):
                for t in range(NT):
                    turn("ffn", b, t, xnc)
                for t in range(NT):
                    wait_taken(pe, ("tr", "ffn", b, t))

                def down(i):
                    wait_taken(pe, ("u", b, i))
                    if i == 0 and b:
                        pe.wait_ge(y16_done, NT * b)
                    for t in range(NT):
                        last = pe.matmul(psum[:, t, :], inter[:, (b * IC + i) % 2, t * P:(t + 1) * P], wd[:, i, :],
                                         start=(i == 0), stop=(i == IC - 1))
                    last.then_inc(down_used, 1)
                    if i == IC - 1:
                        pass

                for i in range(IC):
                    if b == 0:
                        pe.wait_ge(w_done, 2 * (i + 1))
                    for j, name in enumerate("gu"):
                        item = (name, b, i)
                        start(item)
                        last = product(item, [(wgu[:, i, 2 * k + j, :], xTc[:, k, :]) for k in range(KH)])
                        last.then_inc(work_ready, 1)
                    if i >= 1:
                        down(i - 1)
                down(IC - 1)

            pe.wait_ge(ld_att, 64)
            pe.wait_ge(wq_done, 2)
            for b in range(NB):
                for t in range(NT):
                    turn("att", b, t, xnc)
                for t in range(NT):
                    wait_taken(pe, ("tr", "att", b, t))
                start(("qkv", b))
                for t in range(NT):
                    last = product(("qkv", b), [(xTc[:, k, t * P:(t + 1) * P], wqkv[:, k, :]) for k in range(KH)],
                                   cols=slice(t * QKV, (t + 1) * QKV))
                last.then_inc(work_ready, 1)

            pe.wait_ge(ld_moe, 16 * 5)
            pe.wait_ge(ld_moe2, 16 * 3)
            for b in range(NB):
                for t in range(NT):
                    turn("moe", b, t, xnc)
                for t in range(NT):
                    wait_taken(pe, ("tr", "moe", b, t))
                start(("logits", b))
                for t in range(NT):
                    last = product(("logits", b), [(xTc[:, k, t * P:(t + 1) * P], wgate[:, k, :]) for k in range(KH)],
                                   cols=slice(t * NE, (t + 1) * NE))
                last.then_inc(work_ready, 1)
                for m in range(LAT):
                    item = ("fc1", b, m)
                    start(item)
                    product(item, [(wfc1[:, k, m * P:(m + 1) * P], xTc[:, k, :]) for k in range(KH)])\
                        .then_inc(work_ready, 1)
                for m in range(LAT):
                    item = ("exp", b, m)
                    start(item)
                    for k in range(LAT):
                        wait_taken(pe, ("fc1", b, k))
                    product(item, [(wexp[:, k, m * P:(m + 1) * P], lat[:, k, :]) for k in range(LAT)])\
                        .then_inc(work_ready, 1)

                def moe_down(i):
                    pe.wait_ge(h2_done, b * MI + i + 1)
                    if i == 0 and b:
                        pe.wait_ge(ym_done, NT * b)
                    for t in range(NT):
                        last = pe.matmul(psum[:, t, :], h2[:, i % 2, t * P:(t + 1) * P], wdn[:, i, :],
                                         start=(i == 0), stop=(i == MI - 1))
                    last.then_inc(down_used, 1)

                for i in range(MI):
                    item = ("up", b, i)
                    start(item)
                    product(item, [(wup[:, k, i * P:(i + 1) * P], xTc[:, k, :]) for k in range(KH)])\
                        .then_inc(work_ready, 1)
                    if i >= 1:
                        moe_down(i - 1)
                moe_down(MI - 1)
                for k in range(LAT):
                    wait_taken(pe, ("exp", b, k))
                for t in range(NT):
                    item = ("routed", b, t)
                    start(item)
                    product(item, [(eo[:, k, t * P:(t + 1) * P], wfc2[:, k, :]) for k in range(LAT)])\
                        .then_inc(work_ready, 1)

        @block.vector
        def _(dve):
            n_chain = [0]

            def link(ins):
                n_chain[0] += 1
                ins.then_inc(dve_chain, 1)
                dve.wait_ge(dve_chain, n_chain[0])

            def stats(group, tiles):
                n = LN[group]
                for j, tile in enumerate(tiles):
                    last = dve.bn_stats(bst[:, j, :], tile)
                link(last)
                for j in range(len(tiles)):
                    last = dve.bn_aggr(mv[:, n, j, :], bst[:, j, :])
                last.then_inc(stats_ready, 1)
                dve.wait_ge(stats_ready, n + 1)

            def inv_std(group, tiles):
                n = LN[group]
                dve.wait_ge(std_ready, n + 1)
                link(dve.reciprocal(rstd[:, n, 0:tiles], std[:, n, 0:tiles]))

            def mean_of(group, j):
                return mv[:, LN[group], j, 0:1]

            def rstd_of(group, j):
                return rstd[:, LN[group], j:j + 1]

            def normalise(layer, b, dst):
                stats((layer, b), [x[:, b * NT + t, :] for t in range(NT)])
                inv_std((layer, b), NT)
                for t in range(NT):
                    n = XN[(layer, b, t)]
                    if t >= 2:
                        wait_work(dve, ("tr", layer, b, t - 2))
                    dve.tensor_scalar(dst[:, n % 2, :], x[:, b * NT + t, :], mean_of((layer, b), t),
                                      rstd_of((layer, b), t), ALU.subtract, ALU.mult).then_inc(xn_ready, 1)

            dve.memset(epst[:, 0:1], EPS)
            dve.memset(epst[:, 1:2], 0.0).then_inc(eps_ready, 1)
            dve.wait_ge(ld_x[0], 16)
            dve.wait_ge(ld_const, 16 * 6)
            normalise("ssm", 0, xn)
            dve.wait_ge(ld_z, 16 * 5)
            n_words = IPAD // 8
            zi3 = zi[0:8, :].rearrange("p (a b) -> p a b", b=8)
            link(dve.tensor_tensor(zi3, zr[0:8, 0:n_words].unsqueeze(2).broadcast_to([8, n_words, 8]),
                                   shifts[0:8, :].unsqueeze(1).broadcast_to([8, n_words, 8]),
                                   ALU.logical_shift_right))
            link(dve.tensor_scalar(zi[0:8, :], zi[0:8, :], 15, None, ALU.bitwise_and))
            dve.scalar_tensor_tensor(zo[0:8, :], zi[0:8, :], 1.0, zs[0:8, :], ALU.add, ALU.mult).then_inc(z_done, 1)
            zdi3 = zdi[0:IC, :].rearrange("p (a b) -> p a b", b=8)
            link(dve.tensor_tensor(zdi3, zdr[0:IC, :].unsqueeze(2).broadcast_to([IC, 64, 8]),
                                   shifts[0:IC, :].unsqueeze(1).broadcast_to([IC, 64, 8]),
                                   ALU.logical_shift_right))
            link(dve.tensor_scalar(zdi[0:IC, :], zdi[0:IC, :], 15, None, ALU.bitwise_and))
            dve.scalar_tensor_tensor(zdo[0:IC, :], zdi[0:IC, :], 1.0, zds[0:IC, :], ALU.add, ALU.mult)\
                .then_inc(z_done, 1)

            for b in range(NB):
                if b:
                    dve.wait_ge(ld_x[1], 16)
                    wait_work(dve, ("out", b - 1, NT - 1))
                    normalise("ssm", b, xn)
                for c in range(DC):
                    item = ("x", b, c)
                    wait_work(dve, item)
                    if b * DC + c >= 2:
                        dve.wait_ge(u_ready, b * DC + c - 1)
                    a, src = cacc[:, c % 2, :], bank(item)
                    link(dve.tensor_scalar(a, src, convw[:, c, KCONV - 1:KCONV], par[:, 0, c:c + 1],
                                           ALU.mult, ALU.add))
                    for j in range(1, KCONV):
                        last = dve.scalar_tensor_tensor(a[:, j:], src[:, 0:L - j],
                                                        convw[:, c, KCONV - 1 - j:KCONV - j], a[:, j:],
                                                        ALU.mult, ALU.add)
                        if j < KCONV - 1:
                            link(last)
                    last.then_inc(taken_sem(item), 1)
                item = ("ms", b)
                wait_work(dve, item)
                dve.tensor_scalar(rr[0:64, :], bank(item)[0:64, :], EPS_RMS, None, ALU.add)\
                    .then_inc(taken_sem(item), 1)
                wait_taken(dve, item)
                dve.reciprocal(rr[0:64, :], rr[0:64, :]).then_inc(ms_ready, 1)
                dve.wait_ge(rms_ready, b + 1)
                dve.tensor_tensor(ssmn[0:64, :], ssm[0:64, :], rr[0:64, :], ALU.mult).then_inc(ssmn_ready, 1)
                if b == 0:
                    dve.wait_ge(z_done, 2)
                for c in range(DC):
                    item = ("dt", b, c)
                    wait_work(dve, item)
                    dve.tensor_scalar(dtv[:, c, :], bank(item), par[:, 1, c:c + 1], None, ALU.add)\
                        .then_inc(taken_sem(item), 1)
                for c in range(0, DC, 4):
                    if c == 0:
                        for j in range(4):
                            wait_taken(dve, ("dt", b, DC - 1 - j))
                        link(dve.memset(psum[:, 0:2 * SLOTS, 0:1], 0.0))
                    dve.wait_ge(sp_ready, 2 * b + c // 4 + 1)
                    dve.scalar_tensor_tensor(dtv[:, c:c + 4, :], dtv[:, c:c + 4, :], 0.0, sp[:, c:c + 4, :],
                                             ALU.max, ALU.add).then_inc(dt_ready, 1)

                def times_c(i):
                    p = i % PAIRS
                    k = b * NPAIR + i
                    dve.wait_ge(scan_done, k + 1)
                    if p % 2 == 0 and i < PAIRS:
                        dve.wait_ge(ld_bc[b][p // 2], 32)
                    if k >= 2:
                        dve.wait_ge(ysum_done, k - 1)
                    s = 2 * (i % SLOTS)
                    dve.tensor_tensor(hc[:, i % 2, :, :], psum[:, s:s + 2, :],
                                      bc[:, NS + 2 * p:NS + 2 * p + 2, :], ALU.mult).then_inc(cmul_done, 1)

                def gated(c):
                    k = b * DC + c
                    dve.wait_ge(ysum_done, PAIRS * (k + 1))
                    dve.scalar_tensor_tensor(u[:, c, :], u[:, c, :], par[:, 2, c:c + 1], psum[:, 6 + c % 2, :],
                                             ALU.mult, ALU.add).then_inc(y_taken, 1)
                    dve.wait_ge(y_taken, k + 1)
                    dve.tensor_tensor(g[:, c, :], g[:, c, :], u[:, c, :], ALU.mult).then_inc(yg_done, 1)

                for i in range(NPAIR):
                    k = b * NPAIR + i
                    dve.wait_ge(exp_done, k + 1)
                    dve.wait_ge(bmul_done, k + 1)
                    s = 2 * (i % SLOTS)
                    flat = psum[:, s:s + 2, :].rearrange("p a b -> p (a b)")
                    dve.tensor_tensor_scan(flat, flat, dbu[:, i % 2, :, :].rearrange("p a b -> p (a b)"), 0.0,
                                           ALU.mult, ALU.add).then_inc(scan_done, 1)
                    if i >= 1:
                        times_c(i - 1)
                    if i >= PAIRS and i % PAIRS == 2:
                        gated(i // PAIRS - 1)
                times_c(NPAIR - 1)
                gated(DC - 1)

                def out_stats(t):
                    wait_work(dve, ("out", b, t))
                    stats(("out", b, t), [bank(("out", b, t))])

                def out_add(t):
                    group = ("out", b, t)
                    inv_std(group, 1)
                    item = ("out", b, t)
                    dve.tensor_scalar(otmp[:, t % 2, :], bank(item), mean_of(group, 0), rstd_of(group, 0),
                                      ALU.subtract, ALU.mult).then_inc(taken_sem(item), 1)
                    wait_taken(dve, item)
                    link(dve.tensor_tensor(x[:, b * NT + t, :], x[:, b * NT + t, :], otmp[:, t % 2, :], ALU.add))

                for t in range(NT):
                    out_stats(t)
                    if t:
                        out_add(t - 1)
                out_add(NT - 1)

            def unpack(i):
                s = i % 2
                dve.wait_ge(ld_stage[s], 96 * (i // 2 + 1))
                dve.tensor_scalar(q_gu[s], q_gu[s], shift[:, 0:1], 15, ALU.logical_shift_right, ALU.bitwise_and)
                link(dve.tensor_scalar(q_d[s], q_d[s], shift[:, 0:1], 15, ALU.logical_shift_right,
                                       ALU.bitwise_and))
                dve.tensor_tensor(wgu[:, i, :, :].rearrange("p a b -> p (a b)"),
                                  q_gu[s].rearrange("p a b -> p (a b)"), s_gu[s], ALU.mult).then_inc(q_done, 1)
                dve.tensor_tensor(wd[:, i, :], q_d[s], s_d[s], ALU.mult).then_inc(q_done, 1)

            def ffn_stats16(b):
                dve.wait_ge(y16_done, NT * (b + 1))
                n = LN[("ffn16", b)]
                for t in range(NT):
                    last = dve.bn_stats(bst[:, t, :], y16[:, t, :])
                link(last)
                for t in range(NT):
                    last = dve.bn_aggr(mv[:, n, t, :], bst[:, t, :])
                link(last)
                link(dve.tensor_copy(m16[:, b, :, :], mv[:, n, :, :]))
                dve.tensor_scalar(ve16[:, b, :, 0], m16[:, b, :, 1], EPS16, None, ALU.add).then_inc(stats_ready, 1)
                dve.wait_ge(stats_ready, n + 1)

            def ffn_add16(b):
                n = LN[("ffn16", b)]
                dve.wait_ge(std_ready, n + 1)
                link(dve.reciprocal(rstd[:, n, :], ve16[:, b, :, 1]))
                for t in range(NT):
                    link(dve.tensor_scalar(d16, y16[:, t, :], m16[:, b, t, 0:1], None, ALU.subtract))
                    link(dve.tensor_scalar(n16, d16, rstd[:, n, t:t + 1], None, ALU.mult))
                    link(dve.tensor_tensor(x[:, b * NT + t, :], x[:, b * NT + t, :], n16, ALU.add))

            unpack(0)
            unpack(1)
            for b in range(NB):
                normalise("ffn", b, xnc)
                for i in range(IC):
                    k = b * IC + i
                    wait_taken(dve, ("g", b, i))
                    wait_work(dve, ("u", b, i))
                    if k >= 2:
                        dve.wait_ge(down_used, k - 1)
                    dve.tensor_tensor(inter[:, k % 2, :], sg[:, k % 2, :], bank(("u", b, i)), ALU.mult)\
                        .then_inc(taken_sem(("u", b, i)), 1)
                    if b == 0 and i + 2 < IC:
                        unpack(i + 2)
                ffn_stats16(b)
                ffn_add16(b)

            dve.wait_ge(ld_att, 64)
            dve.tensor_reduce(wqkv[:, :, 0:DH], wqraw, AX.X, ALU.add).then_inc(wq_done, 1)
            dve.tensor_reduce(bqkv[:, 0:DH], bqraw, AX.X, ALU.add).then_inc(wq_done, 1)
            dve.wait_ge(wq_done, 2)
            for b in range(NB):
                normalise("att", b, xnc)
            for b in range(NB):
                item = ("qkv", b)
                wait_work(dve, item)
                dve.tensor_tensor(qkv, bank(item)[:, 0:NT * QKV].rearrange("p (a b) -> p a b", a=NT),
                                  bqkv.unsqueeze(1).broadcast_to([P, NT, QKV]), ALU.add)\
                    .then_inc(taken_sem(item), 1)
                wait_taken(dve, item)
                full = [P, NT, DH, DH]
                q_b = qkv[:, :, 0:DH].unsqueeze(3).broadcast_to(full)
                k_b = qkv[:, :, DH:2 * DH].unsqueeze(2).broadcast_to(full)
                v_b = qkv[:, :, 2 * DH:].unsqueeze(2).broadcast_to(full)
                link(dve.tensor_tensor(sc, q_b, k_b, ALU.mult))
                link(dve.tensor_reduce(smax, sc, AX.X, ALU.max))
                dve.tensor_tensor(sc, sc, smax.unsqueeze(3).broadcast_to(full), ALU.subtract).then_inc(s_ready, 1)
                dve.wait_ge(p_ready, b + 1)
                dve.tensor_reduce(den, pr, AX.X, ALU.add)
                link(dve.tensor_tensor(sc, pr, v_b, ALU.mult))
                dve.tensor_reduce(num, sc, AX.X, ALU.add)
                link(dve.reciprocal(den, den))
                link(dve.tensor_tensor(num, num, den, ALU.mult))
                group = ("atto", b)
                stats(group, [num[:, t, :] for t in range(NT)])
                inv_std(group, NT)
                for t in range(NT):
                    last = dve.tensor_scalar(on[:, t, :], num[:, t, :], mean_of(group, t), rstd_of(group, t),
                                             ALU.subtract, ALU.mult)
                link(last)
                for t in range(NT):
                    x3 = x[:, b * NT + t, :].rearrange("p (d h) -> p d h", d=DH)
                    last = dve.tensor_tensor(x3, x3, on[:, t, :].unsqueeze(2).broadcast_to([P, DH, NH]), ALU.add)
                link(last)

            dve.wait_ge(ld_moe2, 16 * 3)
            for b in range(NB):
                normalise("moe", b, xnc)
                item = ("logits", b)
                wait_work(dve, item)
                for t in range(NT):
                    last = dve.max(top8[:, b, t, :], bank(item)[:, t * NE:(t + 1) * NE])
                last.then_inc(taken_sem(item), 1)
                wait_taken(dve, item)
                dve.tensor_tensor(rw[:, b, :], top8[:, b, :, 0], top8[:, b, :, 1], ALU.add).then_inc(rw_ready, 1)
                for t in range(NT):
                    k = b * NT + t
                    y = ym[:, t % 2, :]
                    dve.wait_ge(down_used, NB * IC + MI * (b + 1))
                    wait_taken(dve, ("routed", b, t))
                    dve.tensor_tensor(y, psum[:, t, :], rt[:, t % 2, :], ALU.add).then_inc(ym_done, 1)
                    dve.wait_ge(ym_done, k + 1)
                    group = ("moei", b, t)
                    stats(group, [y])
                    inv_std(group, 1)
                    link(dve.tensor_scalar(y, y, mean_of(group, 0), rstd_of(group, 0), ALU.subtract, ALU.mult))
                    link(dve.tensor_tensor(y, y, gam, ALU.mult))
                    link(dve.tensor_tensor(y, y, bet, ALU.add))
                    group = ("moeo", b, t)
                    stats(group, [y])
                    inv_std(group, 1)
                    link(dve.tensor_scalar(y, y, mean_of(group, 0), rstd_of(group, 0), ALU.subtract, ALU.mult))
                    dve.tensor_tensor(x[:, k, :], x[:, k, :], y, ALU.add).then_inc(x_done, 1)
                    dve.wait_ge(x_done, k + 1)

        @block.scalar
        def _(act):
            def root(group, tiles):
                n = LN[group]
                act.wait_ge(stats_ready, n + 1)
                act.activation(std[:, n, 0:tiles], mv[:, n, 0:tiles, 1], ACT.Sqrt, bias=epst[:, 0:1])\
                    .then_inc(std_ready, 1)

            def take_turned(layer, b, dst):
                for t in range(NT):
                    item = ("tr", layer, b, t)
                    wait_work(act, item)
                    act.copy(dst[:, :, t * P:(t + 1) * P], bank(item).rearrange("p (k t) -> p k t", k=KH))\
                        .then_inc(taken_sem(item), 1)

            act.wait_ge(eps_ready, 1)
            for b in range(NB):
                root(("ssm", b), NT)
                take_turned("ssm", b, xT)
                for c in range(DC):
                    item = ("x", b, c)
                    wait_taken(act, item)
                    act.activation(u[:, c, :], cacc[:, c % 2, :], ACT.Silu).then_inc(u_ready, 1)
                for c in range(DC):
                    item = ("gate", b, c)
                    wait_work(act, item)
                    act.activation(g[:, c, :], bank(item), ACT.Silu).then_inc(taken_sem(item), 1)
                    if c == 1:
                        act.wait_ge(ssm_ready, b + 1)
                        act.copy(ssm[0:64, :], psum[0:64, 3, :])
                        act.activation(sq[0:64, :], psum[0:64, 3, :], ACT.Square).then_inc(sq_ready, 1)
                act.wait_ge(ms_ready, b + 1)
                act.activation(rr[0:64, :], rr[0:64, :], ACT.Sqrt).then_inc(rms_ready, 1)
                if b == 0:
                    act.wait_ge(ld_const, 16 * 6)
                    act.activation(aneg, aneg, ACT.Exp).then_inc(act_chain, 1)
                    act.wait_ge(act_chain, 1)
                    act.mul(aneg, aneg, -1.0).then_inc(a_ready, 1)
                hv = [slice(h * 4, h * 4 + 4) for h in range(2)]
                n0 = 1 + b * 4
                act.wait_ge(ssmn_ready, b + 1)
                for h in range(2):
                    for c in range(4):
                        wait_taken(act, ("dt", b, 4 * h + c))
                    act.activation(sp[:, hv[h], :], dtv[:, hv[h], :], ACT.Abs).then_inc(act_chain, 1)
                for h in range(2):
                    act.wait_ge(act_chain, n0 + h + 1)
                    act.activation(sp[:, hv[h], :], sp[:, hv[h], :], ACT.Exp, scale=-1.0).then_inc(act_chain, 1)
                for h in range(2):
                    act.wait_ge(act_chain, n0 + h + 3)
                    act.activation(sp[:, hv[h], :], sp[:, hv[h], :], ACT.Ln, bias=1.0).then_inc(sp_ready, 1)
                act.wait_ge(a_ready, 1)
                for i in range(NPAIR):
                    c, p = divmod(i, PAIRS)
                    k = b * NPAIR + i
                    act.wait_ge(dt_ready, 2 * b + c // 4 + 1)
                    if i == 0:
                        act.wait_ge(dt_ready, 2 * b + 1)
                    if i >= SLOTS:
                        act.wait_ge(cmul_done, k - SLOTS + 1)
                    for j in range(2):
                        last = act.activation(psum[:, 2 * (i % SLOTS) + j, 1:], dtv[:, c, 1:], ACT.Exp,
                                              scale=aneg[:, c, 2 * p + j:2 * p + j + 1])
                    last.then_inc(exp_done, 1)
                for t in range(NT):
                    root(("out", b, t), 1)

            for b in range(NB):
                root(("ffn", b), NT)
                wait_taken(act, ("out", NB - 1, NT - 1))
                take_turned("ffn", b, xTc)
                for i in range(IC):
                    k = b * IC + i
                    item = ("g", b, i)
                    wait_work(act, item)
                    if k >= 2:
                        wait_taken(act, ("u", (k - 2) // IC, (k - 2) % IC))
                    act.activation(sg[:, k % 2, :], bank(item), ACT.Silu).then_inc(taken_sem(item), 1)
                act.wait_ge(down_used, IC * (b + 1))
                for t in range(NT):
                    act.copy(y16[:, t, :], psum[:, t, :]).then_inc(y16_done, 1)
                n = LN[("ffn16", b)]
                act.wait_ge(stats_ready, n + 1)
                act.activation(ve16[:, b, :, 1], ve16[:, b, :, 0], ACT.Sqrt).then_inc(std_ready, 1)

            for b in range(NB):
                root(("att", b), NT)
                take_turned("att", b, xTc)
            for b in range(NB):
                act.wait_ge(s_ready, b + 1)
                act.activation(pr, sc, ACT.Exp, scale=float(DH) ** -0.5).then_inc(p_ready, 1)
                root(("atto", b), NT)

            for b in range(NB):
                root(("moe", b), NT)
                take_turned("moe", b, xTc)
                for m in range(LAT):
                    item = ("fc1", b, m)
                    wait_work(act, item)
                    act.copy(lat[:, m, :], bank(item)).then_inc(taken_sem(item), 1)
                for m in range(LAT):
                    item = ("exp", b, m)
                    wait_work(act, item)
                    act.copy(eo[:, m, :], bank(item)).then_inc(taken_sem(item), 1)
                for i in range(MI):
                    k = b * MI + i
                    item = ("up", b, i)
                    wait_work(act, item)
                    if k >= 2:
                        act.wait_ge(h2_done, k - 1)
                    act.activation(h1[:, i % 2, :], bank(item), ACT.Relu).then_inc(taken_sem(item), 1)
                act.wait_ge(rw_ready, b + 1)
                for t in range(NT):
                    k = b * NT + t
                    item = ("routed", b, t)
                    wait_work(act, item)
                    if k >= 2:
                        act.wait_ge(ym_done, k - 1)
                    act.activation(rt[:, t % 2, :], bank(item), ACT.Identity, scale=rw[:, b, t:t + 1])\
                        .then_inc(taken_sem(item), 1)
                    root(("moei", b, t), 1)
                    root(("moeo", b, t), 1)

        @block.gpsimd
        def _(pool):
            n_chain = 0
            for b in range(NB):
                for i in range(NPAIR):
                    c, p = divmod(i, PAIRS)
                    k = b * NPAIR + i
                    if p == 0:
                        pool.wait_ge(dt_ready, 2 * b + 2 if c >= 4 else 2 * b + 1)
                        if i == 0:
                            pool.wait_ge(bc_stored, 16 * (b + 1))
                            pool.wait_ge(dt_ready, 2 * b + 2)
                        pool.tensor_tensor(du[:, c % 2, :], dtv[:, c, :], u[:, c, :], ALU.mult)\
                            .then_inc(pool_chain, 1)
                        n_chain += 1
                        pool.wait_ge(pool_chain, n_chain)
                    if i >= 2:
                        pool.wait_ge(scan_done, k - 1)
                    if p % 2 == 0 and i < PAIRS:
                        pool.wait_ge(ld_bc[b][p // 2], 32)
                    pool.tensor_tensor(dbu[:, i % 2, :, :], du[:, c % 2, :].unsqueeze(1).broadcast_to([P, 2, L]),
                                       bc[:, 2 * p:2 * p + 2, :], ALU.mult).then_inc(bmul_done, 1)
            for i in range(IC):
                s = i % 2
                pool.wait_ge(q_done, 2 * i + 2)
                w2 = wgu[:, i, :, :]
                pool.tensor_tensor(w2, w2, z_gu[s], ALU.subtract).then_inc(w_done, 1)
                pool.tensor_tensor(wd[:, i, :], wd[:, i, :], z_d[s], ALU.subtract).then_inc(w_done, 1)
            for b in range(NB):
                for i in range(MI):
                    k = b * MI + i
                    wait_taken(pool, ("up", b, i))
                    if k >= 2:
                        pool.wait_ge(down_used, NB * IC + k - 1)
                    pool.tensor_tensor(h2[:, i % 2, :], h1[:, i % 2, :], h1[:, i % 2, :], ALU.mult)\
                        .then_inc(h2_done, 1)


def kernel(**inputs):
    import concourse.bacc as _bacc
    from concourse.bass_utils import run_bass_kernel_spmd as _run

    def arr(name):
        return np.ascontiguousarray(inputs[name])

    def cols(v):
        return np.reshape(v, (DC, P, -1)).transpose(1, 0, 2).reshape(P, -1)

    def chunks(w):
        k = w.shape[0] // P
        return np.reshape(w, (k, P, -1)).transpose(1, 0, 2).reshape(P, -1)

    def pad(a, rows, width):
        out = np.zeros((rows, width), a.dtype)
        out[:a.shape[0], :a.shape[1]] = a
        return out

    rms = np.zeros((64, 64), np.float32)
    for a, e in ((0, R), (R, R + NS), (R + NS, R + 2 * NS)):
        rms[a:e, a:e] = 1.0 / (e - a)

    def packed(name):
        return pad(arr(name), 64, IPAD).reshape(KH, 16, IC, P)

    def interleave(a, b_):
        return np.stack([a, b_], axis=1)

    qgu = np.stack([packed("L0_ffn_gate_qweight"), packed("L0_ffn_up_qweight")], axis=1)
    qgu = qgu.transpose(3, 2, 0, 1, 4).reshape(IC, 16, 2 * KH * P)
    sgu = interleave(pad(arr("L0_ffn_gate_scales"), KH, IPAD), pad(arr("L0_ffn_up_scales"), KH, IPAD))
    zgu = interleave(pad(arr("L0_ffn_gate_zeros"), KH, IPAD // 8), pad(arr("L0_ffn_up_zeros"), KH, IPAD // 8))

    arrays = {
        "x_in": arr("L0_attn_hidden_states").reshape(NB * L, H),
        "ident_in": np.eye(P, dtype=np.float32),
        "meanmat_in": rms,
        "shift_in": (np.arange(P, dtype=np.int32) % 8 * 4).reshape(P, 1),
        "shifts_in": np.tile(np.arange(8, dtype=np.int32) * 4, (P, 1)),
        "w_in": arr("L0_attn_W_in").T,
        "conv_in": cols(arr("L0_attn_conv_w")),
        "par_in": np.concatenate([cols(arr("L0_attn_conv_b")), cols(arr("L0_attn_b_dt")), cols(arr("L0_attn_D"))], 1),
        "alog_in": cols(arr("L0_attn_A_log")),
        "wx_in": chunks(arr("L0_attn_W_x").T),
        "wdt_in": arr("L0_attn_W_dt").T,
        "wout_in": chunks(arr("L0_attn_W_out").T),
        "qgu_in": qgu,
        "qd_in": pad(arr("L0_ffn_down_qweight"), IC * 16, H).reshape(IC, 16, H),
        "sgu_in": sgu.reshape(2 * KH, IPAD),
        "zgu_in": zgu.reshape(2 * KH, IPAD // 8),
        "sd_in": arr("L0_ffn_down_scales"),
        "zd_in": arr("L0_ffn_down_zeros"),
        "wq_in": chunks(arr("L1_attn_Wq").reshape(H, DH * NH)),
        "wkv_in": chunks(np.concatenate([arr("L1_attn_Wk").reshape(H, DH), arr("L1_attn_Wv").reshape(H, DH)], 1)),
        "bq_in": arr("L1_attn_bq").reshape(1, DH * NH),
        "bkv_in": np.concatenate([arr("L1_attn_bk").reshape(1, DH), arr("L1_attn_bv").reshape(1, DH)], 1),
        "gate_in": chunks(arr("L1_ffn_gate_w")),
        "up_in": arr("L1_ffn_up_w"),
        "down_in": arr("L1_ffn_down_w"),
        "fc1_in": arr("L1_ffn_fc1_w"),
        "fc2_in": arr("L1_ffn_fc2_w"),
        "exp_in": arr("L1_ffn_expert_w"),
        "gamma_in": arr("L1_ffn_ln_gamma").reshape(1, H),
        "beta_in": arr("L1_ffn_ln_beta").reshape(1, H),
    }
    nc = _bacc.Bacc("TRN2", target_bir_lowering=False, num_devices=1)
    args = {}
    for name in list(arrays):
        a = np.ascontiguousarray(arrays[name])
        arrays[name] = a
        args[name] = nc.dram_tensor(name, a.shape, mybir.dt.from_np(a.dtype), kind="ExternalInput").ap()
    args["out"] = nc.dram_tensor("out", [NB * L, H], F32, kind="ExternalOutput").ap()
    build(nc, **args)
    r = _run(nc, [arrays], core_ids=[0])
    return r.results[0]["out"].reshape(NB, L, H)
```

```python
import numpy as np

import concourse.bass as bass
from concourse import mybir
from contextlib import ExitStack

F32 = mybir.dt.float32
F16 = mybir.dt.float16
F32R = mybir.dt.float32r
I32 = mybir.dt.int32
ALU = mybir.AluOpType
ACT = mybir.ActivationFunctionType
AX = mybir.AxisListType

P = 128
NB = 2
L = 512
NT = L // P
H = 512
KH = H // P
DIN = 1024
DC = DIN // P
NS = 16
R = 32
KCONV = 4
INTER = 1376
IC = -(-INTER // P)
IPAD = IC * P
DH = 16
NH = 32
QKV = 3 * DH
MI = 1024 // P
LAT = 256 // P
RING = 3
NE = 8
SLOTS = 3
HCS = 4
EPS = 1e-5
EPS16 = float(np.float16(1e-5))
EPS_RMS = 1e-6


X_AT = [(0, 15)] + [(c, 5) for c in range(1, DC)]
CONV_AT = [(1, 3)] + [(c, 8) for c in range(1, DC)]
SP_PARTS = [slice(0, 2), slice(2, 4), slice(4, DC)]


def side_work(b, c, n):
    if b == 0:
        if c == 0 and n in (8, 9, 12, 13):
            return [("tr", "ssm", 1, (8, 9, 12, 13).index(n))]
        return [("x", 1, k) for k in range(DC) if (c, n) == X_AT[k]] + \
            [("ssm", 1, k) for k in range(DC - 1) if (c, n) == (k + 1, 12)]
    if n == 4:
        return [("gate", 1, c)]
    if c == 0 and n == 9:
        return [("out", 0, NT - 1)]
    return []


def pe_order():
    items = [("tr", "ssm", 0, t) for t in range(NT)] + [("x", 0, c) for c in range(DC)]
    for b in range(NB):
        if b == 0:
            between = [("gate", 0, c) for c in range(DC)]
            items += between[:1] + [("ms", b)] + between[1:3]
        else:
            between = [("out", 0, t) for t in range(NT)]
            items += [("ms", b)] + between[:1]
        items += [("dt", b, c) for c in range(DC)]
        items += between[3:] if b == 0 else between[1:NT - 1]
        for c in range(DC):
            for n in range(NS):
                items += [item for item in side_work(b, c, n) if item[0] != "ssm"]
    items += [("tr", "ffn", 0, t) for t in range(NT)]
    items += [("out", 1, t) for t in range(NT)]
    for i in range(IC):
        items += [("g", 0, i), ("u", 0, i)]
        if i == IC - 1:
            items += [("tr", "ffn", 1, t) for t in range(NT)]
    for i in range(IC):
        items += [("g", 1, i), ("u", 1, i)]
        if i == 4:
            items += [("tr", "att", 0, t) for t in range(NT)]
        if i == 5:
            items += [("qkv", 0)]
        if i == 9:
            items += [("tr", "moe", 0, t) for t in range(NT)]
    for b in range(NB):
        items += [("logits", b)]
        items += [("fc1", b, m) for m in range(LAT)]
        items += [("exp", b, m) for m in range(LAT)]
        items += [("routed", b, t) for t in range(NT)]
        for i in range(MI):
            items += [("up", b, i)]
            if b == 0 and i == 2:
                items += [("tr", "att", 1, t) for t in range(NT)]
            if b == 0 and i == 3:
                items += [("qkv", 1)]
            if b == 0 and i == MI - 1:
                items += [("tr", "moe", 1, t) for t in range(NT)]
    return {item: n for n, item in enumerate(items)}


def ln_order():
    groups = [("ssm", 0), ("ssm", 1), ("out", 0), ("ffn", 0), ("out", 1), ("ffn", 1)]
    for b in range(NB):
        groups += [("ffn16", b), ("att", b), ("atto", b), ("moe", b)]
    for b in range(NB):
        groups += [("moei", b, t) for t in range(NT)] + [("moeo", b, t) for t in range(NT)]
    return {g: n for n, g in enumerate(groups)}


def build(nc, x_in, ident_in, meanmat_in, shift_in, shifts_in, w_in, conv_in, par_in, alog_in, wx_in, wdt_in,
          wout_in, qgu_in, qd_in, sgu_in, zgu_in, sd_in, zd_in, wq_in, wkv_in, bq_in, bkv_in, gate_in, up_in,
          down_in, fc1_in, fc2_in, exp_in, gamma_in, beta_in, out):
    WORK = pe_order()
    LN = ln_order()
    NG = len(LN)
    XN = {}
    for item in WORK:
        if item[0] == "tr":
            XN[item[1:]] = len(XN)
    NSTEP = DC * NS

    bc_dram = nc.dram_tensor("bc_scratch", [NB, 2 * NS, L], F32).ap()
    zgu_dram = nc.dram_tensor("zgu_scratch", [2 * KH, IPAD], F32).ap()
    zd_dram = nc.dram_tensor("zd_scratch", [IC, H], F32).ap()

    with ExitStack() as ctx:
        def sem(name):
            return ctx.enter_context(nc.semaphore(name))

        KB = 1024
        arena = ctx.enter_context(nc.sbuf_tensor("arena", [P, 207 * KB // 4], F32))
        base = nc.sbuf_base - 207 * KB

        def at(name, kb, shape, dt=F32):
            return nc.alloc_sbuf_tensor_at(name, [P, *shape], dt, offset=base + int(kb * KB))

        x = at("x", 0, [NB * NT, H])
        ident = at("ident", 16, [P])
        meanmat = at("meanmat", 16.5, [64])
        shift = at("shift", 16.75, [1], I32)
        epst = at("epst", 16.78125, [1])
        bst = at("bst", 16.8125, [NT, 6])
        mv = at("mv", 17, [NG, NT, 2])
        std = at("std", 18, [NG, NT])
        rstd = at("rstd", 18.5, [NG, NT])
        top8 = at("top8", 19, [NB, NT, 8])
        rw = at("rw", 19.25, [NB, NT])
        m16 = at("m16", 19.375, [NB, NT, 2], F16)
        ve16 = at("ve16", 19.5, [NB, NT, 2], F16)
        wx = at("wx", 20, [DC, 64])
        wdt = at("wdt", 22, [DIN])
        par = at("par", 26, [3, DC])
        convw = at("convw", 26.125, [DC, KCONV])
        aneg = at("aneg", 26.25, [DC, NS])
        w_x = at("w_x", 27, [KH, DIN])
        w_g = at("w_g", 43, [KH, DIN])
        wout = at("wout", 27, [DC, H])
        bc = at("bc", 59, [2 * NS, L])
        u = at("u", 123, [DC, L])
        dtv = at("dtv", 139, [DC, L])
        g = at("g", 155, [DC, L])
        sp = at("sp", 171, [DC, L])
        ssm = at("ssm", 171, [L])
        sq = at("sq", 173, [L])
        rr = at("rr", 175, [L])
        dbu = at("dbu", 171, [2, 2, L])
        hc = at("hc", 179, [HCS, L])
        xT = at("xT", 187, [KH, L])
        xn = at("xn", 195, [2, H])
        cacc = at("cacc", 199, [2, L])
        du = at("du", 203, [2, L])
        ssmn = at("ssmn", 203, [L])
        obuf = [at("obuf0", 195, [NT, H]), at("obuf1", 141, [NT, H])]
        zr = at("zr", 59, [IPAD // 8], I32)
        zi = at("zi", 60, [IPAD], I32)
        zs = at("zs", 66, [IPAD], F16)
        zo = at("zo", 69, [IPAD])
        zdr = at("zdr", 75, [H // 8], I32)
        zdi = at("zdi", 76, [H], I32)
        zds = at("zds", 78, [H], F16)
        zdo = at("zdo", 79, [H])
        shifts = at("shifts", 81, [8], I32)
        gu_hi = at("gu_hi", 59, [IC, 2 * KH * P], F16)
        gu_lo = at("gu_lo", 81, [IC, 2 * KH * P], F16)
        d_hi = at("d_hi", 103, [IC, H], F16)
        d_lo = at("d_lo", 114, [IC, H], F16)
        STG = [171, 43, 125]
        q_gu = [at(f"q_gu{s}", k, [2 * KH * P], I32) for s, k in enumerate(STG)]
        w_gu = [at(f"w_gu{s}", k, [2 * KH * P]) for s, k in enumerate(STG)]
        s_gu = [at(f"s_gu{s}", k + 4, [2 * KH * P], F16) for s, k in enumerate(STG)]
        z_gu = [at(f"z_gu{s}", k + 6, [2 * KH * P]) for s, k in enumerate(STG)]
        q_d = [at(f"q_d{s}", k + 10, [H], I32) for s, k in enumerate(STG)]
        w_d = [at(f"w_d{s}", k + 10, [H]) for s, k in enumerate(STG)]
        s_d = [at(f"s_d{s}", k + 12, [H], F16) for s, k in enumerate(STG)]
        z_d = [at(f"z_d{s}", k + 13, [H]) for s, k in enumerate(STG)]
        xf_hi = [at(f"xf_hi{b}", k, [KH, L], F16) for b, k in enumerate([187, 195])]
        xf_lo = [at(f"xf_lo{b}", k, [KH, L], F16) for b, k in enumerate([191, 199])]
        xnc = at("xnc", 149, [2, H])
        it = at("it", 27, [2, L])
        it_hi = at("it_hi", 31, [2, L], F16)
        it_lo = at("it_lo", 33, [2, L], F16)
        sg = at("sg", 39, [2, L])
        y16 = at("y16", 155, [NT, H], F16)
        d16 = at("d16", 159, [H], F16)
        n16 = at("n16", 160, [H], F16)
        wqraw = at("wqraw", 161, [KH, DH, NH])
        bqraw = at("bqraw", 169, [DH, NH])
        wqkv = at("wqkv", 20, [KH, QKV])
        bqkv = at("bqkv", 20.75, [QKV])
        gam = at("gam", 22, [H])
        bet = at("bet", 25, [H])
        xTa = [at("xTa0", 171, [KH, L]), at("xTa1", 97, [KH, L])]
        sc = at("sc", 179, [NT, DH, DH])
        pr = at("pr", 183, [NT, DH, DH])
        qkv = at("qkv", 153, [NT, QKV])
        smax = at("smax", 153.75, [NT, DH])
        den = at("den", 154, [NT, DH])
        num = at("num", 154.25, [NT, DH])
        on = at("on", 154.5, [NT, DH])
        moe_w = {}
        for name, kb, kb_hi, shape in (("up", 43, 125, [KH, MI * P]), ("down", 59, 81, [MI, H]),
                                       ("fc1", 161, 141, [KH, LAT * P]), ("exp", 165, 145, [LAT, LAT * P]),
                                       ("fc2", 167, 203, [LAT, H]), ("gate", 21, 24.5, [KH, NE])):
            moe_w[name] = (at(f"w_{name}", kb, shape), at(f"w_{name}_hi", kb_hi, shape, F32R),
                           at(f"w_{name}_lo", kb, shape, F32R))
        xm_hi = [at("xm_hi0", 187, [KH, L], F32R), at("xm_hi1", 105, [KH, L], F32R)]
        xm_lo = [at("xm_lo0", 171, [KH, L], F32R), at("xm_lo1", 113, [KH, L], F32R)]
        h1 = at("h1", 27, [2, L])
        h2 = at("h2", 31, [2, L])
        h2_hi = at("h2_hi", 121, [2, L], F32R)
        h2_lo = at("h2_lo", 75, [2, L], F32R)
        lat_hi = at("lat_hi", 195, [LAT, L], F32R)
        lat_lo = at("lat_lo", 199, [LAT, L], F32R)
        eo_hi = at("eo_hi", 97, [LAT, L], F32R)
        eo_lo = at("eo_lo", 101, [LAT, L], F32R)
        rt = [at("rt0", 35, [NT, H]), at("rt1", 171, [NT, H])]
        psum = ctx.enter_context(nc.psum_tensor("psum", [P, 8, L], F32))
        Y_BANK, SSM_BANK = 3, 4

        ld_x = [sem(f"ld_x{b}") for b in range(NB)]
        ld_const = sem("ld_const")
        ld_z = sem("ld_z")
        ld_wx = [sem(f"ld_wx{k}") for k in range(KH)]
        ld_wg = sem("ld_wg")
        ld_ssmw = sem("ld_ssmw")
        ld_wout = sem("ld_wout")
        ld_bc = [[sem(f"ld_bc{b}_{n}") for n in range(4)] for b in range(NB)]
        ld_stage = [sem(f"ld_stage{s}") for s in range(3)]
        ld_att = sem("ld_att")
        ld_moe = [sem(f"ld_moe{n}") for n in range(3)]
        bc_stored = sem("bc_stored")
        z_stored = sem("z_stored")
        x_stored = sem("x_stored")
        z_done = sem("z_done")
        a_ready = sem("a_ready")
        work_ready = sem("work_ready")
        taken = [sem(f"taken{j}") for j in range(RING)]
        ssm_ready = sem("ssm_ready")
        stats_ready = sem("stats_ready")
        std_ready = sem("std_ready")
        xn_ready = sem("xn_ready")
        conv_ready = sem("conv_ready")
        u_ready = sem("u_ready")
        sq_ready = sem("sq_ready")
        ms_ready = sem("ms_ready")
        rms_ready = sem("rms_ready")
        ssmn_ready = sem("ssmn_ready")
        sp_ready = sem("sp_ready")
        dt_ready = sem("dt_ready")
        eps_ready = sem("eps_ready")
        exp_done = sem("exp_done")
        bmul_done = sem("bmul_done")
        scan_done = sem("scan_done")
        cmul_done = sem("cmul_done")
        ysum_done = sem("ysum_done")
        y_taken = sem("y_taken")
        yg_done = sem("yg_done")
        gate_done = sem("gate_done")
        out_done = sem("out_done")
        q_done = sem("q_done")
        w_done = sem("w_done")
        whi_done = sem("whi_done")
        wlo_gu = sem("wlo_gu")
        wlo_d = sem("wlo_d")
        xhi_done = sem("xhi_done")
        it_done = sem("it_done")
        ithi_done = sem("ithi_done")
        itlo_done = sem("itlo_done")
        ffn_used = sem("ffn_used")
        y16_done = sem("y16_done")
        wq_done = sem("wq_done")
        s_ready = sem("s_ready")
        p_ready = sem("p_ready")
        rw_ready = sem("rw_ready")
        mw_hi = [sem(f"mw_hi{n}") for n in range(4)]
        mw_lo = [sem(f"mw_lo{n}") for n in range(4)]
        xmhi_done = sem("xmhi_done")
        lhi_done = sem("lhi_done")
        h2_done = sem("h2_done")
        h2hi_done = sem("h2hi_done")
        h2lo_done = sem("h2lo_done")
        down_done = sem("down_done")
        yn_done = sem("yn_done")
        moe_used = sem("moe_used")
        ym_done = sem("ym_done")
        x_done = sem("x_done")
        dve_chain = sem("dve_chain")
        pool_chain = sem("pool_chain")
        act_chain = sem("act_chain")

        block = ctx.enter_context(nc.Block())

        def bank(item):
            return psum[:, 8 - RING + WORK[item] % RING, :]

        def taken_sem(item):
            return taken[WORK[item] % RING]

        def wait_work(eng, item):
            eng.wait_ge(work_ready, WORK[item] + 1)

        def wait_taken(eng, item):
            eng.wait_ge(taken_sem(item), WORK[item] // RING + 1)

        @block.sync
        def _(sp_):
            def load(dst, src, s):
                sp_.dma_start(dst, src).then_inc(s, 16)

            load(x[:, 0:NT, :], x_in[0:L, :].rearrange("(t p) n -> p t n", p=P), ld_x[0])
            load(ident[:], ident_in, ld_const)
            load(meanmat[0:64, :], meanmat_in, ld_const)
            load(shift[:], shift_in, ld_const)
            load(convw[:], conv_in.rearrange("p (c k) -> p c k", c=DC), ld_const)
            load(par[:], par_in.rearrange("p (c k) -> p c k", c=3), ld_const)
            load(aneg[:], alog_in.rearrange("p (c k) -> p c k", c=DC), ld_const)
            for k in range(KH):
                load(w_x[:, k, :], w_in[k * P:(k + 1) * P, 0:DIN], ld_wx[k])
            load(wx[:], wx_in.rearrange("p (c k) -> p c k", c=DC), ld_ssmw)
            load(wdt[0:R, :], wdt_in, ld_ssmw)
            load(zr[0:2 * KH, :], zgu_in, ld_z)
            load(zs[0:2 * KH, :], sgu_in, ld_z)
            load(zdr[0:IC, :], zd_in, ld_z)
            load(zds[0:IC, :], sd_in, ld_z)
            load(shifts[:], shifts_in, ld_z)
            load(x[:, NT:2 * NT, :], x_in[L:2 * L, :].rearrange("(t p) n -> p t n", p=P), ld_x[1])
            load(w_g[:], w_in[:, DIN:2 * DIN].rearrange("(k p) n -> p k n", p=P), ld_wg)
            sp_.wait_ge(z_done, 2)
            sp_.dma_start(zgu_dram, zo[0:2 * KH, :]).then_inc(z_stored, 16)
            sp_.dma_start(zd_dram, zdo[0:IC, :]).then_inc(z_stored, 16)
            sp_.wait_ge(z_stored, 32)
            for b in range(NB):
                if b:
                    wait_taken(sp_, ("x", 1, DC - 1))
                    load(wout[:], wout_in.rearrange("p (c k) -> p c k", c=DC), ld_wout)
                sp_.wait_ge(ssmn_ready, b + 1)
                sp_.dma_start(bc_dram[b], ssmn[R:R + 2 * NS, :]).then_inc(bc_stored, 16)
                sp_.wait_ge(bc_stored, 16 * (b + 1))
                if b:
                    sp_.wait_ge(cmul_done, NSTEP)
                for n in range(4):
                    for h in range(2):
                        a = h * NS + n * 4
                        load(bc[:, a:a + 4, :], bc_dram[b:b + 1, a:a + 4, :].broadcast_to([P, 4, L]), ld_bc[b][n])

            def stage(i):
                s = i % 3
                cols = slice(i * P, (i + 1) * P)
                load(q_gu[s][:], qgu_in[i].rearrange("r n -> r () n").broadcast_to([16, 8, 2 * KH * P]), ld_stage[s])
                load(q_d[s][:], qd_in[i].rearrange("r n -> r () n").broadcast_to([16, 8, H]), ld_stage[s])
                load(s_gu[s][:].rearrange("p (a b) -> p a b", a=2 * KH),
                     sgu_in[:, cols].rearrange("(o g) n -> o g n", o=1).broadcast_to([P, 2 * KH, P]), ld_stage[s])
                load(z_gu[s][:].rearrange("p (a b) -> p a b", a=2 * KH),
                     zgu_dram[:, cols].rearrange("(o g) n -> o g n", o=1).broadcast_to([P, 2 * KH, P]),
                     ld_stage[s])
                load(s_d[s][:], sd_in[i:i + 1, :].broadcast_to([P, H]), ld_stage[s])
                load(z_d[s][:], zd_dram[i:i + 1, :].broadcast_to([P, H]), ld_stage[s])

            wait_taken(sp_, ("gate", 1, DC - 1))
            stage(1)
            sp_.wait_ge(ysum_done, NB * NSTEP)
            stage(0)
            sp_.wait_ge(yg_done, NB * DC)
            stage(2)
            wait_taken(sp_, ("out", 1, NT - 1))
            load(wqraw[:].rearrange("p a b c -> p (a b c)"), wq_in, ld_att)
            load(bqraw[:].rearrange("p b c -> p (b c)"), bq_in.broadcast_to([P, DH * NH]), ld_att)
            load(wqkv[:, :, DH:QKV], wkv_in.rearrange("p (c k) -> p c k", c=KH), ld_att)
            load(bqkv[:, DH:QKV], bkv_in.broadcast_to([P, 2 * DH]), ld_att)
            load(moe_w["gate"][0][:], gate_in.rearrange("p (c k) -> p c k", c=KH), ld_att)
            load(gam[:], gamma_in.broadcast_to([P, H]), ld_att)
            load(bet[:], beta_in.broadcast_to([P, H]), ld_att)
            for i in range(3, IC):
                sp_.wait_ge(whi_done, 2 * (i - 2))
                sp_.wait_ge(wlo_gu, i - 2)
                sp_.wait_ge(wlo_d, i - 2)
                stage(i)
            sp_.wait_ge(wq_done, 2)
            load(moe_w["fc1"][0][:], fc1_in.rearrange("(k p) n -> p k n", p=P), ld_moe[0])
            load(moe_w["exp"][0][:], exp_in.rearrange("(k p) n -> p k n", p=P), ld_moe[0])
            load(moe_w["fc2"][0][:], fc2_in.rearrange("(k p) n -> p k n", p=P), ld_moe[0])
            sp_.wait_ge(whi_done, 2 * IC)
            sp_.wait_ge(wlo_gu, IC)
            sp_.wait_ge(wlo_d, IC)
            load(moe_w["up"][0][:], up_in.rearrange("(k p) n -> p k n", p=P), ld_moe[1])
            sp_.wait_ge(ffn_used, IC + 8)
            load(moe_w["down"][0][:], down_in.rearrange("(k p) n -> p k n", p=P), ld_moe[2])
            for n in range(NB * NT):
                sp_.wait_ge(x_done, n + 1)
                sp_.dma_start(out[n * P:(n + 1) * P, :], x[:, n, :]).then_inc(x_stored, 16)
            sp_.wait_ge(x_stored, 16 * NB * NT)

        @block.tensor
        def _(pe):
            def start(item):
                if WORK[item] >= RING:
                    pe.wait_ge(taken_sem(item), WORK[item] // RING)

            def turn(layer, b, t, src):
                item = ("tr", layer, b, t)
                start(item)
                pe.wait_ge(xn_ready, XN[item[1:]] + 1)
                n = XN[item[1:]] % 2
                for k in range(KH):
                    last = pe.transpose(bank(item)[:, k * P:(k + 1) * P], src[:, n, k * P:(k + 1) * P], ident[:])
                last.then_inc(work_ready, 1)

            def product(item, parts, rows=P, cols=slice(0, L)):
                for n, (lhsT, rhs) in enumerate(parts):
                    last = pe.matmul(bank(item)[0:rows, cols], lhsT, rhs, start=(n == 0), stop=(n == len(parts) - 1))
                return last

            def halves(w_hi, w_lo, v_hi, v_lo):
                return [(w_hi, v_hi), (w_lo, v_hi), (w_hi, v_lo)]

            def x_part(b, c):
                item = ("x", b, c)
                start(item)
                product(item, [(w_x[:, k, c * P:(c + 1) * P], xT[:, k, :]) for k in range(KH)])\
                    .then_inc(work_ready, 1)

            def ssm_part(b, c):
                pe.wait_ge(u_ready, b * DC + c + 1)
                last = pe.matmul(psum[0:64, SSM_BANK, :], wx[:, c, :], u[:, c, :], start=(c == 0), stop=(c == DC - 1))
                if c == DC - 1:
                    last.then_inc(ssm_ready, 1)

            def gate_part(b, c):
                item = ("gate", b, c)
                start(item)
                product(item, [(w_g[:, k, c * P:(c + 1) * P], xT[:, k, :]) for k in range(KH)])\
                    .then_inc(work_ready, 1)

            def out_part(b, t):
                item = ("out", b, t)
                start(item)
                product(item, [(g[:, c, t * P:(t + 1) * P], wout[:, c, :]) for c in range(DC)])\
                    .then_inc(work_ready, 1)

            def qkv_part(b):
                pe.wait_ge(ld_att, 16 * 7)
                pe.wait_ge(wq_done, 2)
                for t in range(NT):
                    wait_taken(pe, ("tr", "att", b, t))
                start(("qkv", b))
                for t in range(NT):
                    last = product(("qkv", b), [(xTa[b][:, k, t * P:(t + 1) * P], wqkv[:, k, :]) for k in range(KH)],
                                   cols=slice(t * QKV, (t + 1) * QKV))
                last.then_inc(work_ready, 1)

            pe.wait_ge(ld_const, 16 * 6)
            for t in range(NT):
                turn("ssm", 0, t, xn)
            for t in range(NT):
                wait_taken(pe, ("tr", "ssm", 0, t))
            for k in range(KH):
                pe.wait_ge(ld_wx[k], 16)
            for c in range(DC):
                x_part(0, c)
                if c == 2:
                    pe.wait_ge(ld_ssmw, 32)
                if c >= 2:
                    ssm_part(0, c - 2)
            for b in range(NB):
                if b == 0:
                    ssm_part(b, DC - 2)
                ssm_part(b, DC - 1)
                if b == 0:
                    pe.wait_ge(ld_wg, 16)
                    gate_part(0, 0)
                start(("ms", b))
                pe.wait_ge(sq_ready, b + 1)
                pe.matmul(bank(("ms", b))[0:64, :], meanmat[0:64, :], sq[0:64, :], start=True, stop=True)\
                    .then_inc(work_ready, 1)
                if b == 0:
                    gate_part(0, 1)
                    gate_part(0, 2)
                else:
                    pe.wait_ge(ld_wout, 16)
                    pe.wait_ge(yg_done, DC)
                    out_part(0, 0)
                pe.wait_ge(ssmn_ready, b + 1)
                for c in range(DC):
                    item = ("dt", b, c)
                    start(item)
                    pe.matmul(bank(item), wdt[0:R, c * P:(c + 1) * P], ssmn[0:R, :], start=True, stop=True)\
                        .then_inc(work_ready, 1)
                if b == 0:
                    for c in range(3, DC):
                        gate_part(0, c)
                else:
                    for t in range(1, NT - 1):
                        out_part(0, t)
                for c in range(DC):
                    for n in range(NS):
                        k = (b * DC + c) * NS + n
                        for item in side_work(b, c, n):
                            if item[0] == "gate":
                                gate_part(*item[1:])
                            if item[0] == "tr":
                                turn(*item[1:], xn)
                            if item[0] == "x":
                                for t in range(NT):
                                    wait_taken(pe, ("tr", "ssm", 1, t))
                                x_part(*item[1:])
                            if item[0] == "ssm":
                                ssm_part(*item[1:])
                            if item[0] == "out":
                                out_part(*item[1:])
                        if n == 0 and (b or c):
                            pe.wait_ge(y_taken, b * DC + c)
                        pe.wait_ge(cmul_done, k + 1)
                        pe.matmul(psum[:, Y_BANK, :], ident[:], hc[:, k % HCS, :], start=(n == 0),
                                  stop=(n == NS - 1)).then_inc(ysum_done, 1)

            for t in range(NT):
                turn("ffn", 0, t, xnc)
            pe.wait_ge(yg_done, NB * DC)
            for t in range(NT):
                out_part(1, t)

            for b in range(NB):
                for t in range(NT):
                    wait_taken(pe, ("tr", "ffn", b, t))

                def down(i):
                    k = b * IC + i
                    if b == 0:
                        pe.wait_ge(wlo_d, i + 1)
                    pe.wait_ge(itlo_done, k + 1)
                    if i == 0:
                        if b == 0:
                            pe.wait_ge(y_taken, NB * DC)
                        else:
                            pe.wait_ge(y16_done, NT)
                    for t in range(NT):
                        cols = slice(t * P, (t + 1) * P)
                        for n, (v, w) in enumerate(halves(it_hi[:, k % 2, cols], it_lo[:, k % 2, cols],
                                                          d_hi[:, i, :], d_lo[:, i, :])):
                            last = pe.matmul(psum[:, t, :], v, w, start=(i == 0 and n == 0),
                                             stop=(i == IC - 1 and n == 2))
                    last.then_inc(ffn_used, 1)

                for i in range(IC):
                    k = b * IC + i
                    if b == 0:
                        pe.wait_ge(whi_done, 2 * (i + 1))
                        pe.wait_ge(wlo_gu, i + 1)
                    for j, name in enumerate("gu"):
                        item = (name, b, i)
                        start(item)
                        parts = []
                        for kk in range(KH):
                            w = slice((2 * kk + j) * P, (2 * kk + j + 1) * P)
                            parts += halves(gu_hi[:, i, w], gu_lo[:, i, w], xf_hi[b][:, kk, :],
                                            xf_lo[b][:, kk, :])
                        product(item, parts).then_inc(work_ready, 1)
                    if i >= 1:
                        down(i - 1)
                    if b == 0 and i == IC - 1:
                        for t in range(NT):
                            turn("ffn", 1, t, xnc)
                    if b == 1 and i == 4:
                        for t in range(NT):
                            turn("att", 0, t, xnc)
                    if b == 1 and i == 5:
                        qkv_part(0)
                    if b == 1 and i == 9:
                        for t in range(NT):
                            turn("moe", 0, t, xnc)
                down(IC - 1)

            def w_halves(name, k, cols, v_hi, v_lo):
                _, w_hi, w_lo = moe_w[name]
                return halves(w_hi[:, k, cols], w_lo[:, k, cols], v_hi, v_lo)

            def mw_ready(n, count):
                pe.wait_ge(mw_hi[n], count)
                pe.wait_ge(mw_lo[n], count)

            for b in range(NB):
                for t in range(NT):
                    wait_taken(pe, ("tr", "moe", b, t))
                start(("logits", b))
                mw_ready(0, 1)
                for t in range(NT):
                    tok = slice(t * P, (t + 1) * P)
                    parts = []
                    for k in range(KH):
                        parts += halves(xm_hi[b][:, k, tok], xm_lo[b][:, k, tok], moe_w["gate"][1][:, k, :],
                                        moe_w["gate"][2][:, k, :])
                    last = product(("logits", b), parts, cols=slice(t * NE, (t + 1) * NE))
                last.then_inc(work_ready, 1)
                mw_ready(1, 3)
                for m in range(LAT):
                    item = ("fc1", b, m)
                    start(item)
                    parts = []
                    for k in range(KH):
                        parts += w_halves("fc1", k, slice(m * P, (m + 1) * P), xm_hi[b][:, k, :], xm_lo[b][:, k, :])
                    product(item, parts).then_inc(work_ready, 1)
                for k in range(LAT):
                    wait_taken(pe, ("fc1", b, k))
                for m in range(LAT):
                    item = ("exp", b, m)
                    start(item)
                    parts = []
                    for k in range(LAT):
                        parts += w_halves("exp", k, slice(m * P, (m + 1) * P), lat_hi[:, k, :], lat_lo[:, k, :])
                    product(item, parts).then_inc(work_ready, 1)
                for k in range(LAT):
                    wait_taken(pe, ("exp", b, k))
                for t in range(NT):
                    item = ("routed", b, t)
                    tok = slice(t * P, (t + 1) * P)
                    start(item)
                    parts = []
                    for k in range(LAT):
                        parts += halves(eo_hi[:, k, tok], eo_lo[:, k, tok], moe_w["fc2"][1][:, k, :],
                                        moe_w["fc2"][2][:, k, :])
                    product(item, parts).then_inc(work_ready, 1)

                def moe_down(i):
                    k = b * MI + i
                    pe.wait_ge(h2lo_done, k + 1)
                    if i == 0:
                        mw_ready(3, 1)
                        pe.wait_ge(y16_done, NB * NT)
                        if b:
                            pe.wait_ge(ym_done, NT * b)
                    for t in range(NT):
                        tok = slice(t * P, (t + 1) * P)
                        for n, (v, w) in enumerate(halves(h2_hi[:, k % 2, tok], h2_lo[:, k % 2, tok],
                                                          moe_w["down"][1][:, i, :], moe_w["down"][2][:, i, :])):
                            last = pe.matmul(psum[:, t, :], v, w, start=(i == 0 and n == 0),
                                             stop=(i == MI - 1 and n == 2))
                        if i == MI - 1:
                            last.then_inc(down_done, 1)
                    if i < MI - 1:
                        last.then_inc(moe_used, 1)

                mw_ready(2, 1)
                for i in range(MI):
                    item = ("up", b, i)
                    start(item)
                    parts = []
                    for k in range(KH):
                        parts += w_halves("up", k, slice(i * P, (i + 1) * P), xm_hi[b][:, k, :], xm_lo[b][:, k, :])
                    product(item, parts).then_inc(work_ready, 1)
                    if i >= 1:
                        moe_down(i - 1)
                    if b == 0 and i == 2:
                        for t in range(NT):
                            turn("att", 1, t, xnc)
                    if b == 0 and i == 3:
                        qkv_part(1)
                    if b == 0 and i == MI - 1:
                        for t in range(NT):
                            turn("moe", 1, t, xnc)
                moe_down(MI - 1)

        @block.vector
        def _(dve):
            n_chain = [0]

            def link(ins):
                n_chain[0] += 1
                ins.then_inc(dve_chain, 1)
                dve.wait_ge(dve_chain, n_chain[0])

            def stats(group, tiles):
                n = LN[group]
                for j, tile in enumerate(tiles):
                    last = dve.bn_stats(bst[:, j, :], tile)
                link(last)
                for j in range(len(tiles)):
                    last = dve.bn_aggr(mv[:, n, j, :], bst[:, j, :])
                last.then_inc(stats_ready, 1)
                dve.wait_ge(stats_ready, n + 1)

            def inv_std(group, tiles):
                n = LN[group]
                dve.wait_ge(std_ready, n + 1)
                link(dve.reciprocal(rstd[:, n, 0:tiles], std[:, n, 0:tiles]))

            def mean_of(group, j):
                return mv[:, LN[group], j, 0:1]

            def rstd_of(group, j):
                return rstd[:, LN[group], j:j + 1]

            def x_tiles(b):
                return [x[:, b * NT + t, :] for t in range(NT)]

            def norm_tile(layer, b, t, dst):
                n = XN[(layer, b, t)]
                if n >= 2:
                    back = [k for k, v in XN.items() if v == n - 2][0]
                    wait_work(dve, ("tr",) + back)
                dve.tensor_scalar(dst[:, n % 2, :], x[:, b * NT + t, :], mean_of((layer, b), t),
                                  rstd_of((layer, b), t), ALU.subtract, ALU.mult).then_inc(xn_ready, 1)

            def conv(b, c):
                item = ("x", b, c)
                wait_work(dve, item)
                if b * DC + c >= 2:
                    dve.wait_ge(u_ready, b * DC + c - 1)
                a, src = cacc[:, c % 2, :], bank(item)
                link(dve.tensor_scalar(a, src, convw[:, c, KCONV - 1:KCONV], par[:, 0, c:c + 1],
                                       ALU.mult, ALU.add))
                for j in range(1, KCONV):
                    last = dve.scalar_tensor_tensor(a[:, j:], src[:, 0:L - j],
                                                    convw[:, c, KCONV - 1 - j:KCONV - j], a[:, j:],
                                                    ALU.mult, ALU.add)
                    if j < KCONV - 1:
                        link(last)
                last.then_inc(taken_sem(item), 1)

            def times_c(k):
                b, n = k // NSTEP, k % NS
                dve.wait_ge(scan_done, k + 1)
                if n % 4 == 0 and k % NSTEP < NS:
                    dve.wait_ge(ld_bc[b][n // 4], 32)
                if k >= HCS:
                    dve.wait_ge(ysum_done, k - HCS + 1)
                dve.tensor_tensor(hc[:, k % HCS, :], psum[:, k % SLOTS, :], bc[:, NS + n, :], ALU.mult)\
                    .then_inc(cmul_done, 1)

            def plus_d(b, c):
                k = b * DC + c
                dve.wait_ge(ysum_done, NS * (k + 1))
                dve.scalar_tensor_tensor(u[:, c, :], u[:, c, :], par[:, 2, c:c + 1], psum[:, Y_BANK, :],
                                         ALU.mult, ALU.add).then_inc(y_taken, 1)

            def keep_gate(c):
                item = ("gate", 0, c)
                wait_work(dve, item)
                dve.tensor_copy(g[:, c, :], bank(item)).then_inc(taken_sem(item), 1)

            def times_gate(b, c):
                k = b * DC + c
                dve.wait_ge(y_taken, k + 1)
                if b == 0:
                    dve.wait_ge(gate_done, c + 1)
                else:
                    wait_taken(dve, ("gate", b, c))
                dve.tensor_tensor(g[:, c, :], g[:, c, :], u[:, c, :], ALU.mult).then_inc(yg_done, 1)

            def take_out(b, t):
                item = ("out", b, t)
                wait_work(dve, item)
                dve.tensor_copy(obuf[b][:, t, :], bank(item)).then_inc(taken_sem(item), 1)

            def out_add(b):
                group = ("out", b)
                for t in range(NT):
                    link(dve.tensor_scalar(obuf[b][:, t, :], obuf[b][:, t, :], mean_of(group, t),
                                           rstd_of(group, t), ALU.subtract, ALU.mult))
                    dve.tensor_tensor(x[:, b * NT + t, :], x[:, b * NT + t, :], obuf[b][:, t, :], ALU.add)\
                        .then_inc(out_done, 1)
                dve.wait_ge(out_done, NT * (b + 1))

            dve.memset(epst[:], EPS).then_inc(eps_ready, 1)
            dve.wait_ge(ld_x[0], 16)
            dve.wait_ge(ld_const, 16 * 6)
            stats(("ssm", 0), x_tiles(0))
            inv_std(("ssm", 0), NT)
            for t in range(NT):
                norm_tile("ssm", 0, t, xn)
            dve.wait_ge(ld_z, 16 * 5)
            for words, rows, width, scales, raw, done in ((zr, 2 * KH, IPAD, zs, zi, zo), (zdr, IC, H, zds, zdi, zdo)):
                n = width // 8
                link(dve.tensor_tensor(raw[0:rows, :].rearrange("p (a b) -> p a b", b=8),
                                       words[0:rows, :].unsqueeze(2).broadcast_to([rows, n, 8]),
                                       shifts[0:rows, :].unsqueeze(1).broadcast_to([rows, n, 8]),
                                       ALU.logical_shift_right))
                link(dve.tensor_scalar(raw[0:rows, :], raw[0:rows, :], 15, None, ALU.bitwise_and))
                dve.scalar_tensor_tensor(done[0:rows, :], raw[0:rows, :], 1.0, scales[0:rows, :], ALU.add,
                                         ALU.mult).then_inc(z_done, 1)
            for c in range(DC):
                conv(0, c)

            for b in range(NB):
                if b == 0:
                    keep_gate(0)
                item = ("ms", b)
                wait_work(dve, item)
                dve.tensor_scalar(rr[0:64, :], bank(item)[0:64, :], EPS_RMS, None, ALU.add)\
                    .then_inc(taken_sem(item), 1)
                wait_taken(dve, item)
                dve.reciprocal(rr[0:64, :], rr[0:64, :]).then_inc(ms_ready, 1)
                if b == 0:
                    keep_gate(1)
                dve.wait_ge(rms_ready, b + 1)
                dve.tensor_tensor(ssmn[0:64, :], ssm[0:64, :], rr[0:64, :], ALU.mult).then_inc(ssmn_ready, 1)
                if b == 0:
                    keep_gate(2)
                else:
                    take_out(0, 0)
                for c in range(DC):
                    item = ("dt", b, c)
                    wait_work(dve, item)
                    dve.tensor_scalar(dtv[:, c, :], bank(item), par[:, 1, c:c + 1], None, ALU.add)\
                        .then_inc(taken_sem(item), 1)
                if b == 0:
                    keep_gate(3)
                    keep_gate(4)
                for h, part in enumerate(SP_PARTS):
                    dve.wait_ge(sp_ready, 3 * b + h + 1)
                    dve.scalar_tensor_tensor(dtv[:, part, :], dtv[:, part, :], 0.0, sp[:, part, :],
                                             ALU.max, ALU.add).then_inc(dt_ready, 1)
                if b == 0:
                    for c in range(5, DC):
                        keep_gate(c)
                else:
                    take_out(0, 1)
                    take_out(0, 2)

                for c in range(DC):
                    for n in range(NS):
                        k = (b * DC + c) * NS + n
                        dve.wait_ge(exp_done, k + 1)
                        dve.wait_ge(bmul_done, k // 2 + 1)
                        dve.tensor_tensor_scan(psum[:, k % SLOTS, :], psum[:, k % SLOTS, :],
                                               dbu[:, k // 2 % 2, k % 2, :], 0.0, ALU.mult, ALU.add)\
                            .then_inc(scan_done, 1)
                        if c or n:
                            times_c(k - 1)
                        if c and n == 1:
                            plus_d(b, c - 1)
                        if b == 0:
                            if c and n == 2:
                                times_gate(0, c - 1)
                            if (c, n) in CONV_AT:
                                conv(1, CONV_AT.index((c, n)))
                            if c == 0 and n == 1:
                                dve.wait_ge(ld_x[1], 16)
                                stats(("ssm", 1), x_tiles(1))
                            if c == 0 and n == 6:
                                inv_std(("ssm", 1), NT)
                            if c == 0 and n in (6, 7, 10, 11):
                                norm_tile("ssm", 1, (6, 7, 10, 11).index(n), xn)
                        else:
                            if c == 0 and n == 14:
                                take_out(0, NT - 1)
                            if c == 1 and n == 5:
                                for t in range(NT):
                                    wait_taken(dve, ("out", 0, t))
                                stats(("out", 0), [obuf[0][:, t, :] for t in range(NT)])
                            if c == 1 and n == 12:
                                inv_std(("out", 0), NT)
                                out_add(0)
                            if c == 3 and n == 5:
                                stats(("ffn", 0), x_tiles(0))
                            if c == 4 and n == 10:
                                inv_std(("ffn", 0), NT)
                            if c >= 3 and c % 2 and n == 12:
                                times_gate(1, c - 3)
                                times_gate(1, c - 2)
                times_c((b + 1) * NSTEP - 1)
                plus_d(b, DC - 1)
                if b == 0:
                    times_gate(0, DC - 1)
                else:
                    times_gate(1, DC - 2)
                    times_gate(1, DC - 1)

            def unpack(i):
                s = i % 3
                dve.wait_ge(ld_stage[s], 96 * (i // 3 + 1))
                dve.tensor_scalar(q_gu[s][:], q_gu[s][:], shift[:, 0:1], 15, ALU.logical_shift_right,
                                  ALU.bitwise_and)
                link(dve.tensor_scalar(q_d[s][:], q_d[s][:], shift[:, 0:1], 15, ALU.logical_shift_right,
                                       ALU.bitwise_and))
                dve.tensor_tensor(w_gu[s][:], q_gu[s][:], s_gu[s][:], ALU.mult).then_inc(q_done, 1)
                dve.tensor_tensor(w_d[s][:], q_d[s][:], s_d[s][:], ALU.mult).then_inc(q_done, 1)

            def low_weights(i):
                dve.wait_ge(whi_done, 2 * i + 1)
                dve.tensor_tensor(gu_lo[:, i, :], w_gu[i % 3][:], gu_hi[:, i, :], ALU.subtract).then_inc(wlo_gu, 1)

            def low_turned(b):
                for t in range(NT):
                    item = ("tr", "ffn", b, t)
                    cols = slice(t * P, (t + 1) * P)
                    dve.wait_ge(xhi_done, NT * b + t + 1)
                    dve.tensor_tensor(xf_lo[b][:, :, cols], bank(item).rearrange("p (k t) -> p k t", k=KH),
                                      xf_hi[b][:, :, cols], ALU.subtract).then_inc(taken_sem(item), 1)

            def low_moe(b):
                for t in range(NT):
                    item = ("tr", "moe", b, t)
                    cols = slice(t * P, (t + 1) * P)
                    dve.wait_ge(xmhi_done, NT * b + t + 1)
                    dve.tensor_tensor(xm_lo[b][:, :, cols], bank(item).rearrange("p (k t) -> p k t", k=KH),
                                      xm_hi[b][:, :, cols].bitcast(F32), ALU.subtract).then_inc(taken_sem(item), 1)

            def ffn_inner(b, i):
                k = b * IC + i
                wait_taken(dve, ("g", b, i))
                wait_work(dve, ("u", b, i))
                if k >= 2:
                    dve.wait_ge(ithi_done, k - 1)
                dve.tensor_tensor(it[:, k % 2, :], sg[:, k % 2, :], bank(("u", b, i)), ALU.mult)\
                    .then_inc(taken_sem(("u", b, i)), 1)
                wait_taken(dve, ("u", b, i))
                dve.wait_ge(ithi_done, k + 1)
                if k >= 2:
                    dve.wait_ge(ffn_used, k - 1)
                dve.tensor_tensor(it_lo[:, k % 2, :], it[:, k % 2, :], it_hi[:, k % 2, :],
                                  ALU.subtract).then_inc(itlo_done, 1)

            def ffn_stats16(b):
                dve.wait_ge(y16_done, NT * (b + 1))
                n = LN[("ffn16", b)]
                for t in range(NT):
                    last = dve.bn_stats(bst[:, t, :], y16[:, t, :])
                link(last)
                for t in range(NT):
                    last = dve.bn_aggr(mv[:, n, t, :], bst[:, t, :])
                link(last)
                link(dve.tensor_copy(m16[:, b, :, :], mv[:, n, :, :]))
                dve.tensor_scalar(ve16[:, b, :, 0], m16[:, b, :, 1], EPS16, None, ALU.add).then_inc(stats_ready, 1)

            def ffn_inv16(b):
                n = LN[("ffn16", b)]
                dve.wait_ge(std_ready, n + 1)
                link(dve.reciprocal(rstd[:, n, :], ve16[:, b, :, 1]))

            def ffn_add16(b, t):
                n = LN[("ffn16", b)]
                link(dve.tensor_scalar(d16[:], y16[:, t, :], m16[:, b, t, 0:1], None, ALU.subtract))
                link(dve.tensor_scalar(n16[:], d16[:], rstd[:, n, t:t + 1], None, ALU.mult))
                link(dve.tensor_tensor(x[:, b * NT + t, :], x[:, b * NT + t, :], n16[:], ALU.add))

            full = [P, NT, DH, DH]

            def att_scores(b):
                item = ("qkv", b)
                wait_work(dve, item)
                dve.tensor_tensor(qkv[:], bank(item)[:, 0:NT * QKV].rearrange("p (a b) -> p a b", a=NT),
                                  bqkv[:].unsqueeze(1).broadcast_to([P, NT, QKV]), ALU.add)\
                    .then_inc(taken_sem(item), 1)
                wait_taken(dve, item)
                q_b = qkv[:, :, 0:DH].unsqueeze(3).broadcast_to(full)
                k_b = qkv[:, :, DH:2 * DH].unsqueeze(2).broadcast_to(full)
                link(dve.tensor_tensor(sc[:], q_b, k_b, ALU.mult))
                link(dve.tensor_reduce(smax[:], sc[:], AX.X, ALU.max))
                dve.tensor_tensor(sc[:], sc[:], smax[:].unsqueeze(3).broadcast_to(full), ALU.subtract)\
                    .then_inc(s_ready, 1)

            def att_values(b):
                v_b = qkv[:, :, 2 * DH:].unsqueeze(2).broadcast_to(full)
                dve.wait_ge(p_ready, b + 1)
                dve.tensor_reduce(den[:], pr[:], AX.X, ALU.add)
                link(dve.tensor_tensor(sc[:], pr[:], v_b, ALU.mult))
                dve.tensor_reduce(num[:], sc[:], AX.X, ALU.add)
                link(dve.reciprocal(den[:], den[:]))
                link(dve.tensor_tensor(num[:], num[:], den[:], ALU.mult))
                stats(("atto", b), [num[:, t, :] for t in range(NT)])

            def att_add(b):
                group = ("atto", b)
                inv_std(group, NT)
                for t in range(NT):
                    last = dve.tensor_scalar(on[:, t, :], num[:, t, :], mean_of(group, t), rstd_of(group, t),
                                             ALU.subtract, ALU.mult)
                link(last)
                for t in range(NT):
                    x3 = x[:, b * NT + t, :].rearrange("p (d h) -> p d h", d=DH)
                    last = dve.tensor_tensor(x3, x3, on[:, t, :].unsqueeze(2).broadcast_to([P, DH, NH]), ALU.add)
                link(last)

            def between(b, i):
                if i == 0:
                    ffn_stats16(b)
                if i == 1:
                    ffn_inv16(b)
                    ffn_add16(b, 0)
                    ffn_add16(b, 1)
                if i == 2:
                    ffn_add16(b, 2)
                    ffn_add16(b, 3)
                    stats(("att", b), x_tiles(b))
                if i == 3:
                    inv_std(("att", b), NT)
                    norm_tile("att", b, 0, xnc)
                    norm_tile("att", b, 1, xnc)
                if i == 4:
                    norm_tile("att", b, 2, xnc)
                    norm_tile("att", b, 3, xnc)
                if i == 5:
                    att_scores(b)
                if i == 6:
                    att_values(b)
                if i == 7:
                    att_add(b)
                    stats(("moe", b), x_tiles(b))

            for t in range(NT):
                if t == 0:
                    pass
                norm_tile("ffn", 0, t, xnc)
            low_turned(0)
            unpack(0)
            unpack(1)
            low_weights(0)
            unpack(2)
            low_weights(1)
            for t in range(NT):
                wait_taken(dve, ("out", 1, t))
            stats(("out", 1), [obuf[1][:, t, :] for t in range(NT)])
            inv_std(("out", 1), NT)
            out_add(1)
            stats(("ffn", 1), x_tiles(1))
            for i in range(IC):
                ffn_inner(0, i)
                if i + 3 < IC:
                    unpack(i + 3)
                if i + 2 < IC:
                    low_weights(i + 2)
                if i == 3:
                    inv_std(("ffn", 1), NT)
                if i == 4:
                    dve.wait_ge(ld_att, 16 * 7)
                    dve.tensor_reduce(wqkv[:, :, 0:DH], wqraw[:], AX.X, ALU.add).then_inc(wq_done, 1)
                    dve.tensor_reduce(bqkv[:, 0:DH], bqraw[:], AX.X, ALU.add).then_inc(wq_done, 1)
                if i == IC - 3:
                    norm_tile("ffn", 1, 0, xnc)
                    norm_tile("ffn", 1, 1, xnc)
            norm_tile("ffn", 1, 2, xnc)
            norm_tile("ffn", 1, 3, xnc)
            low_turned(1)
            for i in range(IC):
                ffn_inner(1, i)
                between(0, i)
                if i == 8:
                    inv_std(("moe", 0), NT)
                    norm_tile("moe", 0, 0, xnc)
                    norm_tile("moe", 0, 1, xnc)
                if i == 9:
                    norm_tile("moe", 0, 2, xnc)
                    norm_tile("moe", 0, 3, xnc)
                    low_moe(0)

            def route(b):
                item = ("logits", b)
                wait_work(dve, item)
                for t in range(NT):
                    last = dve.max(top8[:, b, t, :], bank(item)[:, t * NE:(t + 1) * NE])
                last.then_inc(taken_sem(item), 1)
                wait_taken(dve, item)
                dve.tensor_tensor(rw[:, b, :], top8[:, b, :, 0], top8[:, b, :, 1], ALU.add).then_inc(rw_ready, 1)

            def low_latent(b, name, hi, lo):
                for m in range(LAT):
                    item = (name, b, m)
                    dve.wait_ge(lhi_done, 2 * LAT * b + LAT * (name == "exp") + m + 1)
                    dve.tensor_tensor(lo[:, m, :], bank(item), hi[:, m, :].bitcast(F32), ALU.subtract)\
                        .then_inc(taken_sem(item), 1)

            def h2_low(b, i):
                k = b * MI + i
                dve.wait_ge(h2hi_done, k + 1)
                dve.tensor_tensor(h2_lo[:, k % 2, :], h2[:, k % 2, :], h2_hi[:, k % 2, :].bitcast(F32),
                                  ALU.subtract).then_inc(h2lo_done, 1)

            def moe_sum(b):
                for t in range(NT):
                    y = rt[b][:, t, :]
                    dve.wait_ge(down_done, NT * b + t + 1)
                    wait_taken(dve, ("routed", b, t))
                    dve.tensor_tensor(y, psum[:, t, :], y, ALU.add).then_inc(ym_done, 1)
                    dve.wait_ge(ym_done, NT * b + t + 1)
                    stats(("moei", b, t), [y])

            def moe_affine(b):
                for t in range(NT):
                    y = rt[b][:, t, :]
                    group = ("moei", b, t)
                    inv_std(group, 1)
                    link(dve.scalar_tensor_tensor(y, y, mean_of(group, 0), gam[:], ALU.subtract, ALU.mult))
                    link(dve.scalar_tensor_tensor(y, y, rstd_of(group, 0), bet[:], ALU.mult, ALU.add))
                    stats(("moeo", b, t), [y])

            def moe_norm(b):
                for t in range(NT):
                    y = rt[b][:, t, :]
                    group = ("moeo", b, t)
                    inv_std(group, 1)
                    dve.tensor_scalar(y, y, mean_of(group, 0), rstd_of(group, 0), ALU.subtract, ALU.mult)\
                        .then_inc(yn_done, 1)

            route(0)
            between(1, 0)
            low_latent(0, "fc1", lat_hi, lat_lo)
            low_latent(0, "exp", eo_hi, eo_lo)
            between(1, 1)
            between(1, 2)
            for i in range(MI):
                h2_low(0, i)
                if i in (0, 1):
                    between(1, i + 3)
                if i in (3, 4, 5):
                    between(1, i + 2)
                if i == 6:
                    inv_std(("moe", 1), NT)
                    norm_tile("moe", 1, 0, xnc)
                    norm_tile("moe", 1, 1, xnc)
                if i == 7:
                    norm_tile("moe", 1, 2, xnc)
                    norm_tile("moe", 1, 3, xnc)
            low_moe(1)
            route(1)
            moe_sum(0)
            low_latent(1, "fc1", lat_hi, lat_lo)
            low_latent(1, "exp", eo_hi, eo_lo)
            moe_affine(0)
            for i in range(MI):
                h2_low(1, i)
                if i == 1:
                    moe_norm(0)
            moe_sum(1)
            moe_affine(1)
            moe_norm(1)

        @block.scalar
        def _(act):
            def root(group, tiles):
                n = LN[group]
                act.wait_ge(stats_ready, n + 1)
                act.activation(std[:, n, 0:tiles], mv[:, n, 0:tiles, 1], ACT.Sqrt, bias=epst[:, 0:1])\
                    .then_inc(std_ready, 1)

            def root16(b):
                act.wait_ge(stats_ready, LN[("ffn16", b)] + 1)
                act.activation(ve16[:, b, :, 1], ve16[:, b, :, 0], ACT.Sqrt).then_inc(std_ready, 1)

            def take_turned(layer, b, t, dst):
                item = ("tr", layer, b, t)
                wait_work(act, item)
                act.copy(dst[:, :, t * P:(t + 1) * P], bank(item).rearrange("p (k t) -> p k t", k=KH))\
                    .then_inc(taken_sem(item), 1)

            def silu_gate(b, c):
                item = ("gate", b, c)
                if b == 0:
                    wait_taken(act, item)
                    act.activation(g[:, c, :], g[:, c, :], ACT.Silu).then_inc(gate_done, 1)
                else:
                    wait_work(act, item)
                    for t in range(NT):
                        wait_taken(act, ("out", 0, t))
                    act.activation(g[:, c, :], bank(item), ACT.Silu).then_inc(taken_sem(item), 1)

            def conv_silu(b, c):
                wait_taken(act, ("x", b, c))
                if b:
                    act.wait_ge(yg_done, c + 1)
                act.activation(u[:, c, :], cacc[:, c % 2, :], ACT.Silu).then_inc(u_ready, 1)

            def take_out(b, t):
                item = ("out", b, t)
                wait_work(act, item)
                act.copy(obuf[b][:, t, :], bank(item)).then_inc(taken_sem(item), 1)

            act.wait_ge(eps_ready, 1)
            root(("ssm", 0), NT)
            for t in range(NT):
                take_turned("ssm", 0, t, xT)
            for c in range(DC):
                conv_silu(0, c)
            for b in range(NB):
                act.wait_ge(ssm_ready, b + 1)
                act.copy(ssm[0:64, :], psum[0:64, SSM_BANK, :])
                act.activation(sq[0:64, :], psum[0:64, SSM_BANK, :], ACT.Square).then_inc(sq_ready, 1)
                act.wait_ge(ms_ready, b + 1)
                act.activation(rr[0:64, :], rr[0:64, :], ACT.Sqrt).then_inc(rms_ready, 1)
                if b == 0:
                    act.wait_ge(ld_const, 16 * 6)
                    act.activation(aneg[:], aneg[:], ACT.Exp).then_inc(act_chain, 1)
                    act.wait_ge(act_chain, 1)
                    act.mul(aneg[:], aneg[:], -1.0).then_inc(a_ready, 1)
                n0 = 1 + b * (DC + 1)
                act.wait_ge(ssmn_ready, b + 1)
                for c in range(DC):
                    wait_taken(act, ("dt", b, c))
                    act.activation(sp[:, c, :], dtv[:, c, :], ACT.Abs).then_inc(act_chain, 1)
                act.wait_ge(act_chain, n0 + DC)
                act.activation(sp[:], sp[:], ACT.Exp, scale=-1.0).then_inc(act_chain, 1)
                act.wait_ge(act_chain, n0 + DC + 1)
                for part in SP_PARTS:
                    act.activation(sp[:, part, :], sp[:, part, :], ACT.Ln, bias=1.0).then_inc(sp_ready, 1)
                act.wait_ge(a_ready, 1)
                for c in range(DC):
                    act.wait_ge(dt_ready, 3 * b + (c > 1) + (c > 3) + 1)
                    for n in range(NS):
                        k = (b * DC + c) * NS + n
                        if k >= SLOTS:
                            act.wait_ge(cmul_done, k - SLOTS + 1)
                        act.activation(psum[:, k % SLOTS, :], dtv[:, c, :], ACT.Exp,
                                       scale=aneg[:, c, n:n + 1]).then_inc(exp_done, 1)
                        if b == 0:
                            if c == 0 and n == 4:
                                root(("ssm", 1), NT)
                            if n == 8:
                                if c:
                                    conv_silu(1, c - 1)
                                silu_gate(0, c)
                            if c == 0 and n in (10, 11):
                                take_turned("ssm", 1, n - 10, xT)
                            if c == 0 and n in (14, 15):
                                take_turned("ssm", 1, n - 12, xT)
                        else:
                            if c == 1 and n == 8:
                                root(("out", 0), NT)
                            if c == 3 and n == 8:
                                root(("ffn", 0), NT)
                            if c % 2 and n == 12:
                                silu_gate(1, c - 1)
                                silu_gate(1, c)
                if b == 0:
                    conv_silu(1, DC - 1)

            def high_weights(i):
                act.wait_ge(w_done, 2 * (i + 1))
                act.copy(gu_hi[:, i, :], w_gu[i % 3][:]).then_inc(whi_done, 1)
                act.copy(d_hi[:, i, :], w_d[i % 3][:]).then_inc(whi_done, 1)

            def high_turned(b):
                for t in range(NT):
                    item = ("tr", "ffn", b, t)
                    wait_work(act, item)
                    act.copy(xf_hi[b][:, :, t * P:(t + 1) * P], bank(item).rearrange("p (k t) -> p k t", k=KH))\
                        .then_inc(xhi_done, 1)

            def high_moe(b):
                for t in range(NT):
                    item = ("tr", "moe", b, t)
                    wait_work(act, item)
                    act.copy(xm_hi[b][:, :, t * P:(t + 1) * P], bank(item).rearrange("p (k t) -> p k t", k=KH))\
                        .then_inc(xmhi_done, 1)

            def high_moe_weights(load_no, n, names):
                act.wait_ge(ld_moe[load_no], 16 * len(names))
                for name in names:
                    w, w_hi, _ = moe_w[name]
                    act.copy(w_hi[:], w[:]).then_inc(mw_hi[n], 1)

            def ffn_silu(k):
                b, i = divmod(k, IC)
                item = ("g", b, i)
                wait_work(act, item)
                if k >= 2:
                    wait_taken(act, ("u", (k - 2) // IC, (k - 2) % IC))
                act.activation(sg[:, k % 2, :], bank(item), ACT.Silu).then_inc(taken_sem(item), 1)

            def ffn_high(k):
                b, i = divmod(k, IC)
                wait_taken(act, ("u", b, i))
                if k >= 2:
                    act.wait_ge(ffn_used, k - 1)
                act.copy(it_hi[:, k % 2, :], it[:, k % 2, :]).then_inc(ithi_done, 1)

            def take16(b):
                act.wait_ge(ffn_used, IC * (b + 1))
                for t in range(NT):
                    act.copy(y16[:, t, :], psum[:, t, :]).then_inc(y16_done, 1)

            def att_exp(b):
                act.wait_ge(s_ready, b + 1)
                act.activation(pr[:], sc[:], ACT.Exp, scale=float(DH) ** -0.5).then_inc(p_ready, 1)

            high_turned(0)
            high_weights(0)
            for t in range(NT):
                take_out(1, t)
            high_weights(1)
            root(("out", 1), NT)
            root(("ffn", 1), NT)
            act.wait_ge(ld_att, 16 * 7)
            act.copy(moe_w["gate"][1][:], moe_w["gate"][0][:]).then_inc(mw_hi[0], 1)
            for k in range(NB * IC):
                b, i = divmod(k, IC)
                ffn_silu(k)
                ffn_high(k)
                if k == IC - 1:
                    high_turned(1)
                    take16(0)
                if b == 1 and i == 4:
                    for t in range(NT):
                        take_turned("att", 0, t, xTa[0])
                if k + 2 < IC:
                    high_weights(k + 2)
                if b == 1:
                    if i == 0:
                        root16(0)
                    if i == 2:
                        root(("att", 0), NT)
                    if i == 5:
                        att_exp(0)
                    if i == 6:
                        root(("atto", 0), NT)
                    if i == 7:
                        root(("moe", 0), NT)
                        high_moe_weights(0, 1, ["fc1", "exp", "fc2"])
                    if i == 8:
                        high_moe_weights(1, 2, ["up"])
                    if i == 9:
                        high_moe(0)
            high_moe_weights(2, 3, ["down"])
            take16(1)

            def relu(b, i):
                k = b * MI + i
                item = ("up", b, i)
                wait_work(act, item)
                if k >= 2:
                    act.wait_ge(h2_done, k - 1)
                act.activation(h1[:, k % 2, :], bank(item), ACT.Relu).then_inc(taken_sem(item), 1)

            def h2_high(b, i):
                k = b * MI + i
                act.wait_ge(h2_done, k + 1)
                if i >= 2:
                    act.wait_ge(moe_used, (MI - 1) * b + i - 1)
                elif b:
                    act.wait_ge(down_done, NT * b)
                act.copy(h2_hi[:, k % 2, :], h2[:, k % 2, :]).then_inc(h2hi_done, 1)

            def high_latent(b, name, hi):
                for m in range(LAT):
                    item = (name, b, m)
                    wait_work(act, item)
                    act.copy(hi[:, m, :], bank(item)).then_inc(lhi_done, 1)

            for b in range(NB):
                high_latent(b, "fc1", lat_hi)
                if b == 0:
                    root16(1)
                high_latent(b, "exp", eo_hi)
                if b:
                    for t in range(NT):
                        root(("moei", 0, t), 1)
                act.wait_ge(rw_ready, b + 1)
                for t in range(NT):
                    item = ("routed", b, t)
                    wait_work(act, item)
                    act.activation(rt[b][:, t, :], bank(item), ACT.Identity, scale=rw[:, b, t:t + 1])\
                        .then_inc(taken_sem(item), 1)
                for i in range(MI):
                    relu(b, i)
                    h2_high(b, i)
                    if b == 0:
                        if i == 0:
                            root(("att", 1), NT)
                        if i == 2:
                            for t in range(NT):
                                take_turned("att", 1, t, xTa[1])
                        if i == 3:
                            att_exp(1)
                        if i == 4:
                            root(("atto", 1), NT)
                        if i == 5:
                            root(("moe", 1), NT)
                        if i == 7:
                            high_moe(1)
                    elif i == 0:
                        for t in range(NT):
                            root(("moeo", 0, t), 1)
            for name in ("moei", "moeo"):
                for t in range(NT):
                    root((name, 1, t), 1)

        @block.gpsimd
        def _(pool):
            n_chain = 0
            for b in range(NB):
                for c in range(DC):
                    pool.wait_ge(dt_ready, 3 * b + (3 if c >= 4 else 2))
                    if c == 0:
                        pool.wait_ge(bc_stored, 16 * (b + 1))
                    pool.tensor_tensor(du[:, c % 2, :], dtv[:, c, :], u[:, c, :], ALU.mult).then_inc(pool_chain, 1)
                    n_chain += 1
                    pool.wait_ge(pool_chain, n_chain)
                    for p in range(NS // 2):
                        k = (b * DC + c) * NS // 2 + p
                        if k >= 2:
                            pool.wait_ge(scan_done, 2 * (k - 1))
                        if c == 0 and p % 2 == 0:
                            pool.wait_ge(ld_bc[b][p // 2], 32)
                        pool.tensor_tensor(dbu[:, k % 2, :, :],
                                           du[:, c % 2, :].unsqueeze(1).broadcast_to([P, 2, L]),
                                           bc[:, 2 * p:2 * p + 2, :], ALU.mult).then_inc(bmul_done, 1)

            for i in range(IC):
                s = i % 3
                pool.wait_ge(q_done, 2 * i + 2)
                pool.tensor_tensor(w_gu[s][:], w_gu[s][:], z_gu[s][:], ALU.subtract).then_inc(w_done, 1)
                pool.tensor_tensor(w_d[s][:], w_d[s][:], z_d[s][:], ALU.subtract).then_inc(w_done, 1)
                pool.wait_ge(whi_done, 2 * i + 2)
                pool.tensor_tensor(d_lo[:, i, :], w_d[s][:], d_hi[:, i, :], ALU.subtract).then_inc(wlo_d, 1)
            def low_moe_weights(n, names):
                pool.wait_ge(mw_hi[n], len(names))
                for name in names:
                    w, w_hi, w_lo = moe_w[name]
                    pool.tensor_tensor(w_lo[:], w[:], w_hi[:].bitcast(F32), ALU.subtract).then_inc(mw_lo[n], 1)

            def add_out(b):
                for t in range(NT):
                    k = b * NT + t
                    pool.wait_ge(yn_done, k + 1)
                    pool.tensor_tensor(x[:, k, :], x[:, k, :], rt[b][:, t, :], ALU.add).then_inc(x_done, 1)

            low_moe_weights(0, ["gate"])
            low_moe_weights(1, ["fc1", "exp", "fc2"])
            low_moe_weights(2, ["up"])
            low_moe_weights(3, ["down"])
            for b in range(NB):
                for i in range(MI):
                    k = b * MI + i
                    wait_taken(pool, ("up", b, i))
                    if k >= 2:
                        pool.wait_ge(h2lo_done, k - 1)
                    pool.tensor_tensor(h2[:, k % 2, :], h1[:, k % 2, :], h1[:, k % 2, :], ALU.mult)\
                        .then_inc(h2_done, 1)
                    if b == 1 and i == 2:
                        add_out(0)
            add_out(1)


def kernel(**inputs):
    import concourse.bacc as _bacc
    from concourse.bass_utils import run_bass_kernel_spmd as _run

    def arr(name):
        return np.ascontiguousarray(inputs[name])

    def cols(v):
        return np.reshape(v, (DC, P, -1)).transpose(1, 0, 2).reshape(P, -1)

    def chunks(w):
        k = w.shape[0] // P
        return np.reshape(w, (k, P, -1)).transpose(1, 0, 2).reshape(P, -1)

    def pad(a, rows, width):
        out = np.zeros((rows, width), a.dtype)
        out[:a.shape[0], :a.shape[1]] = a
        return out

    rms = np.zeros((64, 64), np.float32)
    for a, e in ((0, R), (R, R + NS), (R + NS, R + 2 * NS)):
        rms[a:e, a:e] = 1.0 / (e - a)

    def packed(name):
        return pad(arr(name), 64, IPAD).reshape(KH, 16, IC, P)

    def interleave(a, b_):
        return np.stack([a, b_], axis=1)

    qgu = np.stack([packed("L0_ffn_gate_qweight"), packed("L0_ffn_up_qweight")], axis=1)
    qgu = qgu.transpose(3, 2, 0, 1, 4).reshape(IC, 16, 2 * KH * P)
    sgu = interleave(pad(arr("L0_ffn_gate_scales"), KH, IPAD), pad(arr("L0_ffn_up_scales"), KH, IPAD))
    zgu = interleave(pad(arr("L0_ffn_gate_zeros"), KH, IPAD // 8), pad(arr("L0_ffn_up_zeros"), KH, IPAD // 8))

    arrays = {
        "x_in": arr("L0_attn_hidden_states").reshape(NB * L, H),
        "ident_in": np.eye(P, dtype=np.float32),
        "meanmat_in": rms,
        "shift_in": (np.arange(P, dtype=np.int32) % 8 * 4).reshape(P, 1),
        "shifts_in": np.tile(np.arange(8, dtype=np.int32) * 4, (P, 1)),
        "w_in": arr("L0_attn_W_in").T,
        "conv_in": cols(arr("L0_attn_conv_w")),
        "par_in": np.concatenate([cols(arr("L0_attn_conv_b")), cols(arr("L0_attn_b_dt")), cols(arr("L0_attn_D"))], 1),
        "alog_in": cols(arr("L0_attn_A_log")),
        "wx_in": chunks(arr("L0_attn_W_x").T),
        "wdt_in": arr("L0_attn_W_dt").T,
        "wout_in": chunks(arr("L0_attn_W_out").T),
        "qgu_in": qgu,
        "qd_in": pad(arr("L0_ffn_down_qweight"), IC * 16, H).reshape(IC, 16, H),
        "sgu_in": sgu.reshape(2 * KH, IPAD),
        "zgu_in": zgu.reshape(2 * KH, IPAD // 8),
        "sd_in": arr("L0_ffn_down_scales"),
        "zd_in": arr("L0_ffn_down_zeros"),
        "wq_in": chunks(arr("L1_attn_Wq").reshape(H, DH * NH)),
        "wkv_in": chunks(np.concatenate([arr("L1_attn_Wk").reshape(H, DH), arr("L1_attn_Wv").reshape(H, DH)], 1)),
        "bq_in": arr("L1_attn_bq").reshape(1, DH * NH),
        "bkv_in": np.concatenate([arr("L1_attn_bk").reshape(1, DH), arr("L1_attn_bv").reshape(1, DH)], 1),
        "gate_in": chunks(arr("L1_ffn_gate_w")),
        "up_in": arr("L1_ffn_up_w"),
        "down_in": arr("L1_ffn_down_w"),
        "fc1_in": arr("L1_ffn_fc1_w"),
        "fc2_in": arr("L1_ffn_fc2_w"),
        "exp_in": arr("L1_ffn_expert_w"),
        "gamma_in": arr("L1_ffn_ln_gamma").reshape(1, H),
        "beta_in": arr("L1_ffn_ln_beta").reshape(1, H),
    }
    nc = _bacc.Bacc("TRN2", target_bir_lowering=False, num_devices=1)
    args = {}
    for name in list(arrays):
        a = np.ascontiguousarray(arrays[name])
        arrays[name] = a
        args[name] = nc.dram_tensor(name, a.shape, mybir.dt.from_np(a.dtype), kind="ExternalInput").ap()
    args["out"] = nc.dram_tensor("out", [NB * L, H], F32, kind="ExternalOutput").ap()
    build(nc, **args)
    r = _run(nc, [arrays], core_ids=[0])
    return r.results[0]["out"].reshape(NB, L, H)
```

```python
import numpy as np

import concourse.bass as bass
from concourse import mybir
from contextlib import ExitStack

F32 = mybir.dt.float32
F16 = mybir.dt.float16
F32R = mybir.dt.float32r
I32 = mybir.dt.int32
ALU = mybir.AluOpType
ACT = mybir.ActivationFunctionType
AX = mybir.AxisListType

P = 128
NB = 2
L = 512
NT = L // P
H = 512
KH = H // P
DIN = 1024
DC = DIN // P
NS = 16
R = 32
KCONV = 4
INTER = 1376
IC = -(-INTER // P)
IPAD = IC * P
DH = 16
NH = 32
QKV = 3 * DH
MI = 1024 // P
LAT = 256 // P
NE = 8
SLOTS = 4
HCS = 4
EPS = 1e-5
EPS16 = float(np.float16(1e-5))
EPS_RMS = 1e-6


GATE_AFTER_DT = {3: 2}
X_AT = [((0, 14), (0, 15)), ((1, 1), (1, 3))] + [((c - 1, 5), (c - 1, 10)) for c in range(2, DC)]
CONV_AT = [(1, 4)] + [(c, 8) for c in range(1, DC)]
SP_PARTS = [slice(0, 2), slice(2, 4), slice(4, DC)]


def side_work(b, c, n):
    if b == 0:
        if c == 0 and n in (8, 9, 12, 13):
            return [("tr", "ssm", 1, (8, 9, 12, 13).index(n))]
        return [("x", 1, k, half) for k in range(DC) for half in range(2) if (c, n) == X_AT[k][half]] + \
            [("ssm", 1, k) for k in range(DC - 1) if (c, n) == (k + 1, 12)]
    if c == 0 and n == 3:
        return [("out", 0, NT - 1)]
    if n == (4 if c % 2 else 10):
        return [("gate", 1, c)]
    return []


def pe_order():
    items = [("tr", "ssm", 0, t) for t in range(NT)] + [("x", 0, c) for c in range(DC)]
    for b in range(NB):
        if b == 0:
            between = [("gate", 0, c) for c in range(DC)]
            items += between[:1] + [("ms", b)] + between[1:2]
        else:
            between = [("out", 0, t) for t in range(NT)]
            items += [("ms", b)] + between[:1]
        for c in range(DC):
            items += [("dt", b, c)]
            if b == 0 and c in GATE_AFTER_DT:
                items += [("gate", 0, GATE_AFTER_DT[c])]
        items += between[3:] if b == 0 else between[1:NT - 1]
        for c in range(DC):
            for n in range(NS):
                items += [item for item in side_work(b, c, n) if item[0] not in ("ssm", "x")]
                items += [item[:3] for item in side_work(b, c, n) if item[0] == "x" and item[3] == 0]
    items += [("tr", "ffn", 0, t) for t in range(NT)]
    items += [("out", 1, t) for t in range(NT)]
    for i in range(IC):
        items += [("g", 0, i), ("u", 0, i)]
        if i == IC - 1:
            items += [("tr", "ffn", 1, t) for t in range(NT)]
    for i in range(IC):
        items += [("g", 1, i), ("u", 1, i)]
        if i == 4:
            items += [("tr", "att", 0, t) for t in range(NT)]
        if i == 5:
            items += [("qkv", 0)]
        if i == 9:
            items += [("tr", "moe", 0, t) for t in range(NT)]
    for b in range(NB):
        items += [("lt", b), ("fc1", b, 0), ("logits", b), ("fc1", b, 1)]
        items += [("exp", b, m) for m in range(LAT)]
        items += [("routed", b, t) for t in range(NT)]
        for i in range(MI):
            items += [("up", b, i)]
            if b == 0 and i == 1:
                items += [("tr", "att", 1, t) for t in range(NT)]
            if b == 0 and i == 2:
                items += [("qkv", 1)]
            if b == 0 and i == MI - 1:
                items += [("tr", "moe", 1, t) for t in range(NT)]
    return {item: n for n, item in enumerate(items)}


def ln_order():
    groups = [("ssm", 0), ("ssm", 1), ("out", 0), ("ffn", 0), ("out", 1), ("ffn", 1)]
    for b in range(NB):
        groups += [("ffn16", b), ("att", b), ("atto", b), ("moe", b)]
    for b in range(NB):
        groups += [("moei", b, t) for t in range(NT)] + [("moeo", b, t) for t in range(NT)]
    return {g: n for n, g in enumerate(groups)}


def build(nc, x_in, ident_in, meanmat_in, shift_in, shifts_in, w_in, conv_in, par_in, alog_in, wx_in, wdt_in,
          wout_in, qgu_in, qd_in, sgu_in, zgu_in, sd_in, zd_in, wq_in, wkv_in, bq_in, bkv_in, gate_in, up_in,
          down_in, fc1_in, fc2_in, exp_in, gamma_in, beta_in, out):
    WORK = pe_order()
    FIRST3 = WORK[("tr", "ffn", 0, 0)]
    LN = ln_order()
    NG = len(LN)
    XN = {}
    for item in WORK:
        if item[0] == "tr":
            XN[item[1:]] = len(XN)
    NSTEP = DC * NS

    bc_dram = nc.dram_tensor("bc_scratch", [NB, 2 * NS, L], F32).ap()
    zgu_dram = nc.dram_tensor("zgu_scratch", [2 * KH, IPAD], F32).ap()
    zd_dram = nc.dram_tensor("zd_scratch", [IC, H], F32).ap()

    with ExitStack() as ctx:
        def sem(name):
            return ctx.enter_context(nc.semaphore(name))

        KB = 1024
        arena = ctx.enter_context(nc.sbuf_tensor("arena", [P, 207 * KB // 4], F32))
        base = nc.sbuf_base - 207 * KB

        def at(name, kb, shape, dt=F32):
            return nc.alloc_sbuf_tensor_at(name, [P, *shape], dt, offset=base + int(kb * KB))

        x = at("x", 0, [NB * NT, H])
        ident = at("ident", 16, [P])
        meanmat = at("meanmat", 16.5, [64])
        shift = at("shift", 16.75, [1], I32)
        epst = at("epst", 16.78125, [2])
        bst = at("bst", 16.8125, [NT, 6])
        mv = at("mv", 17, [NG, NT, 2])
        std = at("std", 18, [NG, NT])
        rstd = at("rstd", 18.5, [NG, NT])
        top8 = at("top8", 19, [NB, NT, 8])
        rw = at("rw", 19.25, [NB, NT])
        m16 = at("m16", 19.3125, [NB, NT, 2], F16)
        ve16 = at("ve16", 19.375, [NB, NT, 2], F16)
        diag = at("diag", 19.5, [P])
        wx = at("wx", 20, [DC, 64])
        wdt = at("wdt", 22, [DIN])
        par = at("par", 26, [3, DC])
        convw = at("convw", 26.125, [DC, KCONV])
        aneg = at("aneg", 26.25, [DC, NS])
        w_x = at("w_x", 27, [KH, DIN])
        w_g = at("w_g", 43, [KH, DIN])
        wout = at("wout", 27, [DC, H])
        bc = at("bc", 59, [2 * NS, L])
        u = at("u", 123, [DC, L])
        dtv = at("dtv", 139, [DC, L])
        g = at("g", 155, [DC, L])
        sp = at("sp", 171, [DC, L])
        ssm = at("ssm", 171, [L])
        sq = at("sq", 173, [L])
        rr = at("rr", 175, [L])
        dbu = at("dbu", 171, [2, 2, L])
        hc = at("hc", 179, [HCS, L])
        xT = at("xT", 187, [KH, L])
        xn = at("xn", 195, [2, H])
        cacc = at("cacc", 199, [2, L])
        du = at("du", 203, [2, L])
        ssmn = at("ssmn", 203, [L])
        obuf = [at("obuf0", 195, [NT, H]), at("obuf1", 141, [NT, H])]
        zr = at("zr", 59, [IPAD // 8], I32)
        zi = at("zi", 60, [IPAD], I32)
        zs = at("zs", 66, [IPAD], F16)
        zo = at("zo", 69, [IPAD])
        zdr = at("zdr", 75, [H // 8], I32)
        zdi = at("zdi", 76, [H], I32)
        zds = at("zds", 78, [H], F16)
        zdo = at("zdo", 79, [H])
        shifts = at("shifts", 81, [8], I32)
        gu_hi = at("gu_hi", 59, [IC, 2 * KH * P], F16)
        gu_lo = at("gu_lo", 81, [IC, 2 * KH * P], F16)
        d_hi = at("d_hi", 103, [IC, H], F16)
        d_lo = at("d_lo", 114, [IC, H], F16)
        STG = [171, 43, 125]
        q_gu = [at(f"q_gu{s}", k, [2 * KH * P], I32) for s, k in enumerate(STG)]
        w_gu = [at(f"w_gu{s}", k, [2 * KH * P]) for s, k in enumerate(STG)]
        s_gu = [at(f"s_gu{s}", k + 4, [2 * KH * P], F16) for s, k in enumerate(STG)]
        z_gu = [at(f"z_gu{s}", k + 6, [2 * KH * P]) for s, k in enumerate(STG)]
        q_d = [at(f"q_d{s}", k + 10, [H], I32) for s, k in enumerate(STG)]
        w_d = [at(f"w_d{s}", k + 10, [H]) for s, k in enumerate(STG)]
        s_d = [at(f"s_d{s}", k + 12, [H], F16) for s, k in enumerate(STG)]
        z_d = [at(f"z_d{s}", k + 13, [H]) for s, k in enumerate(STG)]
        xf_hi = [at(f"xf_hi{b}", k, [KH, L], F16) for b, k in enumerate([187, 195])]
        xf_lo = [at(f"xf_lo{b}", k, [KH, L], F16) for b, k in enumerate([191, 199])]
        xnc = at("xnc", 149, [2, H])
        it = at("it", 27, [2, L])
        it_hi = at("it_hi", 31, [2, L], F16)
        it_lo = at("it_lo", 33, [2, L], F16)
        sg = at("sg", 39, [2, L])
        y16 = at("y16", 155, [NT, H], F16)
        d16 = at("d16", 159, [H], F16)
        n16 = at("n16", 160, [H], F16)
        wqraw = at("wqraw", 161, [KH, DH, NH])
        bqraw = at("bqraw", 169, [DH, NH])
        wqkv = at("wqkv", 20, [KH, QKV])
        bqkv = at("bqkv", 20.75, [QKV])
        gam = at("gam", 22, [H])
        bet = at("bet", 25, [H])
        xTa = [at("xTa0", 171, [KH, L]), at("xTa1", 97, [KH, L])]
        sc = at("sc", 179, [NT, DH, DH])
        pr = at("pr", 183, [NT, DH, DH])
        qkv = at("qkv", 153, [NT, QKV])
        smax = at("smax", 153.75, [NT, DH])
        den = at("den", 154, [NT, DH])
        num = at("num", 154.25, [NT, DH])
        on = at("on", 154.5, [NT, DH])
        moe_w = {}
        for name, kb, kb_hi, shape in (("up", 43, 125, [KH, MI * P]), ("down", 59, 81, [MI, H]),
                                       ("fc1", 161, 141, [KH, LAT * P]), ("exp", 165, 145, [LAT, LAT * P]),
                                       ("fc2", 167, 203, [LAT, H]), ("gate", 21, 24.5, [KH, NE])):
            moe_w[name] = (at(f"w_{name}", kb, shape), at(f"w_{name}_hi", kb_hi, shape, F32R),
                           at(f"w_{name}_lo", kb, shape, F32R))
        xm_hi = [at("xm_hi0", 187, [KH, L], F32R), at("xm_hi1", 105, [KH, L], F32R)]
        xm_lo = [at("xm_lo0", 171, [KH, L], F32R), at("xm_lo1", 113, [KH, L], F32R)]
        lt = at("lt", 147, [L])
        h1 = at("h1", 27, [2, L])
        h2 = at("h2", 31, [2, L])
        h2_hi = at("h2_hi", 121, [2, L], F32R)
        h2_lo = at("h2_lo", 75, [2, L], F32R)
        lat_hi = at("lat_hi", 195, [LAT, L], F32R)
        lat_lo = at("lat_lo", 199, [LAT, L], F32R)
        eo_hi = at("eo_hi", 97, [LAT, L], F32R)
        eo_lo = at("eo_lo", 101, [LAT, L], F32R)
        rt = [at("rt0", 35, [NT, H]), at("rt1", 171, [NT, H])]
        psum = ctx.enter_context(nc.psum_tensor("psum", [P, 8, L], F32))
        Y_BANK, SSM_BANK = 3, 4
        SLOT = (0, 1, 2, 5)

        ld_x = [sem(f"ld_x{b}") for b in range(NB)]
        ld_const = sem("ld_const")
        ld_z = sem("ld_z")
        ld_wx = [sem(f"ld_wx{k}") for k in range(KH)]
        ld_wg = sem("ld_wg")
        ld_ssmw = sem("ld_ssmw")
        ld_wout = sem("ld_wout")
        ld_bc = [[sem(f"ld_bc{b}_{n}") for n in range(4)] for b in range(NB)]
        ld_stage = [sem(f"ld_stage{s}") for s in range(3)]
        ld_att = sem("ld_att")
        ld_moe = [sem(f"ld_moe{n}") for n in range(3)]
        bc_stored = sem("bc_stored")
        z_stored = sem("z_stored")
        x_stored = sem("x_stored")
        z_done = sem("z_done")
        a_ready = sem("a_ready")
        work_ready = sem("work_ready")
        taken2 = [sem(f"taken2_{j}") for j in range(2)]
        taken3 = [sem(f"taken3_{j}") for j in range(3)]
        ssm_ready = sem("ssm_ready")
        stats_ready = sem("stats_ready")
        std_ready = sem("std_ready")
        xn_ready = sem("xn_ready")
        conv_ready = sem("conv_ready")
        u_ready = sem("u_ready")
        sq_ready = sem("sq_ready")
        ssmn_ready = sem("ssmn_ready")
        sp_ready = sem("sp_ready")
        dt_ready = sem("dt_ready")
        eps_ready = sem("eps_ready")
        exp_done = sem("exp_done")
        bmul_done = sem("bmul_done")
        scan_done = sem("scan_done")
        cmul_done = sem("cmul_done")
        ysum_done = sem("ysum_done")
        diag_ready = sem("diag_ready")
        y_taken = sem("y_taken")
        yg_done = sem("yg_done")
        gate_done = sem("gate_done")
        out_done = sem("out_done")
        q_done = sem("q_done")
        w_done = sem("w_done")
        whi_done = sem("whi_done")
        wlo_gu = sem("wlo_gu")
        wlo_d = sem("wlo_d")
        xhi_done = sem("xhi_done")
        it_done = sem("it_done")
        ithi_done = sem("ithi_done")
        itlo_done = sem("itlo_done")
        ffn_used = sem("ffn_used")
        y16_done = sem("y16_done")
        wq_done = sem("wq_done")
        s_ready = sem("s_ready")
        p_ready = sem("p_ready")
        rw_ready = sem("rw_ready")
        mw_hi = [sem(f"mw_hi{n}") for n in range(4)]
        mw_lo = [sem(f"mw_lo{n}") for n in range(4)]
        xmhi_done = sem("xmhi_done")
        lhi_done = sem("lhi_done")
        h2_done = sem("h2_done")
        h2hi_done = sem("h2hi_done")
        h2lo_done = sem("h2lo_done")
        down_done = sem("down_done")
        yn_done = sem("yn_done")
        moe_used = sem("moe_used")
        ym_done = sem("ym_done")
        x_done = sem("x_done")
        x_last = sem("x_last")
        dve_chain = sem("dve_chain")
        du_done = sem("du_done")
        act_chain = sem("act_chain")

        block = ctx.enter_context(nc.Block())

        def ring(item):
            n = WORK[item]
            return divmod(n, 2)[::-1] if n < FIRST3 else divmod(n - FIRST3, 3)[::-1]

        def bank(item):
            j = ring(item)[0]
            return psum[:, (6 if WORK[item] < FIRST3 else 5) + j, :]

        def taken_sem(item):
            return (taken2 if WORK[item] < FIRST3 else taken3)[ring(item)[0]]

        def wait_work(eng, item):
            eng.wait_ge(work_ready, WORK[item] + 1)

        def wait_taken(eng, item):
            eng.wait_ge(taken_sem(item), ring(item)[1] + 1)

        @block.sync
        def _(sp_):
            def load(dst, src, s):
                sp_.dma_start(dst, src).then_inc(s, 16)

            load(x[:, 0:NT, :], x_in[0:L, :].rearrange("(t p) n -> p t n", p=P), ld_x[0])
            load(ident[:], ident_in, ld_const)
            load(meanmat[0:64, :], meanmat_in, ld_const)
            load(shift[:], shift_in, ld_const)
            load(convw[:], conv_in.rearrange("p (c k) -> p c k", c=DC), ld_const)
            load(par[:], par_in.rearrange("p (c k) -> p c k", c=3), ld_const)
            load(aneg[:], alog_in.rearrange("p (c k) -> p c k", c=DC), ld_const)
            for k in range(KH):
                load(w_x[:, k, :], w_in[k * P:(k + 1) * P, 0:DIN], ld_wx[k])
            load(wx[:], wx_in.rearrange("p (c k) -> p c k", c=DC), ld_ssmw)
            load(wdt[0:R, :], wdt_in, ld_ssmw)
            load(zr[0:2 * KH, :], zgu_in, ld_z)
            load(zs[0:2 * KH, :], sgu_in, ld_z)
            load(zdr[0:IC, :], zd_in, ld_z)
            load(zds[0:IC, :], sd_in, ld_z)
            load(shifts[:], shifts_in, ld_z)
            load(x[:, NT:2 * NT, :], x_in[L:2 * L, :].rearrange("(t p) n -> p t n", p=P), ld_x[1])
            load(w_g[:], w_in[:, DIN:2 * DIN].rearrange("(k p) n -> p k n", p=P), ld_wg)
            sp_.wait_ge(z_done, 2)
            sp_.dma_start(zgu_dram, zo[0:2 * KH, :]).then_inc(z_stored, 16)
            sp_.dma_start(zd_dram, zdo[0:IC, :]).then_inc(z_stored, 16)
            sp_.wait_ge(z_stored, 32)
            for b in range(NB):
                if b:
                    wait_taken(sp_, ("x", 1, DC - 1))
                    load(wout[:], wout_in.rearrange("p (c k) -> p c k", c=DC), ld_wout)
                sp_.wait_ge(ssmn_ready, b + 1)
                sp_.dma_start(bc_dram[b], ssmn[R:R + 2 * NS, :]).then_inc(bc_stored, 16)
                sp_.wait_ge(bc_stored, 16 * (b + 1))
                if b:
                    sp_.wait_ge(cmul_done, NSTEP)
                for n in range(4):
                    for h in range(2):
                        a = h * NS + n * 4
                        load(bc[:, a:a + 4, :], bc_dram[b:b + 1, a:a + 4, :].broadcast_to([P, 4, L]), ld_bc[b][n])

            def stage(i):
                s = i % 3
                cols = slice(i * P, (i + 1) * P)
                load(q_gu[s][:], qgu_in[i].rearrange("r n -> r () n").broadcast_to([16, 8, 2 * KH * P]), ld_stage[s])
                load(q_d[s][:], qd_in[i].rearrange("r n -> r () n").broadcast_to([16, 8, H]), ld_stage[s])
                load(s_gu[s][:].rearrange("p (a b) -> p a b", a=2 * KH),
                     sgu_in[:, cols].rearrange("(o g) n -> o g n", o=1).broadcast_to([P, 2 * KH, P]), ld_stage[s])
                load(z_gu[s][:].rearrange("p (a b) -> p a b", a=2 * KH),
                     zgu_dram[:, cols].rearrange("(o g) n -> o g n", o=1).broadcast_to([P, 2 * KH, P]),
                     ld_stage[s])
                load(s_d[s][:], sd_in[i:i + 1, :].broadcast_to([P, H]), ld_stage[s])
                load(z_d[s][:], zd_dram[i:i + 1, :].broadcast_to([P, H]), ld_stage[s])

            wait_taken(sp_, ("gate", 1, DC - 1))
            stage(1)
            sp_.wait_ge(ysum_done, NB * NSTEP)
            stage(0)
            sp_.wait_ge(yg_done, DC)
            stage(2)

            def stage_again(i):
                sp_.wait_ge(whi_done, 2 * (i - 2))
                sp_.wait_ge(wlo_gu, i - 2)
                sp_.wait_ge(wlo_d, i - 2)
                stage(i)

            stage_again(3)
            for i in range(4, 7):
                stage_again(i)
            wait_taken(sp_, ("out", 1, NT - 1))
            load(wqraw[:].rearrange("p a b c -> p (a b c)"), wq_in, ld_att)
            load(bqraw[:].rearrange("p b c -> p (b c)"), bq_in.broadcast_to([P, DH * NH]), ld_att)
            load(wqkv[:, :, DH:QKV], wkv_in.rearrange("p (c k) -> p c k", c=KH), ld_att)
            load(bqkv[:, DH:QKV], bkv_in.broadcast_to([P, 2 * DH]), ld_att)
            load(moe_w["gate"][0][:], gate_in.rearrange("p (c k) -> p c k", c=KH), ld_att)
            load(gam[:], gamma_in.broadcast_to([P, H]), ld_att)
            load(bet[:], beta_in.broadcast_to([P, H]), ld_att)
            for i in range(7, IC):
                stage_again(i)
            sp_.wait_ge(wq_done, 2)
            load(moe_w["fc1"][0][:], fc1_in.rearrange("(k p) n -> p k n", p=P), ld_moe[0])
            load(moe_w["exp"][0][:], exp_in.rearrange("(k p) n -> p k n", p=P), ld_moe[0])
            load(moe_w["fc2"][0][:], fc2_in.rearrange("(k p) n -> p k n", p=P), ld_moe[0])
            sp_.wait_ge(whi_done, 2 * IC)
            sp_.wait_ge(wlo_gu, IC)
            sp_.wait_ge(wlo_d, IC)
            load(moe_w["up"][0][:], up_in.rearrange("(k p) n -> p k n", p=P), ld_moe[1])
            sp_.wait_ge(ffn_used, IC + 8)
            load(moe_w["down"][0][:], down_in.rearrange("(k p) n -> p k n", p=P), ld_moe[2])
            for n in range(NB * NT):
                if n < NB * NT - 2:
                    sp_.wait_ge(x_done, n + 1)
                else:
                    sp_.wait_ge(x_last, n - NB * NT + 3)
                sp_.dma_start(out[n * P:(n + 1) * P, :], x[:, n, :]).then_inc(x_stored, 16)
            sp_.wait_ge(x_stored, 16 * NB * NT)

        @block.tensor
        def _(pe):
            def start(item):
                used = ring(item)[1]
                if used:
                    pe.wait_ge(taken_sem(item), used)
                elif WORK[item] == FIRST3:
                    pe.wait_ge(cmul_done, NB * NSTEP)
                    for name, n in WORK.items():
                        if FIRST3 - 2 <= n < FIRST3:
                            wait_taken(pe, name)

            def turn(layer, b, t, src):
                item = ("tr", layer, b, t)
                start(item)
                pe.wait_ge(xn_ready, XN[item[1:]] + 1)
                n = XN[item[1:]] % 2
                for k in range(KH):
                    last = pe.transpose(bank(item)[:, k * P:(k + 1) * P], src[:, n, k * P:(k + 1) * P], ident[:])
                last.then_inc(work_ready, 1)

            def product(item, parts, rows=P, cols=slice(0, L)):
                for n, (lhsT, rhs) in enumerate(parts):
                    last = pe.matmul(bank(item)[0:rows, cols], lhsT, rhs, start=(n == 0), stop=(n == len(parts) - 1))
                return last

            def halves(w_hi, w_lo, v_hi, v_lo):
                return [(w_hi, v_hi), (w_lo, v_hi), (w_hi, v_lo)]

            def x_part(b, c, half):
                item = ("x", b, c)
                if half == 0:
                    start(item)
                for k in range(2 * half, 2 * half + 2):
                    last = pe.matmul(bank(item), w_x[:, k, c * P:(c + 1) * P], xT[:, k, :], start=(k == 0),
                                     stop=(k == KH - 1))
                if half == 1:
                    last.then_inc(work_ready, 1)

            def ssm_part(b, c):
                pe.wait_ge(u_ready, b * DC + c + 1)
                last = pe.matmul(psum[0:64, SSM_BANK, :], wx[:, c, :], u[:, c, :], start=(c == 0), stop=(c == DC - 1))
                if c == DC - 1:
                    last.then_inc(ssm_ready, 1)

            def gate_part(b, c):
                item = ("gate", b, c)
                start(item)
                product(item, [(w_g[:, k, c * P:(c + 1) * P], xT[:, k, :]) for k in range(KH)])\
                    .then_inc(work_ready, 1)

            def out_part(b, t):
                item = ("out", b, t)
                start(item)
                product(item, [(g[:, c, t * P:(t + 1) * P], wout[:, c, :]) for c in range(DC)])\
                    .then_inc(work_ready, 1)

            def qkv_part(b):
                pe.wait_ge(ld_att, 16 * 7)
                pe.wait_ge(wq_done, 2)
                for t in range(NT):
                    wait_taken(pe, ("tr", "att", b, t))
                start(("qkv", b))
                for t in range(NT):
                    last = product(("qkv", b), [(xTa[b][:, k, t * P:(t + 1) * P], wqkv[:, k, :]) for k in range(KH)],
                                   cols=slice(t * QKV, (t + 1) * QKV))
                last.then_inc(work_ready, 1)

            pe.wait_ge(ld_const, 16 * 6)
            for t in range(NT):
                turn("ssm", 0, t, xn)
            for t in range(NT):
                wait_taken(pe, ("tr", "ssm", 0, t))
            for k in range(KH):
                pe.wait_ge(ld_wx[k], 16)
            for c in range(DC):
                x_part(0, c, 0)
                x_part(0, c, 1)
                if c == 2:
                    pe.wait_ge(ld_ssmw, 32)
                if c >= 2:
                    ssm_part(0, c - 2)
            for b in range(NB):
                if b == 0:
                    pe.wait_ge(ld_wg, 16)
                    gate_part(0, 0)
                    ssm_part(b, DC - 2)
                ssm_part(b, DC - 1)
                start(("ms", b))
                pe.wait_ge(sq_ready, b + 1)
                pe.matmul(bank(("ms", b))[0:64, :], meanmat[0:64, :], sq[0:64, :], start=True, stop=True)\
                    .then_inc(work_ready, 1)
                if b == 0:
                    gate_part(0, 1)
                else:
                    pe.wait_ge(ld_wout, 16)
                    pe.wait_ge(y_taken, DC)
                    out_part(0, 0)
                pe.wait_ge(ssmn_ready, b + 1)
                for c in range(DC):
                    item = ("dt", b, c)
                    start(item)
                    pe.matmul(bank(item), wdt[0:R, c * P:(c + 1) * P], ssmn[0:R, :], start=True, stop=True)\
                        .then_inc(work_ready, 1)
                    if b == 0 and c in GATE_AFTER_DT:
                        gate_part(0, GATE_AFTER_DT[c])
                if b == 0:
                    for c in range(3, DC):
                        gate_part(0, c)
                else:
                    for t in range(1, NT - 1):
                        out_part(0, t)
                for c in range(DC):
                    for n in range(NS):
                        k = (b * DC + c) * NS + n
                        for item in side_work(b, c, n):
                            if item[0] == "gate":
                                gate_part(*item[1:])
                            if item[0] == "tr":
                                turn(*item[1:], xn)
                            if item[0] == "x":
                                for t in range(NT):
                                    wait_taken(pe, ("tr", "ssm", 1, t))
                                x_part(*item[1:])
                            if item[0] == "ssm":
                                ssm_part(*item[1:])
                            if item[0] == "out":
                                out_part(*item[1:])
                        if n == 0 and (b or c):
                            pe.wait_ge(y_taken, b * DC + c)
                        if b == 0 and n == 12:
                            pe.wait_ge(diag_ready, c + 1)
                            pe.matmul(psum[:, Y_BANK, :], diag[:], u[:, c, :], start=False, stop=False)
                        pe.wait_ge(cmul_done, k + 1)
                        pe.matmul(psum[:, Y_BANK, :], ident[:], hc[:, k % HCS, :], start=(n == 0),
                                  stop=(n == NS - 1)).then_inc(ysum_done, 1)

            for t in range(NT):
                turn("ffn", 0, t, xnc)
            pe.wait_ge(yg_done, DC)
            for t in range(NT):
                out_part(1, t)

            for b in range(NB):
                for t in range(NT):
                    wait_taken(pe, ("tr", "ffn", b, t))

                def down(i):
                    k = b * IC + i
                    if b == 0:
                        pe.wait_ge(wlo_d, i + 1)
                    pe.wait_ge(itlo_done, k + 1)
                    if i == 0:
                        if b == 0:
                            pe.wait_ge(y_taken, NB * DC)
                        else:
                            pe.wait_ge(y16_done, NT)
                    for t in range(NT):
                        cols = slice(t * P, (t + 1) * P)
                        for n, (v, w) in enumerate(halves(it_hi[:, k % 2, cols], it_lo[:, k % 2, cols],
                                                          d_hi[:, i, :], d_lo[:, i, :])):
                            last = pe.matmul(psum[:, t, :], v, w, start=(i == 0 and n == 0),
                                             stop=(i == IC - 1 and n == 2))
                    last.then_inc(ffn_used, 1)

                for i in range(IC):
                    k = b * IC + i
                    if b == 0:
                        pe.wait_ge(whi_done, 2 * (i + 1))
                        pe.wait_ge(wlo_gu, i + 1)
                    for j, name in enumerate("gu"):
                        item = (name, b, i)
                        start(item)
                        parts = []
                        for kk in range(KH):
                            w = slice((2 * kk + j) * P, (2 * kk + j + 1) * P)
                            parts += halves(gu_hi[:, i, w], gu_lo[:, i, w], xf_hi[b][:, kk, :],
                                            xf_lo[b][:, kk, :])
                        product(item, parts).then_inc(work_ready, 1)
                    if i >= 1:
                        down(i - 1)
                    if b == 0 and i == IC - 1:
                        for t in range(NT):
                            turn("ffn", 1, t, xnc)
                    if b == 1 and i == 4:
                        for t in range(NT):
                            turn("att", 0, t, xnc)
                    if b == 1 and i == 5:
                        qkv_part(0)
                    if b == 1 and i == 9:
                        for t in range(NT):
                            turn("moe", 0, t, xnc)
                down(IC - 1)

            def w_halves(name, k, cols, v_hi, v_lo):
                _, w_hi, w_lo = moe_w[name]
                return halves(w_hi[:, k, cols], w_lo[:, k, cols], v_hi, v_lo)

            def mw_ready(n, count):
                pe.wait_ge(mw_hi[n], count)
                pe.wait_ge(mw_lo[n], count)

            for b in range(NB):
                for t in range(NT):
                    wait_taken(pe, ("tr", "moe", b, t))
                start(("lt", b))
                mw_ready(0, 1)
                parts = []
                for k in range(KH):
                    parts += w_halves("gate", k, slice(0, NE), xm_hi[b][:, k, :], xm_lo[b][:, k, :])
                product(("lt", b), parts, rows=NE).then_inc(work_ready, 1)
                mw_ready(1, 3)
                for m in range(LAT):
                    item = ("fc1", b, m)
                    start(item)
                    parts = []
                    for k in range(KH):
                        parts += w_halves("fc1", k, slice(m * P, (m + 1) * P), xm_hi[b][:, k, :], xm_lo[b][:, k, :])
                    product(item, parts).then_inc(work_ready, 1)
                    if m == 0:
                        start(("logits", b))
                        wait_taken(pe, ("lt", b))
                        for t in range(NT):
                            last = pe.transpose(bank(("logits", b))[:, t * NE:(t + 1) * NE],
                                                lt[0:NE, t * P:(t + 1) * P], ident[0:NE, 0:NE])
                        last.then_inc(work_ready, 1)
                for k in range(LAT):
                    wait_taken(pe, ("fc1", b, k))
                for m in range(LAT):
                    item = ("exp", b, m)
                    start(item)
                    parts = []
                    for k in range(LAT):
                        parts += w_halves("exp", k, slice(m * P, (m + 1) * P), lat_hi[:, k, :], lat_lo[:, k, :])
                    product(item, parts).then_inc(work_ready, 1)
                for k in range(LAT):
                    wait_taken(pe, ("exp", b, k))
                for t in range(NT):
                    item = ("routed", b, t)
                    tok = slice(t * P, (t + 1) * P)
                    start(item)
                    parts = []
                    for k in range(LAT):
                        parts += halves(eo_hi[:, k, tok], eo_lo[:, k, tok], moe_w["fc2"][1][:, k, :],
                                        moe_w["fc2"][2][:, k, :])
                    product(item, parts).then_inc(work_ready, 1)

                def moe_down(i):
                    k = b * MI + i
                    pe.wait_ge(h2lo_done, k + 1)
                    if b == 0:
                        mw_ready(3, i + 1)
                    if i == 0:
                        pe.wait_ge(y16_done, NB * NT)
                        if b:
                            pe.wait_ge(ym_done, NT * b)
                    for t in range(NT):
                        tok = slice(t * P, (t + 1) * P)
                        for n, (v, w) in enumerate(halves(h2_hi[:, k % 2, tok], h2_lo[:, k % 2, tok],
                                                          moe_w["down"][1][:, i, :], moe_w["down"][2][:, i, :])):
                            last = pe.matmul(psum[:, t, :], v, w, start=(i == 0 and n == 0),
                                             stop=(i == MI - 1 and n == 2))
                        if i == MI - 1:
                            last.then_inc(down_done, 1)
                    if i < MI - 1:
                        last.then_inc(moe_used, 1)

                mw_ready(2, KH)
                for i in range(MI):
                    item = ("up", b, i)
                    start(item)
                    parts = []
                    for k in range(KH):
                        parts += w_halves("up", k, slice(i * P, (i + 1) * P), xm_hi[b][:, k, :], xm_lo[b][:, k, :])
                    product(item, parts).then_inc(work_ready, 1)
                    if i >= 1:
                        moe_down(i - 1)
                    if b == 0 and i == 1:
                        for t in range(NT):
                            turn("att", 1, t, xnc)
                    if b == 0 and i == 2:
                        qkv_part(1)
                    if b == 0 and i == MI - 1:
                        for t in range(NT):
                            turn("moe", 1, t, xnc)
                moe_down(MI - 1)

        @block.vector
        def _(dve):
            n_chain = [0]

            def link(ins):
                n_chain[0] += 1
                ins.then_inc(dve_chain, 1)
                dve.wait_ge(dve_chain, n_chain[0])

            def stats(group, tiles):
                n = LN[group]
                for j, tile in enumerate(tiles):
                    last = dve.bn_stats(bst[:, j, :], tile)
                link(last)
                for j in range(len(tiles)):
                    last = dve.bn_aggr(mv[:, n, j, :], bst[:, j, :])
                last.then_inc(stats_ready, 1)
                dve.wait_ge(stats_ready, n + 1)

            def inv_std(group, tiles):
                n = LN[group]
                dve.wait_ge(std_ready, n + 1)
                link(dve.reciprocal(rstd[:, n, 0:tiles], std[:, n, 0:tiles]))

            def mean_of(group, j):
                return mv[:, LN[group], j, 0:1]

            def rstd_of(group, j):
                return rstd[:, LN[group], j:j + 1]

            def x_tiles(b):
                return [x[:, b * NT + t, :] for t in range(NT)]

            def norm_tile(layer, b, t, dst):
                n = XN[(layer, b, t)]
                if n >= 2:
                    back = [k for k, v in XN.items() if v == n - 2][0]
                    wait_work(dve, ("tr",) + back)
                dve.tensor_scalar(dst[:, n % 2, :], x[:, b * NT + t, :], mean_of((layer, b), t),
                                  rstd_of((layer, b), t), ALU.subtract, ALU.mult).then_inc(xn_ready, 1)

            def conv(b, c):
                item = ("x", b, c)
                dve.wait_ge(conv_ready, b * DC + c + 1)
                a, src = cacc[:, c % 2, :], bank(item)
                for j in range(1, KCONV):
                    last = dve.scalar_tensor_tensor(a[:, j:], src[:, 0:L - j],
                                                    convw[:, c, KCONV - 1 - j:KCONV - j], a[:, j:],
                                                    ALU.mult, ALU.add)
                    if j < KCONV - 1:
                        link(last)
                last.then_inc(taken_sem(item), 1)

            def times_c(k):
                b, n = k // NSTEP, k % NS
                dve.wait_ge(scan_done, k + 1)
                if n % 4 == 0 and k % NSTEP < NS:
                    dve.wait_ge(ld_bc[b][n // 4], 32)
                if k >= HCS:
                    dve.wait_ge(ysum_done, k - HCS + 1)
                dve.tensor_tensor(hc[:, k % HCS, :], psum[:, SLOT[k % SLOTS], :], bc[:, NS + n, :], ALU.mult)\
                    .then_inc(cmul_done, 1)

            def keep_gate(c):
                item = ("gate", 0, c)
                wait_work(dve, item)
                dve.tensor_copy(g[:, c, :], bank(item)).then_inc(taken_sem(item), 1)

            def first_y(c):
                dve.wait_ge(ysum_done, NS * (c + 1))
                dve.wait_ge(gate_done, c + 1)
                dve.tensor_tensor(g[:, c, :], g[:, c, :], psum[:, Y_BANK, :], ALU.mult).then_inc(y_taken, 1)

            def plus_d(c):
                dve.wait_ge(ysum_done, NS * (DC + c + 1))
                dve.scalar_tensor_tensor(u[:, c, :], u[:, c, :], par[:, 2, c:c + 1], psum[:, Y_BANK, :],
                                         ALU.mult, ALU.add).then_inc(y_taken, 1)

            def times_gate(c):
                dve.wait_ge(y_taken, DC + c + 1)
                wait_taken(dve, ("gate", 1, c))
                dve.tensor_tensor(g[:, c, :], g[:, c, :], u[:, c, :], ALU.mult).then_inc(yg_done, 1)

            def take_out(b, t):
                item = ("out", b, t)
                wait_work(dve, item)
                dve.tensor_copy(obuf[b][:, t, :], bank(item)).then_inc(taken_sem(item), 1)

            def out_add(b):
                group = ("out", b)
                for t in range(NT):
                    link(dve.tensor_scalar(obuf[b][:, t, :], obuf[b][:, t, :], mean_of(group, t),
                                           rstd_of(group, t), ALU.subtract, ALU.mult))
                    dve.tensor_tensor(x[:, b * NT + t, :], x[:, b * NT + t, :], obuf[b][:, t, :], ALU.add)\
                        .then_inc(out_done, 1)
                dve.wait_ge(out_done, NT * (b + 1))

            dve.memset(epst[:, 0:1], EPS).then_inc(eps_ready, 1)
            dve.memset(epst[:, 1:2], EPS_RMS).then_inc(eps_ready, 1)
            dve.wait_ge(ld_x[0], 16)
            dve.wait_ge(ld_const, 16 * 6)
            stats(("ssm", 0), x_tiles(0))
            inv_std(("ssm", 0), NT)
            for t in range(NT):
                norm_tile("ssm", 0, t, xn)
            dve.wait_ge(ld_z, 16 * 5)
            for words, rows, width, scales, raw, done in ((zr, 2 * KH, IPAD, zs, zi, zo), (zdr, IC, H, zds, zdi, zdo)):
                n = width // 8
                link(dve.tensor_tensor(raw[0:rows, :].rearrange("p (a b) -> p a b", b=8),
                                       words[0:rows, :].unsqueeze(2).broadcast_to([rows, n, 8]),
                                       shifts[0:rows, :].unsqueeze(1).broadcast_to([rows, n, 8]),
                                       ALU.logical_shift_right))
                link(dve.tensor_scalar(raw[0:rows, :], raw[0:rows, :], 15, None, ALU.bitwise_and))
                dve.scalar_tensor_tensor(done[0:rows, :], raw[0:rows, :], 1.0, scales[0:rows, :], ALU.add,
                                         ALU.mult).then_inc(z_done, 1)
            for c in range(DC):
                conv(0, c)

            for b in range(NB):
                if b == 0:
                    keep_gate(0)
                wait_taken(dve, ("ms", b))
                link(dve.reciprocal(rr[0:64, :], rr[0:64, :]))
                dve.tensor_tensor(ssmn[0:64, :], ssm[0:64, :], rr[0:64, :], ALU.mult).then_inc(ssmn_ready, 1)
                if b == 0:
                    keep_gate(1)
                else:
                    take_out(0, 0)
                for c in range(DC):
                    item = ("dt", b, c)
                    wait_work(dve, item)
                    dve.tensor_scalar(dtv[:, c, :], bank(item), par[:, 1, c:c + 1], None, ALU.add)\
                        .then_inc(taken_sem(item), 1)
                    if b == 0 and c in GATE_AFTER_DT:
                        keep_gate(GATE_AFTER_DT[c])
                if b == 0:
                    keep_gate(3)
                for h, part in enumerate(SP_PARTS):
                    dve.wait_ge(sp_ready, 3 * b + h + 1)
                    dve.scalar_tensor_tensor(dtv[:, part, :], dtv[:, part, :], 0.0, sp[:, part, :],
                                             ALU.max, ALU.add).then_inc(dt_ready, 1)
                if b == 0:
                    keep_gate(4)
                else:
                    take_out(0, 1)

                for c in range(DC):
                    for n in range(NS):
                        k = (b * DC + c) * NS + n
                        dve.wait_ge(exp_done, k + 1)
                        dve.wait_ge(bmul_done, k // 2 + 1)
                        dve.tensor_tensor_scan(psum[:, SLOT[k % SLOTS], :], psum[:, SLOT[k % SLOTS], :],
                                               dbu[:, k // 2 % 2, k % 2, :], 0.0, ALU.mult, ALU.add)\
                            .then_inc(scan_done, 1)
                        if c or n:
                            times_c(k - 1)
                        if c and n == (1 if b else 2):
                            (plus_d if b else first_y)(c - 1)
                        if b == 0:
                            if (c, n) in CONV_AT:
                                conv(1, CONV_AT.index((c, n)))
                            if c == 0 and n in (1, 3, 5):
                                keep_gate(5 + n // 2)
                            if c == 0 and n == 2:
                                dve.wait_ge(ld_x[1], 16)
                                stats(("ssm", 1), x_tiles(1))
                            if c == 0 and n == 6:
                                inv_std(("ssm", 1), NT)
                            if c == 0 and n in (6, 7, 10, 11):
                                norm_tile("ssm", 1, (6, 7, 10, 11).index(n), xn)
                        else:
                            if c == 0 and n in (1, 11):
                                take_out(0, 2 + n // 11)
                            if c == 1 and n == 5:
                                for t in range(NT):
                                    wait_taken(dve, ("out", 0, t))
                                stats(("out", 0), [obuf[0][:, t, :] for t in range(NT)])
                            if c == 1 and n == 12:
                                inv_std(("out", 0), NT)
                                out_add(0)
                            if c == 3 and n == 5:
                                stats(("ffn", 0), x_tiles(0))
                            if c == 4 and n == 10:
                                inv_std(("ffn", 0), NT)
                            if c >= 3 and c % 2 and n == 12:
                                times_gate(c - 3)
                                times_gate(c - 2)
                times_c((b + 1) * NSTEP - 1)
                if b == 0:
                    first_y(DC - 1)
                else:
                    plus_d(DC - 1)
                    times_gate(DC - 2)
                    times_gate(DC - 1)

            def unpack(i):
                s = i % 3
                dve.wait_ge(ld_stage[s], 96 * (i // 3 + 1))
                dve.tensor_scalar(q_gu[s][:], q_gu[s][:], shift[:, 0:1], 15, ALU.logical_shift_right,
                                  ALU.bitwise_and)
                link(dve.tensor_scalar(q_d[s][:], q_d[s][:], shift[:, 0:1], 15, ALU.logical_shift_right,
                                       ALU.bitwise_and))
                dve.tensor_tensor(w_gu[s][:], q_gu[s][:], s_gu[s][:], ALU.mult).then_inc(q_done, 1)
                dve.tensor_tensor(w_d[s][:], q_d[s][:], s_d[s][:], ALU.mult).then_inc(q_done, 1)

            def low_weights(i):
                dve.wait_ge(whi_done, 2 * i + 1)
                dve.tensor_tensor(gu_lo[:, i, :], w_gu[i % 3][:], gu_hi[:, i, :], ALU.subtract).then_inc(wlo_gu, 1)

            def low_turned(b):
                for t in range(NT):
                    item = ("tr", "ffn", b, t)
                    cols = slice(t * P, (t + 1) * P)
                    dve.wait_ge(xhi_done, NT * b + t + 1)
                    dve.tensor_tensor(xf_lo[b][:, :, cols], bank(item).rearrange("p (k t) -> p k t", k=KH),
                                      xf_hi[b][:, :, cols], ALU.subtract).then_inc(taken_sem(item), 1)

            def low_moe(b):
                for t in range(NT):
                    item = ("tr", "moe", b, t)
                    cols = slice(t * P, (t + 1) * P)
                    dve.wait_ge(xmhi_done, NT * b + t + 1)
                    dve.tensor_tensor(xm_lo[b][:, :, cols], bank(item).rearrange("p (k t) -> p k t", k=KH),
                                      xm_hi[b][:, :, cols].bitcast(F32), ALU.subtract).then_inc(taken_sem(item), 1)

            def ffn_inner(b, i):
                k = b * IC + i
                wait_taken(dve, ("g", b, i))
                wait_work(dve, ("u", b, i))
                if k >= 2:
                    dve.wait_ge(ithi_done, k - 1)
                dve.tensor_tensor(it[:, k % 2, :], sg[:, k % 2, :], bank(("u", b, i)), ALU.mult)\
                    .then_inc(taken_sem(("u", b, i)), 1)
                wait_taken(dve, ("u", b, i))
                dve.wait_ge(ithi_done, k + 1)
                if k >= 2:
                    dve.wait_ge(ffn_used, k - 1)
                dve.tensor_tensor(it_lo[:, k % 2, :], it[:, k % 2, :], it_hi[:, k % 2, :],
                                  ALU.subtract).then_inc(itlo_done, 1)

            def ffn_stats16(b):
                dve.wait_ge(y16_done, NT * (b + 1))
                n = LN[("ffn16", b)]
                for t in range(NT):
                    last = dve.bn_stats(bst[:, t, :], y16[:, t, :])
                link(last)
                for t in range(NT):
                    last = dve.bn_aggr(mv[:, n, t, :], bst[:, t, :])
                link(last)
                link(dve.tensor_copy(m16[:, b, :, :], mv[:, n, :, :]))
                dve.tensor_scalar(ve16[:, b, :, 0], m16[:, b, :, 1], EPS16, None, ALU.add).then_inc(stats_ready, 1)

            def ffn_inv16(b):
                n = LN[("ffn16", b)]
                dve.wait_ge(std_ready, n + 1)
                link(dve.reciprocal(rstd[:, n, :], ve16[:, b, :, 1]))

            def ffn_add16(b, t):
                n = LN[("ffn16", b)]
                link(dve.tensor_scalar(d16[:], y16[:, t, :], m16[:, b, t, 0:1], None, ALU.subtract))
                link(dve.tensor_scalar(n16[:], d16[:], rstd[:, n, t:t + 1], None, ALU.mult))
                link(dve.tensor_tensor(x[:, b * NT + t, :], x[:, b * NT + t, :], n16[:], ALU.add))

            full = [P, NT, DH, DH]

            def att_scores(b):
                item = ("qkv", b)
                wait_work(dve, item)
                dve.tensor_tensor(qkv[:], bank(item)[:, 0:NT * QKV].rearrange("p (a b) -> p a b", a=NT),
                                  bqkv[:].unsqueeze(1).broadcast_to([P, NT, QKV]), ALU.add)\
                    .then_inc(taken_sem(item), 1)
                wait_taken(dve, item)
                q_b = qkv[:, :, 0:DH].unsqueeze(3).broadcast_to(full)
                k_b = qkv[:, :, DH:2 * DH].unsqueeze(2).broadcast_to(full)
                link(dve.tensor_tensor(sc[:], q_b, k_b, ALU.mult))
                link(dve.tensor_reduce(smax[:], sc[:], AX.X, ALU.max))
                dve.tensor_tensor(sc[:], sc[:], smax[:].unsqueeze(3).broadcast_to(full), ALU.subtract)\
                    .then_inc(s_ready, 1)

            def att_values(b):
                v_b = qkv[:, :, 2 * DH:].unsqueeze(2).broadcast_to(full)
                dve.wait_ge(p_ready, b + 1)
                dve.tensor_reduce(den[:], pr[:], AX.X, ALU.add)
                link(dve.tensor_tensor(sc[:], pr[:], v_b, ALU.mult))
                dve.tensor_reduce(num[:], sc[:], AX.X, ALU.add)
                link(dve.reciprocal(den[:], den[:]))
                link(dve.tensor_tensor(num[:], num[:], den[:], ALU.mult))
                stats(("atto", b), [num[:, t, :] for t in range(NT)])

            def att_add(b):
                group = ("atto", b)
                inv_std(group, NT)
                for t in range(NT):
                    last = dve.tensor_scalar(on[:, t, :], num[:, t, :], mean_of(group, t), rstd_of(group, t),
                                             ALU.subtract, ALU.mult)
                link(last)
                for t in range(NT):
                    x3 = x[:, b * NT + t, :].rearrange("p (d h) -> p d h", d=DH)
                    last = dve.tensor_tensor(x3, x3, on[:, t, :].unsqueeze(2).broadcast_to([P, DH, NH]), ALU.add)
                link(last)

            def between(b, i):
                if i == 0:
                    ffn_stats16(b)
                if i == 1:
                    ffn_inv16(b)
                    ffn_add16(b, 0)
                    ffn_add16(b, 1)
                if i == 2:
                    ffn_add16(b, 2)
                    ffn_add16(b, 3)
                    stats(("att", b), x_tiles(b))
                if i == 3:
                    inv_std(("att", b), NT)
                    norm_tile("att", b, 0, xnc)
                    norm_tile("att", b, 1, xnc)
                if i == 4:
                    norm_tile("att", b, 2, xnc)
                    norm_tile("att", b, 3, xnc)
                if i == 5:
                    att_scores(b)
                if i == 6:
                    att_values(b)
                if i == 7:
                    att_add(b)
                if i == 8:
                    stats(("moe", b), x_tiles(b))

            for t in range(NT):
                norm_tile("ffn", 0, t, xnc)
            low_turned(0)
            unpack(0)
            for i in range(1, 4):
                unpack(i)
                low_weights(i - 1)
            for i in range(IC):
                ffn_inner(0, i)
                if i == 0:
                    for t in range(NT):
                        wait_taken(dve, ("out", 1, t))
                    stats(("out", 1), [obuf[1][:, t, :] for t in range(NT)])
                if i == 1:
                    inv_std(("out", 1), NT)
                    out_add(1)
                if i == 2:
                    stats(("ffn", 1), x_tiles(1))
                if i + 4 < IC:
                    unpack(i + 4)
                if i + 3 < IC:
                    low_weights(i + 3)
                if i == 3:
                    inv_std(("ffn", 1), NT)
                if i == 7:
                    dve.wait_ge(ld_att, 16 * 7)
                    dve.tensor_reduce(wqkv[:, :, 0:DH], wqraw[:], AX.X, ALU.add).then_inc(wq_done, 1)
                    dve.tensor_reduce(bqkv[:, 0:DH], bqraw[:], AX.X, ALU.add).then_inc(wq_done, 1)
                if i == IC - 3:
                    norm_tile("ffn", 1, 0, xnc)
                    norm_tile("ffn", 1, 1, xnc)
            norm_tile("ffn", 1, 2, xnc)
            norm_tile("ffn", 1, 3, xnc)
            low_turned(1)
            for i in range(IC):
                ffn_inner(1, i)
                if i < 8:
                    between(0, i)
                if i == 7:
                    between(0, 8)
                if i == 8:
                    inv_std(("moe", 0), NT)
                    norm_tile("moe", 0, 0, xnc)
                    norm_tile("moe", 0, 1, xnc)
                if i == 9:
                    norm_tile("moe", 0, 2, xnc)
                    norm_tile("moe", 0, 3, xnc)
                    low_moe(0)

            def route(b):
                item = ("logits", b)
                wait_work(dve, item)
                for t in range(NT):
                    last = dve.max(top8[:, b, t, :], bank(item)[:, t * NE:(t + 1) * NE])
                last.then_inc(taken_sem(item), 1)
                wait_taken(dve, item)
                dve.tensor_tensor(rw[:, b, :], top8[:, b, :, 0], top8[:, b, :, 1], ALU.add).then_inc(rw_ready, 1)

            def low_latent(b, name, hi, lo, ms=range(LAT)):
                for m in ms:
                    item = (name, b, m)
                    dve.wait_ge(lhi_done, 2 * LAT * b + LAT * (name == "exp") + m + 1)
                    dve.tensor_tensor(lo[:, m, :], bank(item), hi[:, m, :].bitcast(F32), ALU.subtract)\
                        .then_inc(taken_sem(item), 1)

            def h2_low(b, i):
                k = b * MI + i
                dve.wait_ge(h2hi_done, k + 1)
                dve.tensor_tensor(h2_lo[:, k % 2, :], h2[:, k % 2, :], h2_hi[:, k % 2, :].bitcast(F32),
                                  ALU.subtract).then_inc(h2lo_done, 1)

            def moe_sum(b, tiles=range(NT)):
                for t in tiles:
                    y = rt[b][:, t, :]
                    dve.wait_ge(down_done, NT * b + t + 1)
                    wait_taken(dve, ("routed", b, t))
                    dve.tensor_tensor(y, psum[:, t, :], y, ALU.add).then_inc(ym_done, 1)
                    dve.wait_ge(ym_done, NT * b + t + 1)
                    stats(("moei", b, t), [y])

            def moe_affine(b, tiles=range(NT)):
                for t in tiles:
                    y = rt[b][:, t, :]
                    group = ("moei", b, t)
                    inv_std(group, 1)
                    link(dve.scalar_tensor_tensor(y, y, mean_of(group, 0), gam[:], ALU.subtract, ALU.mult))
                    link(dve.scalar_tensor_tensor(y, y, rstd_of(group, 0), bet[:], ALU.mult, ALU.add))
                    stats(("moeo", b, t), [y])

            def moe_norm(b):
                for t in range(NT):
                    y = rt[b][:, t, :]
                    group = ("moeo", b, t)
                    inv_std(group, 1)
                    dve.tensor_scalar(y, y, mean_of(group, 0), rstd_of(group, 0), ALU.subtract, ALU.mult)\
                        .then_inc(yn_done, 1)

            low_latent(0, "fc1", lat_hi, lat_lo, [0])
            route(0)
            low_latent(0, "fc1", lat_hi, lat_lo, [1])
            low_latent(0, "exp", eo_hi, eo_lo)
            between(1, 0)
            between(1, 1)
            between(1, 2)
            for i in range(MI):
                h2_low(0, i)
                if i == 0:
                    between(1, 3)
                    between(1, 4)
                if i in (2, 3, 4, 5):
                    between(1, i + 3)
                if i == 6:
                    inv_std(("moe", 1), NT)
                    norm_tile("moe", 1, 0, xnc)
                    norm_tile("moe", 1, 1, xnc)
                if i == 7:
                    norm_tile("moe", 1, 2, xnc)
                    norm_tile("moe", 1, 3, xnc)
            low_moe(1)
            moe_sum(0, [0, 1])
            low_latent(1, "fc1", lat_hi, lat_lo, [0])
            route(1)
            low_latent(1, "fc1", lat_hi, lat_lo, [1])
            moe_sum(0, [2])
            low_latent(1, "exp", eo_hi, eo_lo)
            moe_sum(0, [3])
            moe_affine(0, [0, 1])
            for i in range(MI):
                h2_low(1, i)
                if i == 0:
                    moe_affine(0, [2, 3])
                if i == 2:
                    moe_norm(0)
            moe_sum(1)
            moe_affine(1)
            moe_norm(1)
            for t in (2, 3):
                k = NT + t
                dve.wait_ge(yn_done, k + 1)
                dve.tensor_tensor(x[:, k, :], x[:, k, :], rt[1][:, t, :], ALU.add).then_inc(x_last, 1)

        @block.scalar
        def _(act):
            def root(group, tiles):
                n = LN[group]
                act.wait_ge(stats_ready, n + 1)
                act.activation(std[:, n, 0:tiles], mv[:, n, 0:tiles, 1], ACT.Sqrt, bias=epst[:, 0:1])\
                    .then_inc(std_ready, 1)

            def root16(b):
                act.wait_ge(stats_ready, LN[("ffn16", b)] + 1)
                act.activation(ve16[:, b, :, 1], ve16[:, b, :, 0], ACT.Sqrt).then_inc(std_ready, 1)

            def take_turned(layer, b, t, dst):
                item = ("tr", layer, b, t)
                wait_work(act, item)
                act.copy(dst[:, :, t * P:(t + 1) * P], bank(item).rearrange("p (k t) -> p k t", k=KH))\
                    .then_inc(taken_sem(item), 1)

            def silu_gate(b, c):
                item = ("gate", b, c)
                if b == 0:
                    wait_taken(act, item)
                    act.activation(g[:, c, :], g[:, c, :], ACT.Silu).then_inc(gate_done, 1)
                else:
                    wait_work(act, item)
                    for t in range(NT):
                        wait_taken(act, ("out", 0, t))
                    act.activation(g[:, c, :], bank(item), ACT.Silu).then_inc(taken_sem(item), 1)

            def conv_tap(b, c):
                item = ("x", b, c)
                wait_work(act, item)
                if b * DC + c >= 2:
                    act.wait_ge(u_ready, b * DC + c - 1)
                act.activation(cacc[:, c % 2, :], bank(item), ACT.Identity, bias=par[:, 0, c:c + 1],
                               scale=convw[:, c, KCONV - 1:KCONV]).then_inc(conv_ready, 1)

            def conv_silu(b, c):
                wait_taken(act, ("x", b, c))
                if b:
                    act.wait_ge(y_taken, c + 1)
                act.activation(u[:, c, :], cacc[:, c % 2, :], ACT.Silu).then_inc(u_ready, 1)

            def take_out(b, t):
                item = ("out", b, t)
                wait_work(act, item)
                act.copy(obuf[b][:, t, :], bank(item)).then_inc(taken_sem(item), 1)

            act.wait_ge(eps_ready, 2)
            root(("ssm", 0), NT)
            for t in range(NT):
                take_turned("ssm", 0, t, xT)
            conv_tap(0, 0)
            for c in range(DC):
                if c + 1 < DC:
                    conv_tap(0, c + 1)
                conv_silu(0, c)
            for b in range(NB):
                act.wait_ge(ssm_ready, b + 1)
                act.copy(ssm[0:64, :], psum[0:64, SSM_BANK, :])
                act.activation(sq[0:64, :], psum[0:64, SSM_BANK, :], ACT.Square).then_inc(sq_ready, 1)
                item = ("ms", b)
                wait_work(act, item)
                act.activation(rr[0:64, :], bank(item)[0:64, :], ACT.Sqrt, bias=epst[0:64, 1:2])\
                    .then_inc(taken_sem(item), 1)
                if b == 0:
                    act.wait_ge(ld_const, 16 * 6)
                    act.activation(aneg[:], aneg[:], ACT.Exp).then_inc(act_chain, 1)
                    act.wait_ge(act_chain, 1)
                    act.mul(aneg[:], aneg[:], -1.0).then_inc(a_ready, 1)
                n0 = 1 + b * 2 * DC
                act.wait_ge(ssmn_ready, b + 1)
                for c in range(DC + 1):
                    if c < DC:
                        wait_taken(act, ("dt", b, c))
                        act.activation(sp[:, c, :], dtv[:, c, :], ACT.Abs).then_inc(act_chain, 1)
                    if c:
                        act.wait_ge(act_chain, n0 + 2 * c - 1)
                        act.activation(sp[:, c - 1, :], sp[:, c - 1, :], ACT.Exp, scale=-1.0).then_inc(act_chain, 1)
                act.wait_ge(act_chain, n0 + 2 * DC)
                for part in SP_PARTS:
                    act.activation(sp[:, part, :], sp[:, part, :], ACT.Ln, bias=1.0).then_inc(sp_ready, 1)
                act.wait_ge(a_ready, 1)
                for c in range(DC):
                    act.wait_ge(dt_ready, 3 * b + (c > 1) + (c > 3) + 1)
                    for n in range(NS):
                        k = (b * DC + c) * NS + n
                        if k >= SLOTS:
                            act.wait_ge(cmul_done, k - SLOTS + 1)
                        act.activation(psum[:, SLOT[k % SLOTS], :], dtv[:, c, :], ACT.Exp,
                                       scale=aneg[:, c, n:n + 1]).then_inc(exp_done, 1)
                        if b == 0 and n == 6:
                            if c:
                                act.wait_ge(ysum_done, NS * c)
                            act.activation(diag[:], ident[:], ACT.Identity, scale=par[:, 2, c:c + 1])\
                                .then_inc(diag_ready, 1)
                        if b == 0:
                            if c == 0 and n == 4:
                                root(("ssm", 1), NT)
                            if (c, n) == (1, 3):
                                conv_tap(1, 0)
                            if n == 8:
                                if c:
                                    conv_tap(1, c)
                                    conv_silu(1, c - 1)
                                silu_gate(0, c)
                            if c == 0 and n in (10, 11):
                                take_turned("ssm", 1, n - 10, xT)
                            if c == 0 and n in (14, 15):
                                take_turned("ssm", 1, n - 12, xT)
                        else:
                            if c == 1 and n == 8:
                                root(("out", 0), NT)
                            if c == 3 and n == 8:
                                root(("ffn", 0), NT)
                            if c % 2 and n == 12:
                                silu_gate(1, c - 1)
                                silu_gate(1, c)
                if b == 0:
                    conv_silu(1, DC - 1)

            def high_weights(i):
                act.wait_ge(w_done, 2 * (i + 1))
                act.copy(gu_hi[:, i, :], w_gu[i % 3][:]).then_inc(whi_done, 1)
                act.copy(d_hi[:, i, :], w_d[i % 3][:]).then_inc(whi_done, 1)

            def high_turned(b):
                for t in range(NT):
                    item = ("tr", "ffn", b, t)
                    wait_work(act, item)
                    act.copy(xf_hi[b][:, :, t * P:(t + 1) * P], bank(item).rearrange("p (k t) -> p k t", k=KH))\
                        .then_inc(xhi_done, 1)

            def high_moe(b):
                for t in range(NT):
                    item = ("tr", "moe", b, t)
                    wait_work(act, item)
                    act.copy(xm_hi[b][:, :, t * P:(t + 1) * P], bank(item).rearrange("p (k t) -> p k t", k=KH))\
                        .then_inc(xmhi_done, 1)

            def high_moe_weights(load_no, n, names):
                act.wait_ge(ld_moe[load_no], 16 * 3)
                for name in names:
                    w, w_hi, _ = moe_w[name]
                    act.copy(w_hi[:], w[:]).then_inc(mw_hi[n], 1)

            def high_moe_chunk(load_no, n, name, k):
                act.wait_ge(ld_moe[load_no], 16)
                w, w_hi, _ = moe_w[name]
                act.copy(w_hi[:, k], w[:, k]).then_inc(mw_hi[n], 1)

            def ffn_silu(k):
                b, i = divmod(k, IC)
                item = ("g", b, i)
                wait_work(act, item)
                if k >= 2:
                    wait_taken(act, ("u", (k - 2) // IC, (k - 2) % IC))
                act.activation(sg[:, k % 2, :], bank(item), ACT.Silu).then_inc(taken_sem(item), 1)

            def ffn_high(k):
                b, i = divmod(k, IC)
                wait_taken(act, ("u", b, i))
                if k >= 2:
                    act.wait_ge(ffn_used, k - 1)
                act.copy(it_hi[:, k % 2, :], it[:, k % 2, :]).then_inc(ithi_done, 1)

            def take16(b):
                act.wait_ge(ffn_used, IC * (b + 1))
                for t in range(NT):
                    act.copy(y16[:, t, :], psum[:, t, :]).then_inc(y16_done, 1)

            def att_exp(b):
                act.wait_ge(s_ready, b + 1)
                act.activation(pr[:], sc[:], ACT.Exp, scale=float(DH) ** -0.5).then_inc(p_ready, 1)

            high_turned(0)
            high_weights(0)
            high_weights(1)
            take_out(1, 0)
            high_weights(2)
            for t in range(1, NT):
                take_out(1, t)
            for k in range(NB * IC):
                b, i = divmod(k, IC)
                ffn_silu(k)
                ffn_high(k)
                if k == IC - 1:
                    high_turned(1)
                    take16(0)
                if b == 1 and i == 4:
                    for t in range(NT):
                        take_turned("att", 0, t, xTa[0])
                if k == 0:
                    root(("out", 1), NT)
                if k == 2:
                    root(("ffn", 1), NT)
                if k + 3 < IC:
                    high_weights(k + 3)
                if k == 8:
                    act.wait_ge(ld_att, 16 * 7)
                    act.copy(moe_w["gate"][1][:], moe_w["gate"][0][:]).then_inc(mw_hi[0], 1)
                if b == 1:
                    if i == 0:
                        root16(0)
                    if i == 2:
                        root(("att", 0), NT)
                    if i == 5:
                        att_exp(0)
                    if i == 6:
                        root(("atto", 0), NT)
                    if i == 8:
                        root(("moe", 0), NT)
                    if i == 3:
                        high_moe_weights(0, 1, ["fc1"])
                    if i == 4:
                        high_moe_weights(0, 1, ["exp", "fc2"])
                    if i >= 7:
                        high_moe_chunk(1, 2, "up", i - 7)
                    if i == 9:
                        high_moe(0)
            take16(1)

            def relu(b, i):
                k = b * MI + i
                item = ("up", b, i)
                wait_work(act, item)
                if k >= 2:
                    act.wait_ge(h2_done, k - 1)
                act.activation(h1[:, k % 2, :], bank(item), ACT.Relu).then_inc(taken_sem(item), 1)

            def h2_high(b, i):
                k = b * MI + i
                act.wait_ge(h2_done, k + 1)
                if i >= 2:
                    act.wait_ge(moe_used, (MI - 1) * b + i - 1)
                elif b:
                    act.wait_ge(down_done, NT * b)
                act.copy(h2_hi[:, k % 2, :], h2[:, k % 2, :]).then_inc(h2hi_done, 1)

            def high_latent(b, name, hi):
                for m in range(LAT):
                    item = (name, b, m)
                    wait_work(act, item)
                    act.copy(hi[:, m, :], bank(item)).then_inc(lhi_done, 1)

            for b in range(NB):
                wait_work(act, ("lt", b))
                act.copy(lt[0:NE, :], bank(("lt", b))[0:NE, :]).then_inc(taken_sem(("lt", b)), 1)
                high_latent(b, "fc1", lat_hi)
                high_latent(b, "exp", eo_hi)
                if b == 0:
                    root16(1)
                if b:
                    for t in range(NT):
                        root(("moei", 0, t), 1)
                act.wait_ge(rw_ready, b + 1)
                for t in range(NT):
                    item = ("routed", b, t)
                    wait_work(act, item)
                    act.activation(rt[b][:, t, :], bank(item), ACT.Identity, scale=rw[:, b, t:t + 1])\
                        .then_inc(taken_sem(item), 1)
                    if b == 0:
                        high_moe_chunk(2, 3, "down", 2 * t)
                        high_moe_chunk(2, 3, "down", 2 * t + 1)
                for i in range(MI):
                    relu(b, i)
                    h2_high(b, i)
                    if b == 0:
                        if i == 0:
                            root(("att", 1), NT)
                        if i == 1:
                            for t in range(NT):
                                take_turned("att", 1, t, xTa[1])
                        if i == 3:
                            att_exp(1)
                        if i == 4:
                            root(("atto", 1), NT)
                        if i == 6:
                            root(("moe", 1), NT)
                        if i == 7:
                            high_moe(1)
                    elif i == 1:
                        for t in range(NT):
                            root(("moeo", 0, t), 1)
            for name in ("moei", "moeo"):
                for t in range(NT):
                    root((name, 1, t), 1)

        @block.gpsimd
        def _(pool):
            def dt_times_u(b, c):
                pool.wait_ge(dt_ready, 3 * b + (c > 1) + (c > 3) + 1)
                if c >= 2:
                    pool.wait_ge(bmul_done, (b * DC + c - 1) * NS // 2)
                pool.tensor_tensor(du[:, c % 2, :], dtv[:, c, :], u[:, c, :], ALU.mult).then_inc(du_done, 1)

            for b in range(NB):
                pool.wait_ge(bc_stored, 16 * (b + 1))
                dt_times_u(b, 0)
                for c in range(DC):
                    pool.wait_ge(du_done, b * DC + c + 1)
                    if c == 0:
                        pool.wait_ge(dt_ready, 3 * b + 2)
                    for p in range(NS // 2):
                        k = (b * DC + c) * NS // 2 + p
                        if k >= 2:
                            pool.wait_ge(scan_done, 2 * (k - 1))
                        if c == 0 and p % 2 == 0:
                            pool.wait_ge(ld_bc[b][p // 2], 32)
                        pool.tensor_tensor(dbu[:, k % 2, :, :],
                                           du[:, c % 2, :].unsqueeze(1).broadcast_to([P, 2, L]),
                                           bc[:, 2 * p:2 * p + 2, :], ALU.mult).then_inc(bmul_done, 1)
                        if p == 4 and c + 1 < DC:
                            dt_times_u(b, c + 1)

            for i in range(IC):
                s = i % 3
                pool.wait_ge(q_done, 2 * i + 2)
                pool.tensor_tensor(w_gu[s][:], w_gu[s][:], z_gu[s][:], ALU.subtract).then_inc(w_done, 1)
                pool.tensor_tensor(w_d[s][:], w_d[s][:], z_d[s][:], ALU.subtract).then_inc(w_done, 1)
                pool.wait_ge(whi_done, 2 * i + 2)
                pool.tensor_tensor(d_lo[:, i, :], w_d[s][:], d_hi[:, i, :], ALU.subtract).then_inc(wlo_d, 1)
            def low_moe_weights(n, names):
                pool.wait_ge(mw_hi[n], len(names))
                for name in names:
                    w, w_hi, w_lo = moe_w[name]
                    pool.tensor_tensor(w_lo[:], w[:], w_hi[:].bitcast(F32), ALU.subtract).then_inc(mw_lo[n], 1)

            def add_out(b, tiles):
                for t in tiles:
                    k = b * NT + t
                    pool.wait_ge(yn_done, k + 1)
                    pool.tensor_tensor(x[:, k, :], x[:, k, :], rt[b][:, t, :], ALU.add).then_inc(x_done, 1)

            low_moe_weights(0, ["gate"])
            low_moe_weights(1, ["fc1", "exp", "fc2"])

            def low_moe_chunk(n, name, k):
                pool.wait_ge(mw_hi[n], k + 1)
                w, w_hi, w_lo = moe_w[name]
                pool.tensor_tensor(w_lo[:, k], w[:, k], w_hi[:, k].bitcast(F32), ALU.subtract)\
                    .then_inc(mw_lo[n], 1)

            for k in range(KH):
                low_moe_chunk(2, "up", k)
            for k in range(2):
                low_moe_chunk(3, "down", k)
            for b in range(NB):
                for i in range(MI):
                    k = b * MI + i
                    wait_taken(pool, ("up", b, i))
                    if k >= 2:
                        pool.wait_ge(h2lo_done, k - 1)
                    pool.tensor_tensor(h2[:, k % 2, :], h1[:, k % 2, :], h1[:, k % 2, :], ALU.mult)\
                        .then_inc(h2_done, 1)
                    if b == 0 and i < MI - 2:
                        low_moe_chunk(3, "down", i + 2)
                    if b == 1 and i == 3:
                        add_out(0, range(NT))
            add_out(1, range(2))


def kernel(**inputs):
    import concourse.bacc as _bacc
    from concourse.bass_utils import run_bass_kernel_spmd as _run

    def arr(name):
        return np.ascontiguousarray(inputs[name])

    def cols(v):
        return np.reshape(v, (DC, P, -1)).transpose(1, 0, 2).reshape(P, -1)

    def chunks(w):
        k = w.shape[0] // P
        return np.reshape(w, (k, P, -1)).transpose(1, 0, 2).reshape(P, -1)

    def pad(a, rows, width):
        out = np.zeros((rows, width), a.dtype)
        out[:a.shape[0], :a.shape[1]] = a
        return out

    rms = np.zeros((64, 64), np.float32)
    for a, e in ((0, R), (R, R + NS), (R + NS, R + 2 * NS)):
        rms[a:e, a:e] = 1.0 / (e - a)

    def packed(name):
        return pad(arr(name), 64, IPAD).reshape(KH, 16, IC, P)

    def interleave(a, b_):
        return np.stack([a, b_], axis=1)

    qgu = np.stack([packed("L0_ffn_gate_qweight"), packed("L0_ffn_up_qweight")], axis=1)
    qgu = qgu.transpose(3, 2, 0, 1, 4).reshape(IC, 16, 2 * KH * P)
    sgu = interleave(pad(arr("L0_ffn_gate_scales"), KH, IPAD), pad(arr("L0_ffn_up_scales"), KH, IPAD))
    zgu = interleave(pad(arr("L0_ffn_gate_zeros"), KH, IPAD // 8), pad(arr("L0_ffn_up_zeros"), KH, IPAD // 8))

    arrays = {
        "x_in": arr("L0_attn_hidden_states").reshape(NB * L, H),
        "ident_in": np.eye(P, dtype=np.float32),
        "meanmat_in": rms,
        "shift_in": (np.arange(P, dtype=np.int32) % 8 * 4).reshape(P, 1),
        "shifts_in": np.tile(np.arange(8, dtype=np.int32) * 4, (P, 1)),
        "w_in": arr("L0_attn_W_in").T,
        "conv_in": cols(arr("L0_attn_conv_w")),
        "par_in": np.concatenate([cols(arr("L0_attn_conv_b")), cols(arr("L0_attn_b_dt")), cols(arr("L0_attn_D"))], 1),
        "alog_in": cols(arr("L0_attn_A_log")),
        "wx_in": chunks(arr("L0_attn_W_x").T),
        "wdt_in": arr("L0_attn_W_dt").T,
        "wout_in": chunks(arr("L0_attn_W_out").T),
        "qgu_in": qgu,
        "qd_in": pad(arr("L0_ffn_down_qweight"), IC * 16, H).reshape(IC, 16, H),
        "sgu_in": sgu.reshape(2 * KH, IPAD),
        "zgu_in": zgu.reshape(2 * KH, IPAD // 8),
        "sd_in": arr("L0_ffn_down_scales"),
        "zd_in": arr("L0_ffn_down_zeros"),
        "wq_in": chunks(arr("L1_attn_Wq").reshape(H, DH * NH)),
        "wkv_in": chunks(np.concatenate([arr("L1_attn_Wk").reshape(H, DH), arr("L1_attn_Wv").reshape(H, DH)], 1)),
        "bq_in": arr("L1_attn_bq").reshape(1, DH * NH),
        "bkv_in": np.concatenate([arr("L1_attn_bk").reshape(1, DH), arr("L1_attn_bv").reshape(1, DH)], 1),
        "gate_in": chunks(arr("L1_ffn_gate_w")),
        "up_in": arr("L1_ffn_up_w"),
        "down_in": arr("L1_ffn_down_w"),
        "fc1_in": arr("L1_ffn_fc1_w"),
        "fc2_in": arr("L1_ffn_fc2_w"),
        "exp_in": arr("L1_ffn_expert_w"),
        "gamma_in": arr("L1_ffn_ln_gamma").reshape(1, H),
        "beta_in": arr("L1_ffn_ln_beta").reshape(1, H),
    }
    nc = _bacc.Bacc("TRN2", target_bir_lowering=False, num_devices=1)
    args = {}
    for name in list(arrays):
        a = np.ascontiguousarray(arrays[name])
        arrays[name] = a
        args[name] = nc.dram_tensor(name, a.shape, mybir.dt.from_np(a.dtype), kind="ExternalInput").ap()
    args["out"] = nc.dram_tensor("out", [NB * L, H], F32, kind="ExternalOutput").ap()
    build(nc, **args)
    r = _run(nc, [arrays], core_ids=[0])
    return r.results[0]["out"].reshape(NB, L, H)
```
